# Optimizing a Trainium2 kernel written in Bass

```python
import numpy as np
import jax
import jax.numpy as jnp

def _softmax(x, axis=-1):
    return jax.nn.softmax(x, axis=axis)

def _gelu(x):
    return jax.nn.gelu(x, approximate=True)

def _silu(x):
    return jax.nn.silu(x)

def _sigmoid(x):
    return jax.nn.sigmoid(x)

def _layernorm(x, axis=-1, eps=1e-05):
    m = jnp.mean(x, axis=axis, keepdims=True)
    v = jnp.var(x, axis=axis, keepdims=True)
    return (x - m) / jnp.sqrt(v + eps)

def _scatter_add(tgt, idx, src, axis=0):
    return tgt.at[idx].add(src)

def _segment_sum(src, seg, n):
    return jax.ops.segment_sum(src, seg, n)
kernel_name = 'mk_vit_tower_postln_d1_tok_img1024_r4_483d73'

def setup_inputs(seed: int=0):
    np.random.seed(seed)
    _w = jnp.asarray

    def _rec_inputs():
        import jax
        import jax.numpy as jnp
        _rk = jax.random.key(seed)
        x = -0.000222058 + 0.999998 * jax.random.normal(jax.random.fold_in(_rk, 1), (32, 3, 64, 64), jnp.float32)
        return x
    x = _rec_inputs()

    def _L0_tok_setup():
        import jax, jax.numpy as jnp
        import numpy as np
        IMG, PS, C, OUT = (64, 16, 3, 256)
        NP = IMG // PS
        IN_FEAT = C * PS * PS
        key = jax.random.key(seed)
        k1, k2, k3, k4 = jax.random.split(key, 4)
        x = jax.random.normal(k1, (128, C, IMG, IMG), dtype=jnp.float32)
        W = jax.random.normal(k2, (OUT, IN_FEAT), dtype=jnp.float32) / np.sqrt(IN_FEAT)
        b = jax.random.normal(k3, (OUT,), dtype=jnp.float32) * 0.01
        pos_emb = jax.random.normal(k4, (NP * NP, OUT), dtype=jnp.float32)
        return {'x': x, 'W': W, 'b': b, 'pos_emb': pos_emb}
    _L0_tok_all = _L0_tok_setup()
    _L0_tok_in = {k: v for k, v in _L0_tok_all.items() if k in ('W', 'b', 'pos_emb')}
    del _L0_tok_all

    def _L0_attn_setup():
        import jax, jax.numpy as jnp
        import numpy as np
        B_, T_, D_, H_ = (2, 512, 256, 16)
        EPS = 1e-05

        def _layernorm(x, w, b):
            mu = jnp.mean(x, axis=-1, keepdims=True)
            var = jnp.mean(jnp.square(x - mu), axis=-1, keepdims=True)
            return (x - mu) * jax.lax.rsqrt(var + EPS) * w + b

        def _reference_tuple_inner(x, Wg, bg, Wq, Wk, Wv, Wo, A, Wb, Wc, Dp, W1, b1, W2, b2, ln1_w, ln1_b, ln2_w, ln2_b, skip_gate):
            B, T, D = x.shape
            H = H_
            hd = D // H
            scores = (x @ Wg)[..., 0] + bg[0]
            k = max(1, int(T * 0.25))
            _, idx = jax.lax.top_k(scores, k)
            mask = jnp.zeros((B, T), bool).at[jnp.arange(B)[:, None], idx].set(True)
            residual = x
            xn = _layernorm(x, ln1_w, ln1_b)
            q = (xn @ Wq).reshape(B, T, H, hd).transpose(0, 2, 1, 3)
            kk = (xn @ Wk).reshape(B, T, 1, hd).transpose(0, 2, 1, 3)
            vv = (xn @ Wv).reshape(B, T, 1, hd).transpose(0, 2, 1, 3)
            att = jax.nn.softmax(q @ jnp.swapaxes(kk, -1, -2) / np.sqrt(hd).astype(x.dtype), axis=-1)
            attn_out = (att @ vv).transpose(0, 2, 1, 3).reshape(B, T, D) @ Wo

            def step(h, xt):
                h = jnp.tanh(h @ A.T + xt @ Wb)
                y = h @ Wc + Dp * xt
                return (h, y)
            h0 = jnp.zeros((B, D), x.dtype)
            _, ys = jax.lax.scan(step, h0, jnp.swapaxes(xn, 0, 1))
            ssm_out = jnp.swapaxes(ys, 0, 1)
            deep_out = attn_out + ssm_out
            m = mask[..., None].astype(x.dtype)
            x2 = residual + deep_out * m + residual * skip_gate * (1.0 - m)
            xn2 = _layernorm(x2, ln2_w, ln2_b)
            ffn = jax.nn.gelu(xn2 @ W1 + b1, approximate=False) @ W2 + b2
            out = x2 + ffn
            return (out, scores)
        key = jax.random.key(seed)
        ks = jax.random.split(key, 12)
        s = lambda i, shape, scale=0.02: jax.random.normal(ks[i], shape, jnp.float32) * scale
        hd = D_ // H_
        return {'x': jax.random.normal(ks[0], (B_, T_, D_), jnp.float32), 'Wg': s(1, (D_, 1)), 'bg': jnp.zeros((1,), jnp.float32), 'Wq': s(2, (D_, D_)), 'Wk': s(3, (D_, hd)), 'Wv': s(4, (D_, hd)), 'Wo': s(5, (D_, D_)), 'A': s(6, (D_, D_), 0.01), 'Wb': s(7, (D_, D_)), 'Wc': s(8, (D_, D_)), 'Dp': jnp.ones((D_,), jnp.float32), 'W1': s(9, (D_, 4 * D_)), 'b1': jnp.zeros((4 * D_,), jnp.float32), 'W2': s(10, (4 * D_, D_)), 'b2': jnp.zeros((D_,), jnp.float32), 'ln1_w': jnp.ones((D_,), jnp.float32), 'ln1_b': jnp.zeros((D_,), jnp.float32), 'ln2_w': jnp.ones((D_,), jnp.float32), 'ln2_b': jnp.zeros((D_,), jnp.float32), 'skip_gate': jnp.ones((1,), jnp.float32)}
    _L0_attn_all = _L0_attn_setup()
    _L0_attn_in = {k: v for k, v in _L0_attn_all.items() if k in ('Wg', 'bg', 'Wq', 'Wk', 'Wv', 'Wo', 'A', 'Wb', 'Wc', 'Dp', 'W1', 'b1', 'W2', 'b2', 'ln1_w', 'ln1_b', 'ln2_w', 'ln2_b', 'skip_gate')}
    del _L0_attn_all

    def _L0_ffn_setup():
        import jax, jax.numpy as jnp
        import numpy as np
        IN_FEATURES = 256
        ACT_BITS = 4

        def _hadamard(size: int) -> np.ndarray:
            h = np.array([[1.0]], dtype=np.float64)
            while h.shape[0] < size:
                h = np.block([[h, h], [h, -h]])
            return (h / np.sqrt(size)).astype(np.float32)

        def _quantize_activations(x, bits=ACT_BITS):
            pos = 2 ** (bits - 1) - 1
            neg = 2 ** (bits - 1)
            scale = jnp.clip(jnp.max(jnp.abs(jax.lax.stop_gradient(x)), axis=-1, keepdims=True), 1e-05) / pos
            q = jnp.clip(jnp.round(x / scale), -neg, pos) * scale
            return x + jax.lax.stop_gradient(q - x)

        def _ternary_quantize_ste(w):
            scale = jnp.clip(jnp.mean(jnp.abs(jax.lax.stop_gradient(w)), axis=1, keepdims=True), 1e-05)
            n = w / scale
            tern = jnp.where(n > 0.5, 1.0, jnp.where(n < -0.5, -1.0, 0.0))
            q = tern * scale
            return w + jax.lax.stop_gradient(q - w)
        key = jax.random.key(seed)
        k1, k2 = jax.random.split(key)
        x = jax.random.normal(k1, (8, 2048, IN_FEATURES), dtype=jnp.float32)
        bound = 1.0 / np.sqrt(IN_FEATURES)
        weight = jax.random.uniform(k2, (256, IN_FEATURES), dtype=jnp.float32, minval=-bound, maxval=bound)
        return {'x': x, 'weight': weight}
    _L0_ffn_all = _L0_ffn_setup()
    _L0_ffn_in = {k: v for k, v in _L0_ffn_all.items() if k in ('weight',)}
    del _L0_ffn_all
    return {'x': x, 'L0_tok_W': _L0_tok_in['W'], 'L0_tok_b': _L0_tok_in['b'], 'L0_tok_pos_emb': _L0_tok_in['pos_emb'], 'L0_attn_Wg': _L0_attn_in['Wg'], 'L0_attn_bg': _L0_attn_in['bg'], 'L0_attn_Wq': _L0_attn_in['Wq'], 'L0_attn_Wk': _L0_attn_in['Wk'], 'L0_attn_Wv': _L0_attn_in['Wv'], 'L0_attn_Wo': _L0_attn_in['Wo'], 'L0_attn_A': _L0_attn_in['A'], 'L0_attn_Wb': _L0_attn_in['Wb'], 'L0_attn_Wc': _L0_attn_in['Wc'], 'L0_attn_Dp': _L0_attn_in['Dp'], 'L0_attn_W1': _L0_attn_in['W1'], 'L0_attn_b1': _L0_attn_in['b1'], 'L0_attn_W2': _L0_attn_in['W2'], 'L0_attn_b2': _L0_attn_in['b2'], 'L0_attn_ln1_w': _L0_attn_in['ln1_w'], 'L0_attn_ln1_b': _L0_attn_in['ln1_b'], 'L0_attn_ln2_w': _L0_attn_in['ln2_w'], 'L0_attn_ln2_b': _L0_attn_in['ln2_b'], 'L0_attn_skip_gate': _L0_attn_in['skip_gate'], 'L0_ffn_weight': _L0_ffn_in['weight']}

def reference(x, L0_tok_W, L0_tok_b, L0_tok_pos_emb, L0_attn_Wg, L0_attn_bg, L0_attn_Wq, L0_attn_Wk, L0_attn_Wv, L0_attn_Wo, L0_attn_A, L0_attn_Wb, L0_attn_Wc, L0_attn_Dp, L0_attn_W1, L0_attn_b1, L0_attn_W2, L0_attn_b2, L0_attn_ln1_w, L0_attn_ln1_b, L0_attn_ln2_w, L0_attn_ln2_b, L0_attn_skip_gate, L0_ffn_weight):
    import jax
    import jax.numpy as jnp

    def _L0_tok_ref(x, W, b, pos_emb):
        import jax, jax.numpy as jnp
        import numpy as np
        IMG, PS, C, OUT = (64, 16, 3, 256)
        NP = IMG // PS
        IN_FEAT = C * PS * PS
        B = x.shape[0]
        p = x.reshape(B, C, NP, PS, NP, PS).transpose(0, 1, 2, 4, 3, 5)
        p = p.transpose(0, 2, 3, 1, 4, 5)
        p = p.reshape(B, NP * NP, IN_FEAT)
        out = jnp.einsum('bnf,of->bno', p, W) + b + pos_emb
        return out

    def _L0_attn_ref(x, Wg, bg, Wq, Wk, Wv, Wo, A, Wb, Wc, Dp, W1, b1, W2, b2, ln1_w, ln1_b, ln2_w, ln2_b, skip_gate):
        import jax, jax.numpy as jnp
        import numpy as np
        B_, T_, D_, H_ = (2, 512, 256, 16)
        EPS = 1e-05

        def _layernorm(x, w, b):
            mu = jnp.mean(x, axis=-1, keepdims=True)
            var = jnp.mean(jnp.square(x - mu), axis=-1, keepdims=True)
            return (x - mu) * jax.lax.rsqrt(var + EPS) * w + b

        def _reference_tuple_inner(x, Wg, bg, Wq, Wk, Wv, Wo, A, Wb, Wc, Dp, W1, b1, W2, b2, ln1_w, ln1_b, ln2_w, ln2_b, skip_gate):
            B, T, D = x.shape
            H = H_
            hd = D // H
            scores = (x @ Wg)[..., 0] + bg[0]
            k = max(1, int(T * 0.25))
            _, idx = jax.lax.top_k(scores, k)
            mask = jnp.zeros((B, T), bool).at[jnp.arange(B)[:, None], idx].set(True)
            residual = x
            xn = _layernorm(x, ln1_w, ln1_b)
            q = (xn @ Wq).reshape(B, T, H, hd).transpose(0, 2, 1, 3)
            kk = (xn @ Wk).reshape(B, T, 1, hd).transpose(0, 2, 1, 3)
            vv = (xn @ Wv).reshape(B, T, 1, hd).transpose(0, 2, 1, 3)
            att = jax.nn.softmax(q @ jnp.swapaxes(kk, -1, -2) / np.sqrt(hd).astype(x.dtype), axis=-1)
            attn_out = (att @ vv).transpose(0, 2, 1, 3).reshape(B, T, D) @ Wo

            def step(h, xt):
                h = jnp.tanh(h @ A.T + xt @ Wb)
                y = h @ Wc + Dp * xt
                return (h, y)
            h0 = jnp.zeros((B, D), x.dtype)
            _, ys = jax.lax.scan(step, h0, jnp.swapaxes(xn, 0, 1))
            ssm_out = jnp.swapaxes(ys, 0, 1)
            deep_out = attn_out + ssm_out
            m = mask[..., None].astype(x.dtype)
            x2 = residual + deep_out * m + residual * skip_gate * (1.0 - m)
            xn2 = _layernorm(x2, ln2_w, ln2_b)
            ffn = jax.nn.gelu(xn2 @ W1 + b1, approximate=False) @ W2 + b2
            out = x2 + ffn
            return (out, scores)
        return _reference_tuple_inner(x, Wg, bg, Wq, Wk, Wv, Wo, A, Wb, Wc, Dp, W1, b1, W2, b2, ln1_w, ln1_b, ln2_w, ln2_b, skip_gate)[0]

    def _L0_ffn_ref(x, weight):
        import jax, jax.numpy as jnp
        import numpy as np
        IN_FEATURES = 256
        ACT_BITS = 4

        def _hadamard(size: int) -> np.ndarray:
            h = np.array([[1.0]], dtype=np.float64)
            while h.shape[0] < size:
                h = np.block([[h, h], [h, -h]])
            return (h / np.sqrt(size)).astype(np.float32)

        def _quantize_activations(x, bits=ACT_BITS):
            pos = 2 ** (bits - 1) - 1
            neg = 2 ** (bits - 1)
            scale = jnp.clip(jnp.max(jnp.abs(jax.lax.stop_gradient(x)), axis=-1, keepdims=True), 1e-05) / pos
            q = jnp.clip(jnp.round(x / scale), -neg, pos) * scale
            return x + jax.lax.stop_gradient(q - x)

        def _ternary_quantize_ste(w):
            scale = jnp.clip(jnp.mean(jnp.abs(jax.lax.stop_gradient(w)), axis=1, keepdims=True), 1e-05)
            n = w / scale
            tern = jnp.where(n > 0.5, 1.0, jnp.where(n < -0.5, -1.0, 0.0))
            q = tern * scale
            return w + jax.lax.stop_gradient(q - w)
        H = jnp.asarray(_hadamard(IN_FEATURES))
        xh = x @ H
        xq = _quantize_activations(xh)
        wq = _ternary_quantize_ste(weight)
        return jnp.einsum('bsi,oi->bso', xq, wq)
    h = _L0_tok_ref(x, L0_tok_W, L0_tok_b, L0_tok_pos_emb)
    h = _layernorm(h + _L0_attn_ref(h, L0_attn_Wg, L0_attn_bg, L0_attn_Wq, L0_attn_Wk, L0_attn_Wv, L0_attn_Wo, L0_attn_A, L0_attn_Wb, L0_attn_Wc, L0_attn_Dp, L0_attn_W1, L0_attn_b1, L0_attn_W2, L0_attn_b2, L0_attn_ln1_w, L0_attn_ln1_b, L0_attn_ln2_w, L0_attn_ln2_b, L0_attn_skip_gate), axis=-1)
    h = _layernorm(h + _L0_ffn_ref(h, L0_ffn_weight), axis=-1)
    return h

_drawn_inputs = setup_inputs


def setup_inputs(seed=0):
    import zlib

    import numpy as np

    out = dict(_drawn_inputs(seed))
    spreads = {'L0_attn_Dp': (1.0, 0.2),
     'L0_attn_b1': (0.0, 0.325),
     'L0_attn_b2': (0.0, 0.1),
     'L0_attn_ln1_w': (1.0, 0.2),
     'L0_attn_ln1_b': (0.0, 0.364),
     'L0_attn_ln2_w': (1.0, 0.6),
     'L0_attn_ln2_b': (0.0, 0.599)}
    factors = {'L0_tok_b': 3.021,
     'L0_attn_Wq': 8.0,
     'L0_attn_Wk': 8.0,
     'L0_attn_Wv': 5.871,
     'L0_attn_Wo': 5.882,
     'L0_attn_A': 8.0,
     'L0_attn_Wb': 2.853,
     'L0_attn_Wc': 2.856}
    for name, (base, spread) in spreads.items():
        noise = np.random.default_rng([zlib.crc32(name.encode()), seed]).standard_normal(out[name].shape)
        drawn = base * np.exp(spread * noise) if base else spread * noise
        out[name] = jnp.asarray(drawn.astype(out[name].dtype))
    for name, factor in factors.items():
        out[name] = (out[name] * factor).astype(out[name].dtype)
    return out
```

```python
from contextlib import ExitStack

import numpy as np

import concourse.bass as bass
from concourse import mybir

F32 = mybir.dt.float32
F32R = mybir.dt.float32r
ALU = mybir.AluOpType
ACT = mybir.ActivationFunctionType
AX = mybir.AxisListType

P = 128
B = 32
NP = 4
T = NP * NP
PS = 16
CH = 3
D = 256
C = D // P
H = 16
HD = D // H
HPC = P // HD
R = B * T
NT = R // P
TPT = T // NT
KT = CH * PS * PS // P
F = 4 * D
FJ = F // P
TOPK = T // 4
EPS = 1e-5
ROUND = 1.5 * 2.0 ** 23
QMAX, QMIN = 7.0, -8.0
NW = 8


def shape_constants():
    h = np.array([[1.0]])
    while h.shape[0] < D:
        h = np.block([[h, h], [h, -h]])
    h = (h / np.sqrt(D)).astype(np.float32).reshape(C, P, D).transpose(1, 0, 2).reshape(P, C * D)
    head = (np.arange(P)[:, None] // HD == np.arange(HPC)[None, :]).astype(np.float32)
    earlier = (np.arange(T)[None, :] < np.arange(T)[:, None]).astype(np.float32).reshape(1, T * T)
    spread = (np.arange(P)[:, None] % T == np.arange(P)[None, :] % T).astype(np.float32)
    consts = np.concatenate([np.eye(P, dtype=np.float32), head / np.sqrt(HD), head, spread,
                             np.repeat(earlier, P, 0), h], axis=1).astype(np.float32)
    token = np.arange(R) // B
    rows = np.concatenate([(token[None, :] == np.arange(T)[:, None]), np.ones((1, R))], 0).astype(np.float32)
    return np.ascontiguousarray(consts), np.ascontiguousarray(rows)


def vit_block(nc, x, tok_W, tok_b, tok_pos, Wg, bg, Wq, Wk, Wv, Wo, A, Wb, Wc, Dp, W1, b1, W2, b2,
              ln1_w, ln1_b, ln2_w, ln2_b, skip_gate, ffn_w, consts, row_sel, out):
    with ExitStack() as ctx:
        def sb(name, shape, dt=F32):
            return ctx.enter_context(nc.sbuf_tensor(name, shape, dt))

        def sem(name):
            return ctx.enter_context(nc.semaphore(name))

        cst = sb("cst", [P, 2 * P + 2 * HPC + T * T + C * D])
        o = P
        ident = cst[:, 0:P]
        mask_k = cst[:, o:o + HPC]
        mask_v = cst[:, o + HPC:o + 2 * HPC]
        o += 2 * HPC
        spread = cst[:, o:o + P]
        o += P
        earlier = cst[:, o:o + T * T]
        hadamard = cst[:, o + T * T:]
        sel = sb("sel", [T + 1, R])
        posb = sb("posb", [T + 1, D])
        a_in = sb("a_in", [P, C, D])
        AT = sb("AT", [P, C, D])

        def carve(tensor, *shapes):
            at, views = 0, []
            for shape in shapes:
                size = int(np.prod(shape))
                names = " ".join("abcd"[:len(shape)])
                views.append(tensor[:, at:at + size].rearrange(f"p ({names}) -> p {names}",
                                                               **dict(zip("abcd", shape))))
                at += size
            return views

        early = sb("early", [P, CH * (PS * NP * PS + C * PS * PS)])
        x_in, w_in = carve(early, (CH, PS * NP * PS), (CH, C, PS * PS))
        kblk, dw, db = carve(early, (B, HPC, T), (D,), (D,))
        early_r = sb("early_r", [P, 2 * KT * (R + D)], F32R)
        xT_hi, xT_lo, tokWT_hi, tokWT_lo = carve(early_r, (KT, R), (KT, R), (KT, D), (KT, D))
        g_hi, g_lo, hid_hi, hid_lo, ternT_hi, ternT_lo, quantT = carve(
            early_r, (FJ, D), (FJ, D), (C, R), (C, R), (C, D), (C, D), (NT, C, P))
        proj_in = sb("proj_in", [P, 4 * C * D])
        wb_in, wq_in, wc_in, wo_in = carve(proj_in, *[(C, D)] * 4)
        vblk = [carve(t, (B // 2, HPC, HD))[0] for t in (proj_in, early)]

        def halves(name, chunks, cols):
            return sb(name + "_hi", [P, chunks, cols], F32R), sb(name + "_lo", [P, chunks, cols], F32R)

        wb_hi, wb_lo = halves("wb", C, D)
        wq_hi, wq_lo = halves("wq", C, D)
        wc_hi, wc_lo = halves("wc", C, D)
        wo_hi, wo_lo = halves("wo", C, D)
        w1_hi, w1_lo = halves("w1", C, F)
        w2_hi, w2_lo = halves("w2", FJ, D)
        ff_space = sb("ff_space", [P, C * F + FJ * D])
        x_by_patch, = carve(ff_space, (CH, 2, NP, P))
        w1_in, w2_in = carve(ff_space, (C, F), (FJ, D))
        g, s_rows, h2 = carve(ff_space, (FJ, D), (NT, D), (NT, D))
        wk_in = sb("wk_in", [P, C, HD])
        wv_in = sb("wv_in", [P, C, HD])
        wk_hi = sb("wk_hi", [P, C, P], F32R)
        wk_lo = sb("wk_lo", [P, C, P], F32R)
        wv_hi = sb("wv_hi", [P, C, P], F32R)
        wv_lo = sb("wv_lo", [P, C, P], F32R)
        had = sb("had", [P, C, D], F32R)
        ln1w = sb("ln1w", [P, C])
        ln1b = sb("ln1b", [P, C])
        ln2w = sb("ln2w", [P, C])
        ln2b = sb("ln2b", [P, C])
        b1c = sb("b1c", [P, FJ])
        wg_row = sb("wg_row", [P, D])
        b2_row = sb("b2_row", [P, D])
        dp_row = sb("dp_row", [P, D])
        l1w_row = sb("l1w_row", [P, D])
        l1b_row = sb("l1b_row", [P, D])
        bg_col = sb("bg_col", [P, 1])
        sg_col = sb("sg_col", [P, 1])
        fw_in = sb("fw_in", [P, C, D])
        neg_half = sb("neg_half", [P, NT])

        h = sb("h", [P, NT, D])
        hb2_space = sb("hb2_space", [P, NT * D])
        (hb2,), (gt, eq, junk) = carve(hb2_space, (NT, D)), carve(hb2_space, (T, T), (T, T), (D,))
        gt, eq = gt[0:B], eq[0:B]
        base2 = hb2
        xhat = sb("xhat", [P, NT, D])
        skip = xhat
        x2 = sb("x2", [P, NT, D])
        hc = x2
        xn_space = sb("xn_space", [P, C * R])
        xn, = carve(xn_space, (C, R))
        krep = xn_space[:, 0:R]
        vT = xn_space[0:HD, R:2 * R]
        xn2, = carve(xn_space, (2, C, D))
        xn_hi_space = sb("xn_hi_space", [P, C * R], F32R)
        xn_lo_space = sb("xn_lo_space", [P, C * R], F32R)
        (xn_hi,), (xn_lo,) = carve(xn_hi_space, (C, R)), carve(xn_lo_space, (C, R))
        (xn2_hi,), (xn2_lo,) = carve(xn_hi_space, (2, C, D)), carve(xn_lo_space, (2, C, D))
        q_space = sb("q_space", [P, B * C * T])
        (qT,), (x2hat,), (o_rows,) = carve(q_space, (B, C, T)), carve(q_space, (NT, D)), carve(q_space, (NT, D))
        st_sb = sb("st_sb", [P, B * C * T])
        pT = st_sb
        f_rows, = carve(st_sb, (NT, D))
        tern, = carve(st_sb, (C, D))
        prob_space = sb("prob_space", [P, B * C * T])
        (prob,), (quant,) = carve(prob_space, (2, 32, T)), carve(prob_space, (NT, D))
        wpos, wneg = carve(prob_space, (C, D), (C, D))
        v_masked, = carve(prob_space, (HPC, NT, HD))
        o_hi_space = sb("o_hi_space", [P, C * R], F32R)
        o_lo_space = sb("o_lo_space", [P, C * R], F32R)
        (oT_hi,), (oT_lo,) = carve(o_hi_space, (C, R)), carve(o_lo_space, (C, R))
        (h2T_hi,), (h2T_lo,) = carve(o_hi_space, (NT, C, P)), carve(o_lo_space, (NT, C, P))
        stats = sb("stats", [P, NT, 6])
        mv = sb("mv", [P, NT, 2])
        var = sb("var", [P, NT])
        rstd = sb("rstd", [P, NT])
        hid = sb("hid", [P, C, R])
        v_sd = sb("v_sd", [P, B, HD])
        smax = sb("smax", [P, 2, 32])
        ssum = sb("ssum", [P, 2, 32])
        srec = sb("srec", [P, 2, 32])
        sc_rows = sb("sc_rows", [P, NT])
        sc = sb("sc", [B, T])
        rank = sb("rank", [B, T])
        m_bt = sb("m_bt", [B, T])
        m_rows = sb("m_rows", [P, NT])
        c_rows = sb("c_rows", [P, NT])
        gate = sb("gate", [P, 2])
        amax = sb("amax", [P, NT])
        qscale = sb("qscale", [P, NT])
        qinv = sb("qinv", [P, NT])
        wsc = sb("wsc", [P, 3, C])
        bank = [ctx.enter_context(nc.psum_tensor(f"bank{i}", [P, 512], F32)) for i in range(8)]

        def scan_bank(m, par):
            return bank[2 * m + par]

        ld_cst, ld_sel, ld_a = sem("ld_cst"), sem("ld_sel"), sem("ld_a")
        ld_x = [sem(f"ld_x{c}") for c in range(CH)]
        ld_w = [sem(f"ld_tok{c}") for c in range(CH)]
        ld_ln, ld_wb, ld_wkv, ld_wq = sem("ld_ln"), sem("ld_wb"), sem("ld_wkv"), sem("ld_wq")
        ld_wc, ld_wo, ld_rows, ld_gates, ld_fw = sem("ld_wc"), sem("ld_wo"), sem("ld_rows"), sem("ld_gates"), sem("ld_fw")
        ld_w1, ld_w2, stored = sem("ld_w1"), sem("ld_w2"), sem("stored")
        x_grouped_dve, x_grouped_pool = sem("x_grouped_dve"), sem("x_grouped_pool")
        vm_T, vm_ready = sem("vm_T"), sem("vm_ready")
        unit_T, unit_hi, unit_lo = sem("unit_T"), sem("unit_hi"), sem("unit_lo")
        a_T, a_ready = sem("a_T"), sem("a_ready")
        tok_done, h_ready, var1, rstd1 = sem("tok_done"), sem("h_ready"), sem("var1"), sem("rstd1")
        xhat_ready, xhat_T, xn_c0, xn_split = sem("xhat_ready"), sem("xhat_T"), sem("xn_c0"), sem("xn_split")
        wb_split, wkv_split, wq_split, wco_split = sem("wb_split"), sem("wkv_split"), sem("wq_split"), sem("wco_split")
        had_ready, w1_hi_ready, w1_lo_ready, w2_hi_ready, w2_lo_ready = (
            sem("had_ready"), sem("w1_hi_ready"), sem("w1_lo_ready"), sem("w2_hi_ready"), sem("w2_lo_ready"))
        neg_half_ready = sem("neg_half_ready")
        pre_done, step_m0, step_m1 = sem("pre_done"), sem("step_m0"), sem("step_m1")
        state_m0, state_m1, hid_split = sem("state_m0"), sem("state_m1"), sem("hid_split")
        k_done, krep_ready, kblk_ready = sem("k_done"), sem("krep_ready"), sem("kblk_ready")
        v_done, vT_ready, vsd_done, vsd_ready = sem("v_done"), sem("vT_ready"), sem("vsd_done"), sem("vsd_ready")
        vblk_dve, vblk_pool = sem("vblk_dve"), sem("vblk_pool")
        q0_done, q1_done, q0_ready, q1_ready = sem("q0_done"), sem("q1_done"), sem("q0_ready"), sem("q1_ready")
        st_done, st_ready, s_done, s_shifted = sem("st_done"), sem("st_ready"), sem("s_done"), sem("s_shifted")
        exp_done, prob_ready, pT_done, pT_ready = sem("exp_done"), sem("prob_ready"), sem("pT_done"), sem("pT_ready")
        o_done, o_hi, o_lo = sem("o_done"), sem("o_hi"), sem("o_lo")
        mask_ready, skip_ready, hc_ready, hb2_ready = sem("mask_ready"), sem("skip_ready"), sem("hc_ready"), sem("hb2_ready")
        y_done, x2_ready, base2_ready, var2, rstd2 = sem("y_done"), sem("x2_ready"), sem("base2_ready"), sem("var2"), sem("rstd2")
        x2hat_ready, x2hat_T, xn2_chunk, xn2_split = sem("x2hat_ready"), sem("x2hat_T"), sem("xn2_chunk"), sem("xn2_split")
        up_done, gelu_done, g_split, down_done = sem("up_done"), sem("gelu_done"), sem("g_split"), sem("down_done")
        var3, rstd3, h2_ready, h2_T, h2T_hi_s, h2T_lo_s = (
            sem("var3"), sem("rstd3"), sem("h2_ready"), sem("h2_T"), sem("h2T_hi_s"), sem("h2T_lo_s"))
        had_done, quant_ready, quant_T, quantT_ready = sem("had_done"), sem("quant_ready"), sem("quant_T"), sem("quantT_ready")
        tern_ready, tern_T, ternT_hi_s, ternT_split = sem("tern_ready"), sem("tern_T"), sem("ternT_hi_s"), sem("ternT_split")
        fin_done, var4, rstd4, out_ready = sem("fin_done"), sem("var4"), sem("rstd4"), sem("out_ready")
        dve_done = sem("dve_done")
        pool_done = sem("pool_done")

        block = ctx.enter_context(nc.Block())

        units = [(c, part) for c in range(CH) for part in ("w", 0, 1)]

        def unit_bank(u):
            return bank[4 + u % 4]

        def pair_cols(p):
            return slice(p * 2 * P, (p + 1) * 2 * P)

        def tile_cols(t):
            return slice(t * P, (t + 1) * P)

        down_bank = [bank[7], bank[4], bank[5], bank[6]]

        def group_patches(engine, c, part):
            half = PS // 2
            src = x_in[:, c].rearrange("p (r j q) -> p j r q", r=PS, j=NP)[:, :, part * half:(part + 1) * half]
            dst = x_by_patch[:, c, part].rearrange("p j (r q) -> p j r q", r=half)
            return engine.tensor_copy(dst, src)

        @block.sync
        def _(sp):
            sp.dma_start(cst[:], consts).then_inc(ld_cst, 16)
            sp.dma_start(sel[:], row_sel).then_inc(ld_sel, 16)
            sp.dma_start(posb[0:T, :], tok_pos).then_inc(ld_sel, 16)
            sp.dma_start(posb[T:T + 1, :], tok_b.rearrange("(a d) -> a d", a=1)).then_inc(ld_sel, 16)
            for c in range(CH):
                sp.dma_start(w_in[:, c], tok_W.rearrange("(a p) (c f) -> p c a f", p=P, c=CH)[:, c]).then_inc(ld_w[c], 16)
                for i in range(NP):
                    sp.dma_start(x_in[B * i:B * i + B, c], x[:, c, PS * i:PS * i + PS, :].rearrange(
                        "b r w -> b (r w)")).then_inc(ld_x[c], 16)
            sp.dma_start(a_in[:], A.rearrange("(a p) n -> p a n", p=P)).then_inc(ld_a, 16)
            sp.dma_start(wb_in[:], Wb.rearrange("(a p) n -> p a n", p=P)).then_inc(ld_wb, 16)
            for dst, src in ((ln1w, ln1_w), (ln1b, ln1_b), (ln2w, ln2_w), (ln2b, ln2_b)):
                sp.dma_start(dst[:], src.rearrange("(a p) -> p a", p=P), allow_slow_non_contiguous=True).then_inc(ld_ln, 16)
            sp.dma_start(wk_in[:], Wk.rearrange("(a p) n -> p a n", p=P)).then_inc(ld_wkv, 16)
            sp.dma_start(wv_in[:], Wv.rearrange("(a p) n -> p a n", p=P)).then_inc(ld_wkv, 16)
            sp.dma_start(wq_in[:], Wq.rearrange("(a p) n -> p a n", p=P)).then_inc(ld_wq, 16)
            sp.dma_start(bg_col[:], bg.partition_broadcast(P)).then_inc(ld_gates, 16)
            sp.dma_start(sg_col[:], skip_gate.partition_broadcast(P)).then_inc(ld_gates, 16)
            sp.dma_start(wg_row[:], Wg.rearrange("d a -> (d a)").partition_broadcast(P)).then_inc(ld_gates, 16)
            for dst, src in ((dp_row, Dp), (l1w_row, ln1_w), (l1b_row, ln1_b), (b2_row, b2)):
                sp.dma_start(dst[:], src.partition_broadcast(P)).then_inc(ld_rows, 16)
            sp.dma_start(wc_in[:], Wc.rearrange("(a p) n -> p a n", p=P)).then_inc(ld_wc, 16)
            sp.dma_start(wo_in[:], Wo.rearrange("(a p) n -> p a n", p=P)).then_inc(ld_wo, 16)
            sp.dma_start(fw_in[:], ffn_w.rearrange("(a p) n -> p a n", p=P)).then_inc(ld_fw, 16)
            sp.wait_ge(unit_T, len(units))
            sp.dma_start(w1_in[:], W1.rearrange("(a p) n -> p a n", p=P)).then_inc(ld_w1, 16)
            sp.dma_start(b1c[:], b1.rearrange("(a p) -> p a", p=P), allow_slow_non_contiguous=True).then_inc(ld_w1, 16)
            sp.dma_start(w2_in[:], W2.rearrange("(a p) n -> p a n", p=P)).then_inc(ld_w2, 16)
            for t in range(NT):
                sp.wait_ge(out_ready, t + 1)
                for k in range(TPT):
                    sp.dma_start(out[:, TPT * t + k, :], o_rows[B * k:B * k + B, t]).then_inc(stored, 16)
            sp.wait_ge(stored, 16 * NT * TPT)

        @block.tensor
        def _(pe):
            def tr(dst, src, identity=None):
                return nc.tensor.transpose(dst, src, ident if identity is None else identity)

            def product(dst, lhs, rhs, first=True, last=True, check=False):
                n = len(lhs)
                for i in range(n):
                    passes = [(0, 0)] + ([(0, 1)] if rhs[i][1] is not None else []) + ([(1, 0)] if lhs[i][1] is not None else [])
                    for j, (a, b) in enumerate(passes):
                        ins = nc.tensor.matmul(dst, lhs[i][a], rhs[i][b], start=first and i == 0 and j == 0,
                                               stop=last and i == n - 1 and j == len(passes) - 1, skip_group_check=check)
                return ins

            pe.wait_ge(ld_sel, 48)
            for t in range(NT):
                nc.tensor.matmul(bank[t][:, 0:D], sel[:, tile_cols(t)], posb[:, :], start=True, stop=False)

            def unit_transposes(u):
                c, part = units[u]
                if u >= 4:
                    pe.wait_ge(unit_lo, u - 3)
                dst = unit_bank(u)
                if part == "w":
                    pe.wait_ge(ld_w[c], 16)
                    for hf in range(2):
                        for a in range(C):
                            k = hf * C + a
                            ins = tr(dst[:, k * P:(k + 1) * P], w_in[:, c, a, hf * P:(hf + 1) * P])
                else:
                    pe.wait_ge((x_grouped_dve, x_grouped_pool)[part], c + 1)
                    for j in range(NP):
                        ins = tr(dst[:, j * P:(j + 1) * P], x_by_patch[:, c, part, j])
                ins.then_inc(unit_T, 1)

            def patch_product(k):
                c, part = k // 2, k % 2
                pe.wait_ge(unit_lo, 3 * c + part + 2)
                for t in range(NT):
                    ins = product(bank[t][:, 0:D], [(xT_hi[:, k, tile_cols(t)], xT_lo[:, k, tile_cols(t)])],
                                  [(tokWT_hi[:, k], tokWT_lo[:, k])], first=False, last=(k == KT - 1))
                    if k == KT - 1:
                        ins.then_inc(tok_done, 1)

            pe.wait_ge(ld_cst, 16)
            for u in (0, 1, 2, 3):
                unit_transposes(u)
            patch_product(0)
            unit_transposes(4)
            patch_product(1)
            unit_transposes(5)
            patch_product(2)
            unit_transposes(6)
            patch_product(3)
            unit_transposes(7)
            unit_transposes(8)
            patch_product(4)
            pe.wait_ge(ld_a, 16)
            pe.wait_ge(unit_lo, 6)
            for k in range(C):
                for a in range(C):
                    ins = tr(bank[5][:, (2 * k + a) * P:(2 * k + a + 1) * P], a_in[:, a, k * P:(k + 1) * P])
            ins.then_inc(a_T, 1)
            patch_product(5)

            pe.wait_ge(unit_lo, 8)
            for p in range(2):
                for t in (2 * p, 2 * p + 1):
                    pe.wait_ge(xhat_ready, t + 1)
                    for c in range(C):
                        ins = tr(bank[6 + c][:, tile_cols(t)], xhat[:, t, c * P:(c + 1) * P])
                ins.then_inc(xhat_T, 1)
                if p == 0:
                    pe.wait_ge(xn_c0, 1)
                    pe.wait_ge(xn_split, 1)

            def scan_inputs(p, par):
                for m in range(C):
                    rhs = [tuple(v[:, k, pair_cols(p)].rearrange("q (u e b) -> q u e b", e=2, b=B)[:, :, par, :]
                                 for v in (xn_hi, xn_lo)) for k in range(C)]
                    lhs = [(wb_hi[:, k, m * P:(m + 1) * P], wb_lo[:, k, m * P:(m + 1) * P]) for k in range(C)]
                    ins = product(scan_bank(m, par)[:, p * P:(p + 1) * P], lhs, rhs, first=(p == 0), last=(p == 1), check=True)
                ins.then_inc(pre_done, 1)

            pe.wait_ge(wb_split, 1)
            pe.wait_ge(h_ready, NT)
            scan_inputs(0, 0)
            scan_inputs(0, 1)
            pe.wait_ge(a_ready, 1)

            def scan_step(t):
                dst = [scan_bank(m, t % 2)[:, t // 2 * B:(t // 2 + 1) * B] for m in range(C)]
                for k, state in ((0, state_m0), (1, state_m1)):
                    pe.wait_ge(state, t)
                    for m in range(C):
                        ins = nc.tensor.matmul(dst[m], AT[:, k, m * P:(m + 1) * P], hid[:, k, (t - 1) * B:t * B],
                                               start=False, stop=(k == 1), skip_group_check=True)
                        if k == 1:
                            ins.then_inc((step_m0, step_m1)[m], 1)

            xn_pairs = [(xn_hi[:, k], xn_lo[:, k]) for k in range(C)]

            scan_step(1)
            pe.wait_ge(xn_split, 2)
            scan_inputs(1, 0)
            scan_step(2)
            scan_inputs(1, 1)
            scan_step(3)
            pe.wait_ge(unit_lo, 9)
            pe.wait_ge(wkv_split, 1)
            product(bank[4][:, :], [(wk_hi[:, k], wk_lo[:, k]) for k in range(C)], xn_pairs).then_inc(k_done, 1)
            scan_step(4)
            product(bank[5][:, :], [(wv_hi[:, k], wv_lo[:, k]) for k in range(C)], xn_pairs).then_inc(v_done, 1)

            def queries(m, done):
                pe.wait_ge(xn_c0, 2)
                pe.wait_ge(wq_split, 1)
                product(bank[6 + m][:, :], [(wq_hi[:, k, m * P:(m + 1) * P], wq_lo[:, k, m * P:(m + 1) * P])
                                            for k in range(C)], xn_pairs).then_inc(done, 1)

            scan_step(5)
            queries(0, q0_done)
            scan_step(6)
            queries(1, q1_done)
            scan_step(7)
            pe.wait_ge(krep_ready, 1)
            pe.wait_ge(vT_ready, 1)
            for t in range(NT):
                ins = tr(bank[5][:, t * HD:(t + 1) * HD], vT[:, t * P:(t + 1) * P], ident[0:HD, 0:HD])
            ins.then_inc(vm_T, 1)
            pe.wait_ge(vm_ready, 1)
            nc.tensor.matmul(bank[4][:, :], spread, v_masked.rearrange("p e t d -> p (e t d)"),
                             start=True, stop=True).then_inc(vsd_done, 1)
            pe.wait_ge(tern_ready, 1)
            for k in range(C):
                for a in range(C):
                    ins = tr(bank[5][:, (2 * k + a) * P:(2 * k + a + 1) * P], tern[:, a, k * P:(k + 1) * P])
            ins.then_inc(tern_T, 1)

            def scores(n):
                pe.wait_ge((q0_ready, q1_ready)[n], 1)
                if n == 0:
                    pe.wait_ge(q1_ready, 1)
                for b in range(16 * n, 16 * n + 16):
                    if b % NW == 0:
                        pe.wait_ge(kblk_ready, b // NW + 1)
                    ins = nc.tensor.matmul(bank[6 + n][:, (b % 16) * 32:(b % 16 + 1) * 32],
                                           kblk[:, b].rearrange("p h s -> p (h s)"),
                                           qT[:, b].rearrange("p c t -> p (c t)"), start=True, stop=True)
                ins.then_inc(st_done, 1)

            def scores_to_rows(n):
                pe.wait_ge(st_ready, n + 1)
                pe.wait_ge((vsd_ready, ternT_split)[n], 1)
                for i in range(4):
                    ins = tr(bank[4 + n][:, i * P:(i + 1) * P], st_sb[:, n * 512 + i * P:n * 512 + (i + 1) * P])
                ins.then_inc(s_done, 1)

            def probs_to_keys(n):
                pe.wait_ge(prob_ready, n + 1)
                for i in range(4):
                    ins = tr(bank[6 + n][:, i * P:(i + 1) * P],
                             prob[:, n, i * 8:i * 8 + 8, :].rearrange("p h s -> p (h s)"))
                ins.then_inc(pT_done, 1)

            def attend(n):
                pe.wait_ge(pT_ready, n + 1)
                if n == 0:
                    pe.wait_ge(vblk_dve, 2)
                else:
                    pe.wait_ge(vblk_pool, 2)
                for b in range(16 * n, 16 * n + 16):
                    ins = nc.tensor.matmul(bank[6 + n][:, (b % 16) * 32:(b % 16 + 1) * 32],
                                           vblk[n][:, b % 16].rearrange("p h d -> p (h d)"), pT[:, b * 32:(b + 1) * 32],
                                           start=True, stop=True)
                ins.then_inc(o_done, 1)

            def mix_dst(t):
                return bank[4 + t // 2][:, (t % 2) * D:(t % 2 + 1) * D]

            def mix_states(t):
                pe.wait_ge(s_shifted, t // 2 + 1)
                pe.wait_ge(hid_split, t + 1)
                pe.wait_ge(wco_split, 1)
                product(mix_dst(t), [(hid_hi[:, k, tile_cols(t)], hid_lo[:, k, tile_cols(t)]) for k in range(C)],
                        [(wc_hi[:, k], wc_lo[:, k]) for k in range(C)], first=(t % 2 == 0), last=False, check=True)

            def mix_heads(t):
                pe.wait_ge(wco_split, 2)
                pe.wait_ge(o_lo, 2)
                product(mix_dst(t), [(oT_hi[:, k, tile_cols(t)], oT_lo[:, k, tile_cols(t)]) for k in range(C)],
                        [(wo_hi[:, k], wo_lo[:, k]) for k in range(C)], first=False, last=True, check=True).then_inc(y_done, 1)

            scan_step(8)
            scores(0)
            scan_step(9)
            scores(1)
            scan_step(10)
            scores_to_rows(0)
            scan_step(11)
            scores_to_rows(1)
            scan_step(12)
            mix_states(0)
            scan_step(13)
            mix_states(1)
            probs_to_keys(0)
            scan_step(14)
            mix_states(2)
            probs_to_keys(1)
            attend(0)
            scan_step(15)
            attend(1)
            mix_states(3)
            mix_heads(0)
            mix_heads(1)
            mix_heads(2)
            mix_heads(3)

            def norm2_transposes(p):
                pe.wait_ge(x2hat_ready, 2 * p + 2)
                if p == 0:
                    pe.wait_ge(o_lo, 2)
                for t in range(2):
                    for c in range(C):
                        ins = tr(bank[6][:, c * D + t * P:c * D + (t + 1) * P], x2hat[:, 2 * p + t, c * P:(c + 1) * P])
                ins.then_inc(x2hat_T, 1)

            def up(p, j):
                n = p * FJ + j
                if n == 0:
                    pe.wait_ge(state_m0, T)
                    pe.wait_ge(state_m1, T)
                    pe.wait_ge(w1_hi_ready, 1)
                    pe.wait_ge(w1_lo_ready, 1)
                if n >= 4:
                    pe.wait_ge(gelu_done, n - 3)
                if j == 0:
                    pe.wait_ge(xn2_split, p + 1)
                product(bank[j % 4][:, (j // 4) * D:(j // 4 + 1) * D],
                        [(w1_hi[:, k, j * P:(j + 1) * P], w1_lo[:, k, j * P:(j + 1) * P]) for k in range(C)],
                        [(xn2_hi[:, p, k], xn2_lo[:, p, k]) for k in range(C)]).then_inc(up_done, 1)

            def down(t):
                p, i = t // 2, t % 2
                pe.wait_ge(w2_hi_ready, 1)
                pe.wait_ge(w2_lo_ready, 1)
                if t == 0:
                    pe.wait_ge(o_lo, 2)
                elif t == 3:
                    pe.wait_ge(xn2_split, 2)
                else:
                    pe.wait_ge(x2_ready, 2 * t)
                for j in range(FJ):
                    pe.wait_ge(g_split, p * FJ + j + 1)
                    ins = product(down_bank[t][:, 0:D], [(g_hi[:, j, i * P:(i + 1) * P], g_lo[:, j, i * P:(i + 1) * P])],
                                  [(w2_hi[:, j], w2_lo[:, j])], first=(j == 0), last=(j == FJ - 1))
                ins.then_inc(down_done, 1)

            def tail_transposes(t):
                pe.wait_ge(h2_ready, t + 1)
                for c in range(C):
                    ins = tr(down_bank[t][:, c * P:(c + 1) * P], h2[:, t, c * P:(c + 1) * P])
                ins.then_inc(h2_T, 1)

            def rotate(t):
                pe.wait_ge(had_ready, 1)
                pe.wait_ge(h2T_lo_s, t + 1)
                product(down_bank[t][:, 0:D], [(h2T_hi[:, t, k], h2T_lo[:, t, k]) for k in range(C)],
                        [(had[:, k], None) for k in range(C)]).then_inc(had_done, 1)

            def quant_transposes(t):
                pe.wait_ge(quant_ready, t + 1)
                for c in range(C):
                    ins = tr(down_bank[t][:, c * P:(c + 1) * P], quant[:, t, c * P:(c + 1) * P])
                ins.then_inc(quant_T, 1)

            def ternary(t):
                pe.wait_ge(quantT_ready, t + 1)
                product(down_bank[t][:, 0:D], [(quantT[:, t, k], None) for k in range(C)],
                        [(ternT_hi[:, k], ternT_lo[:, k]) for k in range(C)]).then_inc(fin_done, 1)

            norm2_transposes(0)
            for j in range(FJ):
                up(0, j)
            down(0)
            norm2_transposes(1)
            down(1)
            up(1, 0)
            up(1, 1)
            tail_transposes(0)
            up(1, 2)
            tail_transposes(1)
            up(1, 3)
            rotate(0)
            up(1, 4)
            rotate(1)
            up(1, 5)
            up(1, 6)
            quant_transposes(0)
            up(1, 7)
            quant_transposes(1)
            ternary(0)
            ternary(1)
            down(2)
            down(3)
            tail_transposes(2)
            rotate(2)
            tail_transposes(3)
            quant_transposes(2)
            rotate(3)
            ternary(2)
            quant_transposes(3)
            ternary(3)

        @block.scalar
        def _(act):
            def unit_views(u):
                c, part = units[u]
                if part == "w":
                    dst = [v[:, 2 * c:2 * c + 2].rearrange("p k n -> p (k n)") for v in (tokWT_hi, tokWT_lo)]
                    return unit_bank(u)[:, :], *dst
                src = unit_bank(u)[:, :].rearrange("p (j i b) -> p j i b", j=NP, i=NP)
                return src, *[v[:, 2 * c + part].rearrange("p (i j b) -> p j i b", i=NP, j=NP) for v in (xT_hi, xT_lo)]

            for u in range(len(units)):
                act.wait_ge(unit_T, u + 1)
                src, hi, _lo = unit_views(u)
                nc.scalar.copy(hi, src).then_inc(unit_hi, 1)
            act.wait_ge(a_T, 1)
            nc.scalar.copy(AT[:].rearrange("p k n -> p (k n)"), bank[5][:, :]).then_inc(a_ready, 1)
            for t in range(NT):
                act.wait_ge(tok_done, t + 1)
                nc.scalar.copy(h[:, t], bank[t][:, 0:D]).then_inc(h_ready, 1)
            act.wait_ge(ld_ln, 64)

            def norm1(p):
                act.wait_ge(xhat_T, p + 1)
                nc.scalar.activation(xn[:, 0, pair_cols(p)], bank[6][:, pair_cols(p)], ACT.Identity,
                                     scale=ln1w[:, 0:1], bias=ln1b[:, 0:1]).then_inc(xn_c0, 1)

            def tanh_step(t):
                for m, (step, state) in enumerate(((step_m0, state_m0), (step_m1, state_m1))):
                    if t == 0:
                        act.wait_ge(pre_done, 1)
                    else:
                        act.wait_ge(step, t)
                    nc.scalar.activation(hid[:, m, t * B:(t + 1) * B], scan_bank(m, t % 2)[:, t // 2 * B:(t // 2 + 1) * B],
                                         ACT.Tanh).then_inc(state, 1)

            def copy_after(ready, n, dst, src, done):
                act.wait_ge(ready, n)
                nc.scalar.copy(dst, src).then_inc(done, 1)

            norm1(0)
            tanh_step(0)
            norm1(1)
            tanh_step(1)
            tanh_step(2)
            tanh_step(3)
            act.wait_ge(ld_w1, 32)
            nc.scalar.copy(w1_hi[:, 0], w1_in[:, 0])
            copy_after(k_done, 1, krep[:, :], bank[4][:, :], krep_ready)
            tanh_step(4)
            copy_after(v_done, 1, vT.rearrange("p (b s) -> p s b", b=B),
                       bank[5][0:HD, :].rearrange("p (s b) -> p s b", b=B), vT_ready)
            tanh_step(5)
            copy_after(q0_done, 1, qT[:, :, 0, :].rearrange("p b t -> p t b"),
                       bank[6][:, :].rearrange("p (t b) -> p t b", b=B), q0_ready)
            tanh_step(6)
            nc.scalar.copy(w1_hi[:, 1], w1_in[:, 1]).then_inc(w1_hi_ready, 1)
            tanh_step(7)
            copy_after(vsd_done, 1, v_sd[:].rearrange("p (t e) d -> p e t d", e=HPC),
                       bank[4][:, :].rearrange("p (e t d) -> p e t d", e=HPC, t=NT), vsd_ready)
            copy_after(tern_T, 1, ternT_hi[:].rearrange("p k n -> p (k n)"), bank[5][:, :], ternT_hi_s)
            tanh_step(8)
            copy_after(st_done, 1, st_sb[:, 0:512], bank[6][:, :], st_ready)
            tanh_step(9)
            copy_after(st_done, 2, st_sb[:, 512:1024], bank[7][:, :], st_ready)
            tanh_step(10)

            def exp_half(n):
                act.wait_ge(s_shifted, n + 1)
                v = prob[:, n].rearrange("p h s -> p (h s)")
                nc.scalar.activation(v, v, ACT.Exp).then_inc(exp_done, 1)

            exp_half(0)
            tanh_step(11)
            exp_half(1)
            tanh_step(12)
            act.wait_ge(ld_w2, 16)
            nc.scalar.copy(w2_hi[:, 0:4], w2_in[:, 0:4])
            tanh_step(13)
            copy_after(pT_done, 1, pT[:, 0:512], bank[6][:, :], pT_ready)
            tanh_step(14)
            copy_after(pT_done, 2, pT[:, 512:1024], bank[7][:, :], pT_ready)

            def heads_hi(n):
                act.wait_ge(o_done, n + 1)
                for c in range(C):
                    ins = nc.scalar.copy(
                        oT_hi[:, c].rearrange("p (t b) -> p b t", b=B)[:, 16 * n:16 * n + 16],
                        bank[6 + n][:, :].rearrange("p (b c t) -> p b c t", c=C, t=T)[:, :, c])
                ins.then_inc(o_hi, 1)

            heads_hi(0)
            tanh_step(15)
            heads_hi(1)
            nc.scalar.copy(w2_hi[:, 4:8], w2_in[:, 4:8]).then_inc(w2_hi_ready, 1)

            def norm2(p):
                act.wait_ge(x2hat_T, p + 1)
                for c in range(C):
                    nc.scalar.activation(xn2[:, p, c], bank[6][:, c * D:(c + 1) * D], ACT.Identity,
                                         scale=ln2w[:, c:c + 1], bias=ln2b[:, c:c + 1]).then_inc(xn2_chunk, 1)

            def gelu(p, j):
                n = p * FJ + j
                act.wait_ge(up_done, n + 1)
                if n >= FJ:
                    act.wait_ge(g_split, n - FJ + 1)
                nc.scalar.activation(g[:, j], bank[j % 4][:, (j // 4) * D:(j // 4 + 1) * D], ACT.Gelu,
                                     bias=b1c[:, j:j + 1]).then_inc(gelu_done, 1)

            def tail_hi(t):
                act.wait_ge(h2_T, t + 1)
                nc.scalar.copy(h2T_hi[:, t].rearrange("p k n -> p (k n)"), down_bank[t][:, 0:D]).then_inc(h2T_hi_s, 1)

            def quant_copy(t):
                act.wait_ge(quant_T, t + 1)
                nc.scalar.activation(quantT[:, t].rearrange("p k n -> p (k n)"), down_bank[t][:, 0:D], ACT.Copy,
                                     bias=-ROUND).then_inc(quantT_ready, 1)

            norm2(0)
            for j in range(FJ):
                gelu(0, j)
            norm2(1)
            gelu(1, 0)
            gelu(1, 1)
            tail_hi(0)
            gelu(1, 2)
            tail_hi(1)
            for j in range(3, 7):
                gelu(1, j)
            quant_copy(0)
            gelu(1, 7)
            quant_copy(1)
            tail_hi(2)
            tail_hi(3)
            quant_copy(2)
            quant_copy(3)

        @block.vector
        def _(dve):
            count = [0]

            def step(ins):
                ins.then_inc(dve_done, 1)
                count[0] += 1
                return count[0]

            def after(n):
                dve.wait_ge(dve_done, n)

            def lo_part(dst, full, hi):
                return nc.vector.tensor_tensor(dst, full, hi.bitcast(F32), ALU.subtract)

            dve.wait_ge(ld_x[0], 16 * NP)
            group_patches(nc.vector, 0, 0).then_inc(x_grouped_dve, 1)
            for u in range(len(units)):
                c, part = units[u]
                if part == 0 and c + 1 < CH:
                    dve.wait_ge(ld_x[c + 1], 16 * NP)
                    group_patches(nc.vector, c + 1, 0).then_inc(x_grouped_dve, 1)
                dve.wait_ge(unit_hi, u + 1)
                if part == "w":
                    hi, lo = [v[:, 2 * c:2 * c + 2].rearrange("p k n -> p (k n)") for v in (tokWT_hi, tokWT_lo)]
                    src = unit_bank(u)[:, :]
                else:
                    src = unit_bank(u)[:, :].rearrange("p (j i b) -> p j i b", j=NP, i=NP)
                    hi, lo = [v[:, 2 * c + part].rearrange("p (i j b) -> p j i b", i=NP, j=NP) for v in (xT_hi, xT_lo)]
                lo_part(lo, src, hi).then_inc(unit_lo, 1)

            def moments(rows, t):
                after(step(nc.vector.bn_stats(stats[:, t], rows)))
                return step(nc.vector.bn_aggr(mv[:, t], stats[:, t]))

            for t in range(NT):
                dve.wait_ge(h_ready, t + 1)
                n = moments(h[:, t], t)
            after(n)
            nc.vector.tensor_scalar(var[:, :], mv[:, :, 1], EPS, None, ALU.add).then_inc(var1, 1)
            dve.wait_ge(rstd1, 1)
            for t in range(NT):
                nc.vector.tensor_scalar(xhat[:, t], h[:, t], mv[:, t, 0:1], rstd[:, t:t + 1],
                                        ALU.subtract, ALU.mult).then_inc(xhat_ready, 1)
            for p in range(2):
                dve.wait_ge(xhat_T, p + 1)
                dve.wait_ge(ld_ln, 64)
                n = step(nc.vector.tensor_scalar(xn[:, 1, pair_cols(p)], bank[7][:, pair_cols(p)],
                                                 ln1w[:, 1:2], ln1b[:, 1:2], ALU.mult, ALU.add))
                dve.wait_ge(xn_c0, p + 1)
                after(n)
                after(step(nc.vector.tensor_copy(xn_hi[:, :, pair_cols(p)], xn[:, :, pair_cols(p)])))
                lo_part(xn_lo[:, :, pair_cols(p)], xn[:, :, pair_cols(p)], xn_hi[:, :, pair_cols(p)]).then_inc(xn_split, 1)

            dve.wait_ge(ld_fw, 16)
            after(step(nc.vector.tensor_reduce(wsc[:, 0], fw_in[:], AX.X, ALU.add, apply_absolute_value=True)))
            after(step(nc.vector.tensor_scalar(wsc[:, 0], wsc[:, 0], 1.0 / D, 1e-5, ALU.mult, ALU.max)))
            step(nc.vector.tensor_scalar(wsc[:, 1], wsc[:, 0], 0.5, None, ALU.mult))
            after(step(nc.vector.tensor_scalar(wsc[:, 2], wsc[:, 0], -0.5, None, ALU.mult)))
            for a in range(C):
                step(nc.vector.tensor_scalar(wpos[:, a], fw_in[:, a], wsc[:, 1, a:a + 1], wsc[:, 0, a:a + 1],
                                             ALU.is_gt, ALU.mult))
                n = step(nc.vector.tensor_scalar(wneg[:, a], fw_in[:, a], wsc[:, 2, a:a + 1], wsc[:, 0, a:a + 1],
                                                 ALU.is_lt, ALU.mult))
            after(n)
            nc.vector.tensor_tensor(tern[:], wpos[:], wneg[:], ALU.subtract).then_inc(tern_ready, 1)

            dve.wait_ge(krep_ready, 1)
            k_by_image = krep[:, :].rearrange("p (s b) -> p b s", b=B)
            for n in range(B // NW):
                for b in range(n * NW, (n + 1) * NW, NW):
                    src = k_by_image[:, b:b + NW].unsqueeze(2).to_broadcast([P, NW, HPC, T])
                    msk = mask_k.unsqueeze(1).unsqueeze(3).to_broadcast([P, NW, HPC, T])
                    nc.vector.tensor_tensor(kblk[:, b:b + NW], src, msk, ALU.mult).then_inc(kblk_ready, 1)
            dve.wait_ge(q1_done, 1)
            nc.vector.tensor_copy(qT[:, :, 1, :].rearrange("p b t -> p t b"),
                                  bank[7][:, :].rearrange("p (t b) -> p t b", b=B)).then_inc(q1_ready, 1)

            dve.wait_ge(ld_gates, 48)
            for t in range(NT):
                if t:
                    after(n)
                n = step(nc.vector.scalar_tensor_tensor(junk, h[:, t], 1.0, wg_row[:, :], ALU.mult, ALU.mult,
                                                        accum_out=sc_rows[:, t:t + 1]))
            after(n)
            after(step(nc.vector.tensor_scalar(sc_rows[:, :], sc_rows[:, :], bg_col[:, 0:1], None, ALU.add)))
            for k in range(TPT):
                n = step(nc.vector.tensor_copy(sc[:, :].rearrange("b (t k) -> b t k", k=TPT)[:, :, k],
                                               sc_rows[B * k:B * k + B, :]))
            after(n)
            other = sc[:, :].unsqueeze(1).to_broadcast([B, T, T])
            own = sc[:, :].unsqueeze(2).to_broadcast([B, T, T])
            step(nc.vector.tensor_tensor(gt[:], other, own, ALU.is_gt))
            after(step(nc.vector.tensor_tensor(eq[:], other, own, ALU.is_equal)))
            after(step(nc.vector.tensor_tensor(eq[:], eq[:], earlier[0:B].rearrange("b (t s) -> b t s", s=T), ALU.mult)))
            after(step(nc.vector.tensor_tensor(gt[:], gt[:], eq[:], ALU.add)))
            after(step(nc.vector.tensor_reduce(rank[:, :], gt[:], AX.X, ALU.add)))
            after(step(nc.vector.tensor_scalar(m_bt[:, :], rank[:, :], TOPK - 0.5, None, ALU.is_lt)))
            for k in range(TPT):
                step(nc.vector.tensor_copy(m_rows[B * k:B * k + B, :],
                                           m_bt[:, :].rearrange("b (t k) -> b t k", k=TPT)[:, :, k]))
            step(nc.vector.tensor_scalar(gate[:, 0:1], sg_col[:, :], -1.0, None, ALU.mult))
            after(step(nc.vector.tensor_scalar(gate[:, 1:2], sg_col[:, :], 1.0, None, ALU.add)))
            nc.vector.tensor_scalar(c_rows[:, :], m_rows[:, :], gate[:, 0:1], gate[:, 1:2],
                                    ALU.mult, ALU.add).then_inc(mask_ready, 1)

            def split_states(t):
                dve.wait_ge(state_m0, TPT * (t + 1))
                dve.wait_ge(state_m1, TPT * (t + 1))
                after(step(nc.vector.tensor_copy(hid_hi[:, :, tile_cols(t)], hid[:, :, tile_cols(t)])))
                lo_part(hid_lo[:, :, tile_cols(t)], hid[:, :, tile_cols(t)], hid_hi[:, :, tile_cols(t)]).then_inc(hid_split, 1)

            split_states(0)
            dve.wait_ge(vm_T, 1)
            dve.wait_ge(tern_ready, 1)
            nc.vector.tensor_tensor(v_masked, bank[5][:, 0:NT * HD].rearrange("p (t d) -> p t d", t=NT)
                                    .unsqueeze(1).to_broadcast([P, HPC, NT, HD]),
                                    mask_v.unsqueeze(2).unsqueeze(3).to_broadcast([P, HPC, NT, HD]),
                                    ALU.mult).then_inc(vm_ready, 1)
            dve.wait_ge(vsd_ready, 1)
            dve.wait_ge(wb_split, 1)
            dve.wait_ge(wq_split, 1)
            dve.wait_ge(wco_split, 2)
            for b in range(0, B // 2, NW):
                src = v_sd[:, b:b + NW].unsqueeze(2).to_broadcast([P, NW, HPC, HD])
                msk = mask_v.unsqueeze(1).unsqueeze(3).to_broadcast([P, NW, HPC, HD])
                nc.vector.tensor_tensor(vblk[0][:, b:b + NW], src, msk, ALU.mult).then_inc(vblk_dve, 1)
            dve.wait_ge(ternT_hi_s, 1)
            lo_part(ternT_lo[:].rearrange("p k n -> p (k n)"), bank[5][:, :],
                    ternT_hi[:].rearrange("p k n -> p (k n)")).then_inc(ternT_split, 1)
            split_states(1)

            def shift(n):
                dve.wait_ge(s_done, n + 1)
                s = bank[4 + n][:, :].rearrange("p (h s) -> p h s", s=T)
                after(step(nc.vector.tensor_reduce(smax[:, n], s, AX.X, ALU.max)))
                nc.vector.tensor_tensor(prob[:, n], s, smax[:, n].unsqueeze(2).to_broadcast([P, 32, T]),
                                        ALU.subtract).then_inc(s_shifted, 1)

            def normalise(n):
                dve.wait_ge(exp_done, n + 1)
                after(step(nc.vector.tensor_reduce(ssum[:, n], prob[:, n], AX.X, ALU.add)))
                after(step(nc.vector.reciprocal(srec[:, n], ssum[:, n])))
                nc.vector.tensor_tensor(prob[:, n], prob[:, n], srec[:, n].unsqueeze(2).to_broadcast([P, 32, T]),
                                        ALU.mult).then_inc(prob_ready, 1)

            shift(0)
            shift(1)
            normalise(0)
            normalise(1)
            split_states(2)

            def heads_lo(n):
                dve.wait_ge(o_hi, n + 1)
                for c in range(C):
                    ins = lo_part(oT_lo[:, c].rearrange("p (t b) -> p b t", b=B)[:, 16 * n:16 * n + 16],
                                  bank[6 + n][:, :].rearrange("p (b c t) -> p b c t", c=C, t=T)[:, :, c],
                                  oT_hi[:, c].rearrange("p (t b) -> p b t", b=B)[:, 16 * n:16 * n + 16])
                ins.then_inc(o_lo, 1)

            def residual(t):
                dve.wait_ge(skip_ready, t + 1)
                dve.wait_ge(hc_ready, t + 1)
                return step(nc.vector.scalar_tensor_tensor(skip[:, t], skip[:, t], m_rows[:, t:t + 1], hc[:, t],
                                                           ALU.mult, ALU.add))

            for t in range(NT):
                n_residual = residual(t)
            heads_lo(0)
            split_states(3)
            heads_lo(1)
            after(n_residual)

            def add_mixed(p):
                dve.wait_ge(y_done, 2 * p + 2)
                for t in (2 * p, 2 * p + 1):
                    nc.vector.scalar_tensor_tensor(x2[:, t], bank[4 + p][:, (t % 2) * D:(t % 2 + 1) * D],
                                                   m_rows[:, t:t + 1], skip[:, t], ALU.mult, ALU.add).then_inc(x2_ready, 1)
                for t in (2 * p, 2 * p + 1):
                    dve.wait_ge(x2_ready, t + 1)
                    n = moments(x2[:, t], t)
                after(n)
                nc.vector.tensor_scalar(var[:, 2 * p:2 * p + 2], mv[:, 2 * p:2 * p + 2, 1], EPS, None,
                                        ALU.add).then_inc(var2, 1)

            def norm2(p):
                dve.wait_ge(rstd2, p + 1)
                for t in (2 * p, 2 * p + 1):
                    nc.vector.tensor_scalar(x2hat[:, t], x2[:, t], mv[:, t, 0:1], rstd[:, t:t + 1],
                                            ALU.subtract, ALU.mult).then_inc(x2hat_ready, 1)

            def split_norm2(p):
                dve.wait_ge(xn2_chunk, C * (p + 1))
                after(step(nc.vector.tensor_copy(xn2_hi[:, p], xn2[:, p])))
                lo_part(xn2_lo[:, p], xn2[:, p], xn2_hi[:, p]).then_inc(xn2_split, 1)

            def split_gelu(p, j):
                dve.wait_ge(gelu_done, p * FJ + j + 1)
                if p == 1:
                    dve.wait_ge(down_done, 2)
                after(step(nc.vector.tensor_copy(g_hi[:, j], g[:, j])))
                lo_part(g_lo[:, j], g[:, j], g_hi[:, j]).then_inc(g_split, 1)

            def tail_norm_a(t):
                dve.wait_ge(down_done, t + 1)
                dve.wait_ge(base2_ready, t + 1)
                after(step(nc.vector.tensor_tensor(s_rows[:, t], down_bank[t][:, 0:D], base2[:, t], ALU.add)))
                after(moments(s_rows[:, t], t))
                nc.vector.tensor_scalar(var[:, t:t + 1], mv[:, t, 1:2], EPS, None, ALU.add).then_inc(var3, 1)

            def tail_norm_b(t):
                dve.wait_ge(rstd3, t + 1)
                nc.vector.tensor_scalar(h2[:, t], s_rows[:, t], mv[:, t, 0:1], rstd[:, t:t + 1],
                                        ALU.subtract, ALU.mult).then_inc(h2_ready, 1)

            def tail_lo(t):
                dve.wait_ge(h2T_hi_s, t + 1)
                lo_part(h2T_lo[:, t].rearrange("p k n -> p (k n)"), down_bank[t][:, 0:D],
                        h2T_hi[:, t].rearrange("p k n -> p (k n)")).then_inc(h2T_lo_s, 1)

            def quantise(t):
                dve.wait_ge(had_done, t + 1)
                after(step(nc.vector.tensor_reduce(amax[:, t:t + 1], down_bank[t][:, 0:D], AX.X, ALU.max,
                                                   apply_absolute_value=True)))
                after(step(nc.vector.tensor_scalar(qscale[:, t:t + 1], amax[:, t:t + 1], 1e-5, 1.0 / QMAX,
                                                   ALU.max, ALU.mult)))
                after(step(nc.vector.reciprocal(qinv[:, t:t + 1], qscale[:, t:t + 1])))
                after(step(nc.vector.tensor_scalar(quant[:, t], down_bank[t][:, 0:D], qinv[:, t:t + 1], QMAX,
                                                   ALU.mult, ALU.min)))
                nc.vector.tensor_scalar(quant[:, t], quant[:, t], QMIN, ROUND, ALU.max, ALU.add).then_inc(quant_ready, 1)

            def last_norm_a(t):
                dve.wait_ge(fin_done, t + 1)
                after(step(nc.vector.scalar_tensor_tensor(f_rows[:, t], down_bank[t][:, 0:D], qscale[:, t:t + 1],
                                                          h2[:, t], ALU.mult, ALU.add)))
                after(moments(f_rows[:, t], t))
                nc.vector.tensor_scalar(var[:, t:t + 1], mv[:, t, 1:2], EPS, None, ALU.add).then_inc(var4, 1)

            def last_norm_b(t):
                dve.wait_ge(rstd4, t + 1)
                nc.vector.tensor_scalar(o_rows[:, t], f_rows[:, t], mv[:, t, 0:1], rstd[:, t:t + 1],
                                        ALU.subtract, ALU.mult).then_inc(out_ready, 1)

            add_mixed(0)
            norm2(0)
            split_norm2(0)
            add_mixed(1)
            norm2(1)
            for j in range(FJ):
                split_gelu(0, j)
            split_norm2(1)
            tail_norm_a(0)
            tail_norm_b(0)
            split_gelu(1, 0)
            tail_norm_a(1)
            tail_norm_b(1)
            split_gelu(1, 1)
            tail_lo(0)
            split_gelu(1, 2)
            tail_lo(1)
            split_gelu(1, 3)
            quantise(0)
            split_gelu(1, 4)
            quantise(1)
            split_gelu(1, 5)
            split_gelu(1, 6)
            split_gelu(1, 7)
            last_norm_a(0)
            last_norm_b(0)
            last_norm_a(1)
            last_norm_b(1)
            tail_norm_a(2)
            tail_norm_b(2)
            tail_lo(2)
            tail_norm_a(3)
            tail_norm_b(3)
            quantise(2)
            tail_lo(3)
            quantise(3)
            last_norm_a(2)
            last_norm_b(2)
            last_norm_a(3)
            last_norm_b(3)

        @block.gpsimd
        def _(pool):
            count = [0]

            def step(ins):
                ins.then_inc(pool_done, 1)
                count[0] += 1
                return count[0]

            def after(n):
                pool.wait_ge(pool_done, n)

            def split(full, hi, lo, done):
                after(step(nc.gpsimd.tensor_copy(hi, full)))
                nc.gpsimd.tensor_tensor(lo, full, hi.bitcast(F32), ALU.subtract).then_inc(done, 1)

            def inverse_root(t, n, ready, value, done):
                pool.wait_ge(ready, value)
                nc.gpsimd.tensor_tensor(rstd[:, t:t + n], var[:, t:t + n], neg_half[:, 0:n], ALU.pow).then_inc(done, 1)

            n_half = step(nc.gpsimd.memset(neg_half[:, :], -0.5))
            for c in range(CH):
                pool.wait_ge(ld_x[c], 16 * NP)
                group_patches(nc.gpsimd, c, 1).then_inc(x_grouped_pool, 1)
            pool.wait_ge(ld_cst, 16)
            nc.gpsimd.tensor_copy(had[:].rearrange("p k n -> p (k n)"), hadamard).then_inc(had_ready, 1)
            pool.wait_ge(ld_wb, 16)
            split(wb_in[:], wb_hi[:], wb_lo[:], wb_split)
            pool.wait_ge(ld_wkv, 32)
            for w, hi, lo in ((wk_in, wk_hi, wk_lo), (wv_in, wv_hi, wv_lo)):
                rep = w[:].unsqueeze(2).to_broadcast([P, C, HPC, HD])
                after(step(nc.gpsimd.tensor_copy(hi[:].rearrange("p k (h d) -> p k h d", h=HPC), rep)))
                ins = nc.gpsimd.tensor_tensor(lo[:].rearrange("p k (h d) -> p k h d", h=HPC), rep,
                                              hi[:].bitcast(F32).rearrange("p k (h d) -> p k h d", h=HPC), ALU.subtract)
            ins.then_inc(wkv_split, 1)
            after(n_half)
            inverse_root(0, NT, var1, 1, rstd1)
            pool.wait_ge(ld_wq, 16)
            split(wq_in[:], wq_hi[:], wq_lo[:], wq_split)
            pool.wait_ge(ld_rows, 64)
            pool.wait_ge(xhat_T, 2)
            step(nc.gpsimd.tensor_tensor(dw, dp_row[:, :], l1w_row[:, :], ALU.mult))
            after(step(nc.gpsimd.tensor_tensor(db, dp_row[:, :], l1b_row[:, :], ALU.mult)))
            pool.wait_ge(xhat_ready, NT)
            for t in range(NT):
                after(step(nc.gpsimd.tensor_tensor(skip[:, t], xhat[:, t], dw, ALU.mult)))
                nc.gpsimd.tensor_tensor(skip[:, t], skip[:, t], db, ALU.add).then_inc(skip_ready, 1)
            pool.wait_ge(ld_wc, 16)
            split(wc_in[:], wc_hi[:], wc_lo[:], wco_split)
            pool.wait_ge(ld_wo, 16)
            split(wo_in[:], wo_hi[:], wo_lo[:], wco_split)
            pool.wait_ge(vsd_ready, 1)
            pool.wait_ge(st_done, 1)
            for b in range(B // 2, B, NW):
                src = v_sd[:, b:b + NW].unsqueeze(2).to_broadcast([P, NW, HPC, HD])
                msk = mask_v.unsqueeze(1).unsqueeze(3).to_broadcast([P, NW, HPC, HD])
                nc.gpsimd.tensor_tensor(vblk[1][:, b - B // 2:b - B // 2 + NW], src, msk, ALU.mult).then_inc(vblk_pool, 1)
            pool.wait_ge(mask_ready, 1)
            for t in range(NT):
                nc.gpsimd.tensor_scalar(hc[:, t], h[:, t], c_rows[:, t:t + 1], None, ALU.mult).then_inc(hc_ready, 1)
            pool.wait_ge(ld_w1, 32)
            pool.wait_ge(w1_hi_ready, 1)
            nc.gpsimd.tensor_tensor(w1_lo[:], w1_in[:], w1_hi[:].bitcast(F32), ALU.subtract).then_inc(w1_lo_ready, 1)
            inverse_root(0, 2, var2, 1, rstd2)
            inverse_root(2, 2, var2, 2, rstd2)
            pool.wait_ge(w2_hi_ready, 1)
            nc.gpsimd.tensor_tensor(w2_lo[:], w2_in[:], w2_hi[:].bitcast(F32), ALU.subtract).then_inc(w2_lo_ready, 1)
            for t in range(NT):
                n = step(nc.gpsimd.tensor_tensor(hb2[:, t], h[:, t], b2_row[:, :], ALU.add))
            after(n)
            for t in range(NT):
                pool.wait_ge(x2_ready, t + 1)
                nc.gpsimd.tensor_tensor(base2[:, t], x2[:, t], hb2[:, t], ALU.add).then_inc(base2_ready, 1)
            inverse_root(0, 1, var3, 1, rstd3)
            inverse_root(1, 1, var3, 2, rstd3)
            inverse_root(0, 1, var4, 1, rstd4)
            inverse_root(1, 1, var4, 2, rstd4)
            inverse_root(2, 1, var3, 3, rstd3)
            inverse_root(3, 1, var3, 4, rstd3)
            inverse_root(2, 1, var4, 3, rstd4)
            inverse_root(3, 1, var4, 4, rstd4)


_INS = ['x', 'L0_tok_W', 'L0_tok_b', 'L0_tok_pos_emb', 'L0_attn_Wg', 'L0_attn_bg', 'L0_attn_Wq', 'L0_attn_Wk',
        'L0_attn_Wv', 'L0_attn_Wo', 'L0_attn_A', 'L0_attn_Wb', 'L0_attn_Wc', 'L0_attn_Dp', 'L0_attn_W1',
        'L0_attn_b1', 'L0_attn_W2', 'L0_attn_b2', 'L0_attn_ln1_w', 'L0_attn_ln1_b', 'L0_attn_ln2_w',
        'L0_attn_ln2_b', 'L0_attn_skip_gate', 'L0_ffn_weight']


def kernel(**inputs):
    import numpy as _np
    import concourse.bacc as _bacc
    from concourse import mybir as _mybir
    from concourse.bass_utils import run_bass_kernel_spmd as _run

    nc = _bacc.Bacc("TRN2", target_bir_lowering=False, num_devices=1)
    arrays, args = {}, []
    consts, row_sel = shape_constants()
    given = [(name, inputs[name]) for name in _INS] + [("consts", consts), ("row_sel", row_sel)]
    for name, value in given:
        a = _np.ascontiguousarray(value)
        arrays[f"in_{name}_dram"] = a
        args.append(nc.dram_tensor(f"in_{name}_dram", a.shape, _mybir.dt.from_np(a.dtype), kind="ExternalInput").ap())
    args.append(nc.dram_tensor("out_0_dram", (B, T, D), F32, kind="ExternalOutput").ap())
    vit_block(nc, *args)
    r = _run(nc, [arrays], core_ids=[0])
    return r.results[0]["out_0_dram"]
```

```python
from contextlib import ExitStack

import numpy as np

import concourse.bass as bass
from concourse import mybir

F32 = mybir.dt.float32
F32R = mybir.dt.float32r
ALU = mybir.AluOpType
ACT = mybir.ActivationFunctionType
AX = mybir.AxisListType

P = 128
B = 32
NP = 4
T = NP * NP
PS = 16
CH = 3
D = 256
C = D // P
H = 16
HD = D // H
HPC = P // HD
R = B * T
NT = R // P
TPT = T // NT
KT = CH * PS * PS // P
F = 4 * D
FJ = F // P
TOPK = T // 4
EPS = 1e-5
ROUND = 1.5 * 2.0 ** 23
QMAX, QMIN = 7.0, -8.0
NW = 8


def shape_constants():
    h = np.array([[1.0]])
    while h.shape[0] < D:
        h = np.block([[h, h], [h, -h]])
    h = (h / np.sqrt(D)).astype(np.float32).reshape(C, P, D).transpose(1, 0, 2).reshape(P, C * D)
    head = (np.arange(P)[:, None] // HD == np.arange(HPC)[None, :]).astype(np.float32)
    earlier = (np.arange(T)[None, :] < np.arange(T)[:, None]).astype(np.float32).reshape(1, T * T)
    spread = (np.arange(P)[:, None] % T == np.arange(P)[None, :] % T).astype(np.float32)
    consts = np.concatenate([np.eye(P, dtype=np.float32), head / np.sqrt(HD), head, spread,
                             np.repeat(earlier, P, 0), h], axis=1).astype(np.float32)
    token = np.arange(R) // B
    rows = np.concatenate([(token[None, :] == np.arange(T)[:, None]), np.ones((1, R))], 0).astype(np.float32)
    return np.ascontiguousarray(consts), np.ascontiguousarray(rows)


def vit_block(nc, x, tok_W, tok_b, tok_pos, Wg, bg, Wq, Wk, Wv, Wo, A, Wb, Wc, Dp, W1, b1, W2, b2,
              ln1_w, ln1_b, ln2_w, ln2_b, skip_gate, ffn_w, consts, row_sel, out):
    with ExitStack() as ctx:
        def sb(name, shape, dt=F32):
            return ctx.enter_context(nc.sbuf_tensor(name, shape, dt))

        def sem(name):
            return ctx.enter_context(nc.semaphore(name))

        cst = sb("cst", [P, 2 * P + 2 * HPC + T * T + C * D])
        o = P
        ident = cst[:, 0:P]
        mask_k = cst[:, o:o + HPC]
        mask_v = cst[:, o + HPC:o + 2 * HPC]
        o += 2 * HPC
        spread = cst[:, o:o + P]
        o += P
        earlier = cst[:, o:o + T * T]
        hadamard = cst[:, o + T * T:]
        a_in = sb("a_in", [P, C, D])
        AT = sb("AT", [P, C, D])

        def carve(tensor, *shapes):
            at, views = 0, []
            for shape in shapes:
                size = int(np.prod(shape))
                names = " ".join("abcd"[:len(shape)])
                views.append(tensor[:, at:at + size].rearrange(f"p ({names}) -> p {names}",
                                                               **dict(zip("abcd", shape))))
                at += size
            return views

        early = sb("early", [P, CH * (PS * NP * PS + C * PS * PS)])
        x_in, w_in = carve(early, (CH, PS * NP * PS), (CH, C, PS * PS))
        kblk, dw, db = carve(early, (B, HPC, T), (D,), (D,))
        early_r = sb("early_r", [P, 2 * KT * (R + D)], F32R)
        xT_hi, xT_lo, tokWT_hi, tokWT_lo = carve(early_r, (KT, R), (KT, R), (KT, D), (KT, D))
        g_hi, g_lo, hid_hi, hid_lo, ternT_hi, ternT_lo, quantT, g2_lo_b = carve(
            early_r, (FJ, D), (FJ, D), (C, R), (C, R), (C, D), (C, D), (NT, C, P), (FJ // 2, D))
        proj_in = sb("proj_in", [P, 4 * C * D])
        wb_in, wq_in, wc_in, wo_in = carve(proj_in, *[(C, D)] * 4)
        vblk = [carve(t, (B // 2, HPC, HD))[0] for t in (proj_in, early)]

        def halves(name, chunks, cols):
            return sb(name + "_hi", [P, chunks, cols], F32R), sb(name + "_lo", [P, chunks, cols], F32R)

        proj_r = sb("proj_r", [P, 4 * C * D + 4 * C * P], F32R)
        wb_hi, wb_lo, wq_hi, wq_lo, wk_hi, wk_lo, wv_hi, wv_lo = carve(proj_r, *[(C, D)] * 4, *[(C, P)] * 4)
        g2_hi, g2_lo_a = carve(proj_r, (FJ, D), (FJ // 2, D))
        wc_hi, wc_lo = halves("wc", C, D)
        wo_hi, wo_lo = halves("wo", C, D)
        w1_hi, w1_lo = halves("w1", C, F)
        w2_hi, w2_lo = halves("w2", FJ, D)
        ff_space = sb("ff_space", [P, C * F + FJ * D])
        x_by_patch, = carve(ff_space, (CH, 2, NP, P))
        w1_in, w2_in = carve(ff_space, (C, F), (FJ, D))
        g, h2 = carve(ff_space, (FJ, D), (NT, D))

        def hidden(p, part, j):
            if p == 0:
                return (g_hi, g_lo)[part][:, j]
            if part == 0:
                return g2_hi[:, j]
            return g2_lo_a[:, j] if j < FJ // 2 else g2_lo_b[:, j - FJ // 2]
        wk_in = sb("wk_in", [P, C, HD])
        wv_in = sb("wv_in", [P, C, HD])
        had = sb("had", [P, C, D], F32R)
        ln1w = sb("ln1w", [P, C])
        ln1b = sb("ln1b", [P, C])
        ln2w = sb("ln2w", [P, C])
        ln2b = sb("ln2b", [P, C])
        b1c = sb("b1c", [P, FJ])
        wg_row = sb("wg_row", [P, D])
        b2_row = sb("b2_row", [P, D])
        dp_row = sb("dp_row", [P, D])
        l1w_row = sb("l1w_row", [P, D])
        l1b_row = sb("l1b_row", [P, D])
        bg_col = sb("bg_col", [P, 1])
        sg_col = sb("sg_col", [P, 1])
        fw_in = sb("fw_in", [P, C, D])
        neg_half = sb("neg_half", [P, NT])

        h = sb("h", [P, NT, D])
        hb2_space = sb("hb2_space", [P, NT * D])
        (hb2,), (gt, eq, junk) = carve(hb2_space, (NT, D)), carve(hb2_space, (T, T), (T, T), (D,))
        gt, eq = gt[0:B], eq[0:B]
        sel, posb = [v[0:T + 1] for v in carve(hb2_space, (R,), (D,))]
        _, v_masked = carve(hb2_space, (2 * D,), (HPC, NT, HD))
        base2 = hb2
        xhat = sb("xhat", [P, NT, D])
        skip = xhat
        x2 = sb("x2", [P, NT, D])
        hc = x2
        xn_space = sb("xn_space", [P, C * R])
        xn, = carve(xn_space, (C, R))
        krep = xn_space[:, 0:R]
        vT = xn_space[0:HD, R:2 * R]
        xn2, = carve(xn_space, (2, C, D))
        xn_hi_space = sb("xn_hi_space", [P, C * R], F32R)
        xn_lo_space = sb("xn_lo_space", [P, C * R], F32R)
        (xn_hi,), (xn_lo,) = carve(xn_hi_space, (C, R)), carve(xn_lo_space, (C, R))
        (xn2_hi,), (xn2_lo,) = carve(xn_hi_space, (2, C, D)), carve(xn_lo_space, (2, C, D))
        q_space = sb("q_space", [P, B * C * T])
        (qT,), (x2hat,), (o_rows,) = carve(q_space, (B, C, T)), carve(q_space, (NT, D)), carve(q_space, (NT, D))
        pT = sb("pT", [P, B * C * T])
        f_rows, = carve(pT, (NT, D))
        tern, = carve(pT, (C, D))
        prob_space = sb("prob_space", [P, B * C * T])
        (prob,), (head_rows,), (quant,) = [carve(prob_space, shape) for shape in ((2, 32, T), (2, 512), (NT, D))]
        wpos, wneg = carve(prob_space, (C, D), (C, D))
        o_hi_space = sb("o_hi_space", [P, C * R], F32R)
        o_lo_space = sb("o_lo_space", [P, C * R], F32R)
        (oT_hi,), (oT_lo,) = carve(o_hi_space, (C, R)), carve(o_lo_space, (C, R))
        sel_hi, (posb_hi, posb_lo) = o_hi_space[0:T + 1, 0:R], [v[0:T + 1] for v in carve(o_lo_space, (D,), (D,))]
        (h2T_hi,), (h2T_lo,) = carve(o_hi_space, (NT, C, P)), carve(o_lo_space, (NT, C, P))
        stats = sb("stats", [P, NT, 6])
        mv = sb("mv", [P, NT, 2])
        var = sb("var", [P, NT])
        rstd = sb("rstd", [P, NT])
        hid = sb("hid", [P, C, R])
        v_sd = sb("v_sd", [P, B, HD])
        smax = sb("smax", [P, 2, 32])
        ssum = sb("ssum", [P, 2, 32])
        srec = sb("srec", [P, 2, 32])
        sc_rows = sb("sc_rows", [P, NT])
        sc = sb("sc", [B, T])
        rank = sb("rank", [B, T])
        m_bt = sb("m_bt", [B, T])
        m_rows = sb("m_rows", [P, NT])
        c_rows = sb("c_rows", [P, NT])
        gate = sb("gate", [P, 2])
        amax = sb("amax", [P, NT])
        qscale = sb("qscale", [P, NT])
        qinv = sb("qinv", [P, NT])
        wsc = sb("wsc", [P, 3, C])
        bank = [ctx.enter_context(nc.psum_tensor(f"bank{i}", [P, 512], F32)) for i in range(8)]

        def scan_bank(m, par):
            return bank[2 * m + par]

        ld_ident, ld_cst, ld_sel, ld_a = sem("ld_ident"), sem("ld_cst"), sem("ld_sel"), sem("ld_a")
        ld_x = [sem(f"ld_x{c}") for c in range(CH)]
        ld_w = [sem(f"ld_tok{c}") for c in range(CH)]
        ld_ln, ld_wb, ld_wkv, ld_wq = sem("ld_ln"), sem("ld_wb"), sem("ld_wkv"), sem("ld_wq")
        ld_wc, ld_wo, ld_rows, ld_gates, ld_fw = sem("ld_wc"), sem("ld_wo"), sem("ld_rows"), sem("ld_gates"), sem("ld_fw")
        ld_w1, ld_w2, stored = sem("ld_w1"), sem("ld_w2"), sem("stored")
        x_grouped_dve, x_grouped_pool = sem("x_grouped_dve"), sem("x_grouped_pool")
        vm_T, vm_ready = sem("vm_T"), sem("vm_ready")
        unit_T, unit_hi, unit_lo = sem("unit_T"), sem("unit_hi"), sem("unit_lo")
        a_T, a_ready = sem("a_T"), sem("a_ready")
        tok_done, h_ready, var1, rstd1 = sem("tok_done"), sem("h_ready"), sem("var1"), sem("rstd1")
        xhat_ready, xhat_T, xn_c0, xn_c1, xn_split = (
            sem("xhat_ready"), sem("xhat_T"), sem("xn_c0"), sem("xn_c1"), sem("xn_split"))
        wb_split, wkv_split, wq_split, wco_split = sem("wb_split"), sem("wkv_split"), sem("wq_split"), sem("wco_split")
        had_ready, w1_hi_ready, w1_lo_ready, w2_hi_ready, w2_lo_ready = (
            sem("had_ready"), sem("w1_hi_ready"), sem("w1_lo_ready"), sem("w2_hi_ready"), sem("w2_lo_ready"))
        wb_hi_ready, wkv_hi_ready, wq_hi_ready, wco_hi_ready, hid_hi_ready = (
            sem("wb_hi_ready"), sem("wkv_hi_ready"), sem("wq_hi_ready"), sem("wco_hi_ready"), sem("hid_hi_ready"))
        pre_done, step_m0, step_m1 = sem("pre_done"), sem("step_m0"), sem("step_m1")
        state_m0, state_m1, hid_split = sem("state_m0"), sem("state_m1"), sem("hid_split")
        k_done, krep_ready, kblk_ready = sem("k_done"), sem("krep_ready"), sem("kblk_ready")
        v_done, vT_ready, vsd_done, vsd_ready = sem("v_done"), sem("vT_ready"), sem("vsd_done"), sem("vsd_ready")
        vblk_act, vblk_dve, o_rows_done, o_rows_ready = sem("vblk_act"), sem("vblk_dve"), sem("o_rows_done"), sem("o_rows_ready")
        q0_done, q1_done, q0_ready, q1_ready = sem("q0_done"), sem("q1_done"), sem("q0_ready"), sem("q1_ready")
        s_done, s_shifted = sem("s_done"), sem("s_shifted")
        exp_done, pT_done, pT_ready = sem("exp_done"), sem("pT_done"), sem("pT_ready")
        o_done, o_hi, o_lo = sem("o_done"), sem("o_hi"), sem("o_lo")
        mask_ready, skip_ready, hc_ready, hb2_ready = sem("mask_ready"), sem("skip_ready"), sem("hc_ready"), sem("hb2_ready")
        y_done, x2_ready, base2_ready, var2, rstd2 = sem("y_done"), sem("x2_ready"), sem("base2_ready"), sem("var2"), sem("rstd2")
        x2hat_ready, x2hat_T, xn2_c0, xn2_c1, xn2_split = (
            sem("x2hat_ready"), sem("x2hat_T"), sem("xn2_c0"), sem("xn2_c1"), sem("xn2_split"))
        up_done, gelu_done, g_even, g_odd, down_done = (
            sem("up_done"), sem("gelu_done"), sem("g_even"), sem("g_odd"), sem("down_done"))
        var3, rstd3, h2_ready, h2_T, h2T_hi_s, h2T_lo_s = (
            sem("var3"), sem("rstd3"), sem("h2_ready"), sem("h2_T"), sem("h2T_hi_s"), sem("h2T_lo_s"))
        had_done, quant_ready, quant_T, quantT_ready = sem("had_done"), sem("quant_ready"), sem("quant_T"), sem("quantT_ready")
        wsc_ready, posb_hi_ready, posb_split = sem("wsc_ready"), sem("posb_hi_ready"), sem("posb_split")
        tern_ready, tern_T, ternT_hi_s, ternT_split = sem("tern_ready"), sem("tern_T"), sem("ternT_hi_s"), sem("ternT_split")
        fin_done, var4, rstd4, out_ready = sem("fin_done"), sem("var4"), sem("rstd4"), sem("out_ready")
        dve_done = sem("dve_done")
        pool_done = sem("pool_done")

        block = ctx.enter_context(nc.Block())

        units = [(c, part) for c in range(CH) for part in ("w", 0, 1)]

        def unit_bank(u):
            return bank[4 + u % 4]

        def pair_cols(p):
            return slice(p * 2 * P, (p + 1) * 2 * P)

        def tile_cols(t):
            return slice(t * P, (t + 1) * P)

        down_bank = [bank[7], bank[4], bank[5], bank[6]]

        def norm1_bank(p, c):
            return bank[(6, 4)[p] + c]

        def norm2_bank(p, c):
            return bank[6] if c == 0 else (bank[7], bank[5])[p]

        def group_patches(engine, c, part):
            half = PS // 2
            src = x_in[:, c].rearrange("p (r j q) -> p j r q", r=PS, j=NP)[:, :, part * half:(part + 1) * half]
            dst = x_by_patch[:, c, part].rearrange("p j (r q) -> p j r q", r=half)
            return engine.tensor_copy(dst, src)

        @block.sync
        def _(sp):
            for c in range(CH):
                sp.dma_start(x_in[:, c], x.rearrange("b c (i r) w -> c b i (r w)", i=NP)[c]).then_inc(ld_x[c], 16)
                if c == 0:
                    sp.dma_start(cst[:, 0:P], consts[:, 0:P]).then_inc(ld_ident, 16)
                sp.dma_start(w_in[:, c], tok_W.rearrange("(a p) (c f) -> p c a f", p=P, c=CH)[:, c]).then_inc(ld_w[c], 16)
            sp.dma_start(fw_in[:], ffn_w.rearrange("(a p) n -> p a n", p=P)).then_inc(ld_fw, 16)
            sp.dma_start(a_in[:], A.rearrange("(a p) n -> p a n", p=P)).then_inc(ld_a, 16)
            sp.dma_start(wb_in[:], Wb.rearrange("(a p) n -> p a n", p=P)).then_inc(ld_wb, 16)
            for dst, src in ((ln1w, ln1_w), (ln1b, ln1_b), (ln2w, ln2_w), (ln2b, ln2_b)):
                sp.dma_start(dst[:], src.rearrange("(a p) -> p a", p=P), allow_slow_non_contiguous=True).then_inc(ld_ln, 16)
            sp.dma_start(wk_in[:], Wk.rearrange("(a p) n -> p a n", p=P)).then_inc(ld_wkv, 16)
            sp.dma_start(wv_in[:], Wv.rearrange("(a p) n -> p a n", p=P)).then_inc(ld_wkv, 16)
            sp.dma_start(wq_in[:], Wq.rearrange("(a p) n -> p a n", p=P)).then_inc(ld_wq, 16)
            sp.dma_start(cst[:, P:], consts[:, P:]).then_inc(ld_cst, 16)
            sp.dma_start(bg_col[:], bg.partition_broadcast(P)).then_inc(ld_gates, 16)
            sp.dma_start(sg_col[:], skip_gate.partition_broadcast(P)).then_inc(ld_gates, 16)
            sp.dma_start(wg_row[:], Wg.rearrange("d a -> (d a)").partition_broadcast(P)).then_inc(ld_gates, 16)
            for dst, src in ((dp_row, Dp), (l1w_row, ln1_w), (l1b_row, ln1_b), (b2_row, b2)):
                sp.dma_start(dst[:], src.partition_broadcast(P)).then_inc(ld_rows, 16)
            sp.dma_start(wc_in[:], Wc.rearrange("(a p) n -> p a n", p=P)).then_inc(ld_wc, 16)
            sp.dma_start(wo_in[:], Wo.rearrange("(a p) n -> p a n", p=P)).then_inc(ld_wo, 16)
            sp.wait_ge(unit_T, len(units))
            sp.dma_start(w1_in[:], W1.rearrange("(a p) n -> p a n", p=P)).then_inc(ld_w1, 16)
            sp.dma_start(b1c[:], b1.rearrange("(a p) -> p a", p=P), allow_slow_non_contiguous=True).then_inc(ld_w1, 16)
            sp.dma_start(w2_in[:], W2.rearrange("(a p) n -> p a n", p=P)).then_inc(ld_w2, 16)
            for t in range(NT):
                sp.wait_ge(out_ready, t + 1)
                sp.dma_start(out[:, TPT * t:TPT * (t + 1), :].rearrange("b k d -> k b d"), o_rows[:, t]).then_inc(stored, 16)
            sp.wait_ge(stored, 16 * NT)

        @block.tensor
        def _(pe):
            def tr(dst, src, identity=None):
                return nc.tensor.transpose(dst, src, ident if identity is None else identity)

            def product(dst, lhs, rhs, first=True, last=True, check=False, parts=((0, 0), (1, 0), (0, 1))):
                passes = [(i, a, b) for a, b in parts for i in range(len(lhs))
                          if lhs[i][a] is not None and rhs[i][b] is not None]
                for n, (i, a, b) in enumerate(passes):
                    ins = nc.tensor.matmul(dst, lhs[i][a], rhs[i][b], start=first and n == 0,
                                           stop=last and n == len(passes) - 1, skip_group_check=check)
                return ins

            rhs_hi_part, rhs_lo_part = ((0, 0), (1, 0)), ((0, 1),)

            def unit_transposes(u):
                c, part = units[u]
                if u >= 4:
                    pe.wait_ge(unit_lo, u - 3)
                dst = unit_bank(u)
                if part == "w":
                    pe.wait_ge(ld_w[c], 16)
                    for hf in range(2):
                        for a in range(C):
                            k = hf * C + a
                            ins = tr(dst[:, k * P:(k + 1) * P], w_in[:, c, a, hf * P:(hf + 1) * P])
                else:
                    pe.wait_ge((x_grouped_dve, x_grouped_pool)[part], c + 1)
                    for j in range(NP):
                        ins = tr(dst[:, j * P:(j + 1) * P], x_by_patch[:, c, part, j])
                ins.then_inc(unit_T, 1)

            def patch_product(k, p):
                c, part = k // 2, k % 2
                pe.wait_ge(unit_lo, 3 * c + part + 2)
                for t in (2 * p, 2 * p + 1):
                    ins = product(bank[t][:, 0:D], [(xT_hi[:, k, tile_cols(t)], xT_lo[:, k, tile_cols(t)])],
                                  [(tokWT_hi[:, k], tokWT_lo[:, k])], first=(k == 0), last=(k == KT - 1))
                    if k == KT - 1:
                        ins.then_inc(tok_done, 1)

            pe.wait_ge(ld_ident, 16)
            for u in (0, 1, 2, 3):
                unit_transposes(u)
            patch_product(0, 0)
            unit_transposes(4)
            patch_product(1, 0)
            patch_product(0, 1)
            unit_transposes(5)
            pe.wait_ge(posb_split, 1)
            for t in range(NT):
                product(bank[t][:, 0:D], [(sel_hi[:, tile_cols(t)], None)], [(posb_hi, posb_lo)], first=False, last=False)
            patch_product(2, 0)
            unit_transposes(6)
            patch_product(3, 0)
            unit_transposes(7)
            unit_transposes(8)
            patch_product(1, 1)
            patch_product(4, 0)
            patch_product(5, 0)
            for k in range(2, KT):
                patch_product(k, 1)

            def norm1_transposes(p):
                if p == 0:
                    pe.wait_ge(unit_lo, 8)
                else:
                    pe.wait_ge(unit_lo, 9)
                    pe.wait_ge(a_ready, 1)
                for t in (2 * p, 2 * p + 1):
                    pe.wait_ge(xhat_ready, t + 1)
                    for c in range(C):
                        ins = tr(norm1_bank(p, c)[:, t % 2 * P:(t % 2 + 1) * P], xhat[:, t, c * P:(c + 1) * P])
                ins.then_inc(xhat_T, 1)

            norm1_transposes(0)
            pe.wait_ge(ld_a, 16)
            for k in range(C):
                for a in range(C):
                    ins = tr(bank[5][:, (2 * k + a) * P:(2 * k + a + 1) * P], a_in[:, a, k * P:(k + 1) * P])
            ins.then_inc(a_T, 1)

            def scan_inputs(p, par, parts, first, last):
                for m in range(C):
                    rhs = [tuple(v[:, k, pair_cols(p)].rearrange("q (u e b) -> q u e b", e=2, b=B)[:, :, par, :]
                                 for v in (xn_hi, xn_lo)) for k in range(C)]
                    lhs = [(wb_hi[:, k, m * P:(m + 1) * P], wb_lo[:, k, m * P:(m + 1) * P]) for k in range(C)]
                    ins = product(scan_bank(m, par)[:, p * P:(p + 1) * P], lhs, rhs, first=first, last=last, check=True,
                                  parts=parts)
                return ins

            pe.wait_ge(wb_split, 1)
            pe.wait_ge(xn_c0, 2)
            pe.wait_ge(xn_c1, 1)
            pe.wait_ge(h_ready, NT)
            for par in range(2):
                scan_inputs(0, par, rhs_hi_part, True, False)
            pe.wait_ge(xn_split, 1)
            for par in range(2):
                scan_inputs(0, par, rhs_lo_part, False, False).then_inc(pre_done, 1)
            norm1_transposes(1)

            def scan_step(t):
                dst = [scan_bank(m, t % 2)[:, t // 2 * B:(t // 2 + 1) * B] for m in range(C)]
                for k, state in ((0, state_m0), (1, state_m1)):
                    pe.wait_ge(state, t)
                    for m in range(C):
                        ins = nc.tensor.matmul(dst[m], AT[:, k, m * P:(m + 1) * P], hid[:, k, (t - 1) * B:t * B],
                                               start=False, stop=(k == 1), skip_group_check=True)
                        if k == 1:
                            ins.then_inc((step_m0, step_m1)[m], 1)

            xn_pairs = [(xn_hi[:, k], xn_lo[:, k]) for k in range(C)]

            def project(dst, lhs, done):
                product(dst[:, :], lhs, xn_pairs).then_inc(done, 1)

            def queries(m, p, done):
                ins = product(bank[6 + m][:, pair_cols(p)], [(wq_hi[:, k, m * P:(m + 1) * P], wq_lo[:, k, m * P:(m + 1) * P])
                                                             for k in range(C)],
                              [(hi[:, pair_cols(p)], lo[:, pair_cols(p)]) for hi, lo in xn_pairs])
                if p == 1:
                    ins.then_inc(done, 1)

            def scores(n):
                pe.wait_ge(q0_ready, 1)
                pe.wait_ge(q1_ready, 1)
                pe.wait_ge(kblk_ready, HPC)
                for b in range(16 * n, 16 * n + 16):
                    i, q = b % 16 // 4, b % 4
                    ins = nc.tensor.matmul(bank[6 + n][32 * q:32 * q + 32, i * P:(i + 1) * P],
                                           qT[:, b].rearrange("p c t -> p (c t)"),
                                           kblk[:, b].rearrange("p h s -> p (h s)"), start=True, stop=True)
                ins.then_inc(s_done, 1)

            scan_step(1)
            pe.wait_ge(wq_split, 1)
            queries(0, 0, q0_done)
            queries(1, 0, q1_done)
            pe.wait_ge(wkv_split, 1)
            pe.wait_ge(xn_split, 2)
            project(bank[4], [(wk_hi[:, k], wk_lo[:, k]) for k in range(C)], k_done)
            scan_step(2)
            project(bank[5], [(wv_hi[:, k], wv_lo[:, k]) for k in range(C)], v_done)
            scan_step(3)
            queries(0, 1, q0_done)
            pe.wait_ge(vT_ready, 1)
            for t in range(NT):
                ins = tr(bank[5][:, t * HD:(t + 1) * HD], vT[:, t * P:(t + 1) * P], ident[0:HD, 0:HD])
            ins.then_inc(vm_T, 1)
            scan_step(4)
            queries(1, 1, q1_done)
            pe.wait_ge(krep_ready, 1)
            pe.wait_ge(vm_ready, 1)
            nc.tensor.matmul(bank[4][:, :], spread, v_masked.rearrange("p e t d -> p (e t d)"),
                             start=True, stop=True).then_inc(vsd_done, 1)
            pe.wait_ge(tern_ready, 1)
            for k in range(C):
                for a in range(C):
                    ins = tr(bank[5][:, (2 * k + a) * P:(2 * k + a + 1) * P], tern[:, a, k * P:(k + 1) * P])
            ins.then_inc(tern_T, 1)
            scan_step(5)
            scores(0)
            scan_step(6)
            scores(1)
            scan_step(7)
            scan_inputs(1, 0, rhs_hi_part + rhs_lo_part, False, True)

            def probs_to_keys(n):
                pe.wait_ge(exp_done, n + 1)
                for i in range(4):
                    ins = tr(bank[6 + n][:, i * P:(i + 1) * P],
                             prob[:, n, i * 8:i * 8 + 8, :].rearrange("p h s -> p (h s)"))
                ins.then_inc(pT_done, 1)

            def attend(n):
                pe.wait_ge(pT_ready, n + 1)
                pe.wait_ge((vblk_act, vblk_dve)[n], HPC)
                for b in range(16 * n, 16 * n + 16):
                    i, q = b % 16 // 4, b % 4
                    ins = nc.tensor.matmul(bank[6 + n][32 * q:32 * q + 32, i * P:(i + 1) * P], pT[:, b * 32:(b + 1) * 32],
                                           vblk[n][:, b % 16].rearrange("p h d -> p (h d)"), start=True, stop=True)
                ins.then_inc(o_rows_done, 1)

            def heads_to_features(n):
                pe.wait_ge(o_rows_ready, n + 1)
                for i in range(4):
                    ins = tr(bank[6 + n][:, i * P:(i + 1) * P], head_rows[:, n, i * P:(i + 1) * P])
                ins.then_inc(o_done, 1)

            def mix_dst(t):
                return bank[4 + t // 2][:, (t % 2) * D:(t % 2 + 1) * D]

            def mix_states(t):
                if t < 2:
                    pe.wait_ge(vsd_ready, 1)
                else:
                    pe.wait_ge(ternT_split, 1)
                pe.wait_ge(hid_split, t + 1)
                pe.wait_ge(wco_split, 1)
                product(mix_dst(t), [(hid_hi[:, k, tile_cols(t)], hid_lo[:, k, tile_cols(t)]) for k in range(C)],
                        [(wc_hi[:, k], wc_lo[:, k]) for k in range(C)], first=(t % 2 == 0), last=False, check=True)

            def mix_heads(t):
                pe.wait_ge(wco_split, 2)
                pe.wait_ge(o_lo, 2)
                product(mix_dst(t), [(oT_hi[:, k, tile_cols(t)], oT_lo[:, k, tile_cols(t)]) for k in range(C)],
                        [(wo_hi[:, k], wo_lo[:, k]) for k in range(C)], first=False, last=True, check=True).then_inc(y_done, 1)

            probs_to_keys(0)
            scan_step(8)
            scan_inputs(1, 1, rhs_hi_part + rhs_lo_part, False, True)
            probs_to_keys(1)
            attend(0)
            scan_step(9)
            attend(1)
            mix_states(0)
            heads_to_features(0)
            scan_step(10)
            heads_to_features(1)
            mix_states(1)
            scan_step(11)
            mix_heads(0)
            mix_heads(1)
            scan_step(12)
            mix_states(2)
            mix_heads(2)
            scan_step(13)
            scan_step(14)

            def norm2_transposes(p):
                pe.wait_ge(x2hat_ready, 2 * p + 2)
                if p == 0:
                    pe.wait_ge(o_lo, 2)
                else:
                    pe.wait_ge(x2_ready, NT)
                    pe.wait_ge(xn2_c0, 2)
                for t in range(2):
                    for c in range(C):
                        ins = tr(norm2_bank(p, c)[:, t * P:(t + 1) * P], x2hat[:, 2 * p + t, c * P:(c + 1) * P])
                ins.then_inc(x2hat_T, 1)

            def up(p, j, parts=rhs_hi_part + rhs_lo_part):
                n = p * FJ + j
                if parts[0] == (0, 0):
                    if n == 0:
                        pe.wait_ge(state_m0, T)
                        pe.wait_ge(state_m1, T)
                        pe.wait_ge(w1_hi_ready, 2)
                        pe.wait_ge(w1_lo_ready, 1)
                    if n >= 4:
                        pe.wait_ge(gelu_done, n - 3)
                    if j == 0:
                        pe.wait_ge(xn2_c0, 2 * p + 1)
                        pe.wait_ge(xn2_c1, 2 * p + 1)
                if parts[-1] == (0, 1):
                    pe.wait_ge(xn2_split, p + 1)
                ins = product(bank[j % 4][:, (j // 4) * D:(j // 4 + 1) * D],
                              [(w1_hi[:, k, j * P:(j + 1) * P], w1_lo[:, k, j * P:(j + 1) * P]) for k in range(C)],
                              [(xn2_hi[:, p, k], xn2_lo[:, p, k]) for k in range(C)],
                              first=(parts[0] == (0, 0)), last=(parts[-1] == (0, 1)), parts=parts)
                if parts[-1] == (0, 1):
                    ins.then_inc(up_done, 1)

            def down(t, chunks=range(FJ)):
                p, i = t // 2, t % 2
                pe.wait_ge(w2_hi_ready, 4)
                pe.wait_ge(w2_lo_ready, 4)
                if t == 0:
                    pe.wait_ge(xn2_c1, 2)
                elif t == 1:
                    pe.wait_ge(x2_ready, 2)
                elif t == 2:
                    pe.wait_ge(xn2_c1, 4)
                else:
                    pe.wait_ge(xn2_c0, 4)
                if chunks[0] == 0:
                    pe.wait_ge(base2_ready, t + 1)
                    nc.tensor.matmul(down_bank[t][:, 0:D], ident, base2[:, t], start=True, stop=False)
                for j in chunks:
                    pe.wait_ge((g_even, g_odd)[j % 2], p * FJ // 2 + j // 2 + 1)
                    ins = product(down_bank[t][:, 0:D], [tuple(hidden(p, part, j)[:, i * P:(i + 1) * P] for part in (0, 1))],
                                  [(w2_hi[:, j], w2_lo[:, j])], first=False, last=(j == FJ - 1))
                if chunks[-1] == FJ - 1:
                    ins.then_inc(down_done, 1)

            def tail_transposes(t):
                pe.wait_ge(h2_ready, t + 1)
                for c in range(C):
                    ins = tr(down_bank[t][:, c * P:(c + 1) * P], h2[:, t, c * P:(c + 1) * P])
                ins.then_inc(h2_T, 1)

            def rotate(t):
                pe.wait_ge(had_ready, 1)
                pe.wait_ge(h2T_lo_s, t + 1)
                product(down_bank[t][:, 0:D], [(h2T_hi[:, t, k], h2T_lo[:, t, k]) for k in range(C)],
                        [(had[:, k], None) for k in range(C)]).then_inc(had_done, 1)

            def quant_transposes(t):
                pe.wait_ge(quant_ready, t + 1)
                for c in range(C):
                    ins = tr(down_bank[t][:, c * P:(c + 1) * P], quant[:, t, c * P:(c + 1) * P])
                ins.then_inc(quant_T, 1)

            def ternary(t):
                pe.wait_ge(quantT_ready, t + 1)
                product(down_bank[t][:, 0:D], [(quantT[:, t, k], None) for k in range(C)],
                        [(ternT_hi[:, k], ternT_lo[:, k]) for k in range(C)]).then_inc(fin_done, 1)

            norm2_transposes(0)
            scan_step(15)
            for j in (0, 1):
                up(0, j, rhs_hi_part)
            for j in (0, 1):
                up(0, j, rhs_lo_part)
            mix_states(3)
            mix_heads(3)
            for j in range(2, FJ):
                up(0, j)
            norm2_transposes(1)
            down(0)
            up(1, 0)
            up(1, 1)
            up(1, 2)
            up(1, 3)
            tail_transposes(0)
            for j in range(4, FJ):
                up(1, j)
            down(1, range(0, 4))
            rotate(0)
            down(1, range(4, FJ))
            down(2, range(0, 4))
            quant_transposes(0)
            down(2, range(4, FJ))
            tail_transposes(1)
            ternary(0)
            down(3, range(0, 4))
            rotate(1)
            tail_transposes(2)
            down(3, range(4, FJ))
            rotate(2)
            quant_transposes(1)
            ternary(1)
            tail_transposes(3)
            quant_transposes(2)
            rotate(3)
            ternary(2)
            quant_transposes(3)
            ternary(3)

        @block.scalar
        def _(act):
            def unit_views(u):
                c, part = units[u]
                if part == "w":
                    dst = [v[:, 2 * c:2 * c + 2].rearrange("p k n -> p (k n)") for v in (tokWT_hi, tokWT_lo)]
                    return unit_bank(u)[:, :], *dst
                src = unit_bank(u)[:, :].rearrange("p (j b i) -> p j i b", j=NP, i=NP)
                return src, *[v[:, 2 * c + part].rearrange("p (i j b) -> p j i b", i=NP, j=NP) for v in (xT_hi, xT_lo)]

            for u in range(len(units)):
                act.wait_ge(unit_T, u + 1)
                src, hi, _lo = unit_views(u)
                nc.scalar.copy(hi, src).then_inc(unit_hi, 1)
                if u == 3:
                    act.wait_ge(ld_sel, 48)
                    nc.scalar.copy(posb_hi, posb)
                    nc.scalar.copy(sel_hi, sel).then_inc(posb_hi_ready, 1)

            def token_rows(t):
                act.wait_ge(tok_done, t + 1)
                nc.scalar.copy(h[:, t], bank[t][:, 0:D]).then_inc(h_ready, 1)

            def weights_hi(load, n, pairs, done):
                act.wait_ge(load, n)
                for dst, src in pairs:
                    ins = nc.scalar.copy(dst, src)
                ins.then_inc(done, 1)

            token_rows(0)
            token_rows(1)
            weights_hi(ld_wb, 16, [(wb_hi[:], wb_in[:])], wb_hi_ready)
            weights_hi(ld_wkv, 32, [(hi[:].rearrange("p k (h d) -> p k h d", h=HPC),
                                     w[:].unsqueeze(2).to_broadcast([P, C, HPC, HD]))
                                    for w, hi in ((wk_in, wk_hi), (wv_in, wv_hi))], wkv_hi_ready)
            token_rows(2)
            token_rows(3)
            act.wait_ge(ld_ln, 64)

            def norm1(p):
                act.wait_ge(xhat_T, p + 1)
                for dst in (xn_hi, xn):
                    nc.scalar.activation(dst[:, 0, pair_cols(p)], norm1_bank(p, 0)[:, 0:2 * P], ACT.Identity,
                                         scale=ln1w[:, 0:1], bias=ln1b[:, 0:1]).then_inc(xn_c0, 1)

            def down_weights_hi(j):
                weights_hi(ld_w2, 16, [(w2_hi[:, j:j + 2], w2_in[:, j:j + 2])], w2_hi_ready)

            def tanh_step(t):
                for m, (step, state) in enumerate(((step_m0, state_m0), (step_m1, state_m1))):
                    if t == 0:
                        act.wait_ge(pre_done, 1)
                    else:
                        act.wait_ge(step, t)
                    nc.scalar.activation(hid[:, m, t * B:(t + 1) * B], scan_bank(m, t % 2)[:, t // 2 * B:(t // 2 + 1) * B],
                                         ACT.Tanh).then_inc(state, 1)

            def copy_after(ready, n, dst, src, done):
                act.wait_ge(ready, n)
                nc.scalar.copy(dst, src).then_inc(done, 1)

            def states_hi(t):
                act.wait_ge(state_m0, TPT * (t + 1))
                act.wait_ge(state_m1, TPT * (t + 1))
                nc.scalar.copy(hid_hi[:, :, tile_cols(t)], hid[:, :, tile_cols(t)]).then_inc(hid_hi_ready, 1)

            def exp_half(n):
                act.wait_ge(s_shifted, n + 1)
                v = prob[:, n].rearrange("p h s -> p (h s)")
                nc.scalar.activation(v, v, ACT.Exp).then_inc(exp_done, 1)

            norm1(0)
            act.wait_ge(a_T, 1)
            nc.scalar.copy(AT[:].rearrange("p k n -> p (k n)"), bank[5][:, :]).then_inc(a_ready, 1)
            weights_hi(ld_wq, 16, [(wq_hi[:], wq_in[:])], wq_hi_ready)
            tanh_step(0)
            norm1(1)
            tanh_step(1)
            weights_hi(ld_w1, 32, [(w1_hi[:, 0], w1_in[:, 0])], w1_hi_ready)
            weights_hi(ld_w1, 32, [(w1_hi[:, 1], w1_in[:, 1])], w1_hi_ready)
            copy_after(k_done, 1, krep.rearrange("p (b s) -> p s b", b=B),
                       bank[4][:, :].rearrange("p (s b) -> p s b", b=B), krep_ready)
            tanh_step(2)
            weights_hi(ld_wc, 16, [(wc_hi[:], wc_in[:])], wco_hi_ready)
            copy_after(v_done, 1, vT.rearrange("p (b s) -> p s b", b=B),
                       bank[5][0:HD, :].rearrange("p (s b) -> p s b", b=B), vT_ready)
            tanh_step(3)
            weights_hi(ld_wo, 16, [(wo_hi[:], wo_in[:])], wco_hi_ready)
            copy_after(q0_done, 1, qT[:, :, 0, :].rearrange("p b t -> p t b"),
                       bank[6][:, :].rearrange("p (t b) -> p t b", b=B), q0_ready)
            tanh_step(4)
            down_weights_hi(0)
            copy_after(q1_done, 1, qT[:, :, 1, :].rearrange("p b t -> p t b"),
                       bank[7][:, :].rearrange("p (t b) -> p t b", b=B), q1_ready)
            down_weights_hi(2)
            tanh_step(5)
            copy_after(vsd_done, 1, v_sd[:].rearrange("p (t e) d -> p e t d", e=HPC),
                       bank[4][:, :].rearrange("p (e t d) -> p e t d", e=HPC, t=NT), vsd_ready)

            def block_values_first(heads):
                act.wait_ge(vsd_ready, 1)
                act.wait_ge(wb_split, 1)
                act.wait_ge(wq_split, 1)
                act.wait_ge(wco_split, 2)
                for e in heads:
                    nc.scalar.activation(vblk[0][:, :, e], v_sd[:, 0:B // 2], ACT.Copy,
                                         scale=mask_v[:, e:e + 1]).then_inc(vblk_act, 1)

            states_hi(0)
            tanh_step(6)
            block_values_first(range(0, 2))
            exp_half(0)
            tanh_step(7)
            block_values_first(range(2, 4))
            exp_half(1)
            act.wait_ge(tern_T, 1)
            copy_after(pT_done, 1, pT[:, 0:512], bank[6][:, :], pT_ready)
            block_values_first(range(4, 6))
            tanh_step(8)
            block_values_first(range(6, HPC))
            copy_after(pT_done, 2, pT[:, 512:1024], bank[7][:, :], pT_ready)
            states_hi(1)
            down_weights_hi(4)
            tanh_step(9)
            down_weights_hi(6)
            copy_after(tern_T, 1, ternT_hi[:].rearrange("p k n -> p (k n)"), bank[5][:, :], ternT_hi_s)
            tanh_step(10)

            def heads_hi(n):
                act.wait_ge(o_done, n + 1)
                for c in range(C):
                    ins = nc.scalar.copy(
                        oT_hi[:, c].rearrange("p (t b) -> p b t", b=B)[:, 16 * n:16 * n + 16],
                        bank[6 + n][:, :].rearrange("p (b c t) -> p b c t", c=C, t=T)[:, :, c])
                ins.then_inc(o_hi, 1)

            heads_hi(0)
            heads_hi(1)
            tanh_step(11)
            states_hi(2)
            tanh_step(12)
            tanh_step(13)
            tanh_step(14)

            def norm2(p):
                act.wait_ge(x2hat_T, p + 1)
                for dst in (xn2_hi, xn2):
                    nc.scalar.activation(dst[:, p, 0], norm2_bank(p, 0)[:, 0:2 * P], ACT.Identity,
                                         scale=ln2w[:, 0:1], bias=ln2b[:, 0:1]).then_inc(xn2_c0, 1)

            def gelu(p, j):
                n = p * FJ + j
                act.wait_ge(up_done, n + 1)
                if n >= FJ:
                    act.wait_ge((g_even, g_odd)[j % 2], j // 2 + 1)
                for dst in (g[:, j], hidden(p, 0, j)):
                    ins = nc.scalar.activation(dst, bank[j % 4][:, (j // 4) * D:(j // 4 + 1) * D], ACT.Gelu,
                                               bias=b1c[:, j:j + 1])
                ins.then_inc(gelu_done, 1)

            def tail_hi(t):
                act.wait_ge(h2_T, t + 1)
                nc.scalar.copy(h2T_hi[:, t].rearrange("p k n -> p (k n)"), down_bank[t][:, 0:D]).then_inc(h2T_hi_s, 1)

            def quant_copy(t):
                act.wait_ge(quant_T, t + 1)
                nc.scalar.activation(quantT[:, t].rearrange("p k n -> p (k n)"), down_bank[t][:, 0:D], ACT.Copy,
                                     bias=-ROUND).then_inc(quantT_ready, 1)

            norm2(0)
            tanh_step(15)
            states_hi(3)
            for j in range(FJ):
                gelu(0, j)
            norm2(1)
            for j in range(FJ):
                gelu(1, j)
                if j == 2:
                    tail_hi(0)
            quant_copy(0)
            tail_hi(1)
            tail_hi(2)
            quant_copy(1)
            tail_hi(3)
            quant_copy(2)
            quant_copy(3)

        @block.vector
        def _(dve):
            count = [0]

            def step(ins):
                ins.then_inc(dve_done, 1)
                count[0] += 1
                return count[0]

            def after(n):
                dve.wait_ge(dve_done, n)

            def lo_part(dst, full, hi):
                return nc.vector.tensor_tensor(dst, full, hi.bitcast(F32), ALU.subtract)

            dve.wait_ge(ld_x[0], 16)
            group_patches(nc.vector, 0, 0).then_inc(x_grouped_dve, 1)
            for u in range(len(units)):
                c, part = units[u]
                if part == 0 and c + 1 < CH:
                    dve.wait_ge(ld_x[c + 1], 16)
                    group_patches(nc.vector, c + 1, 0).then_inc(x_grouped_dve, 1)
                dve.wait_ge(unit_hi, u + 1)
                if part == "w":
                    hi, lo = [v[:, 2 * c:2 * c + 2].rearrange("p k n -> p (k n)") for v in (tokWT_hi, tokWT_lo)]
                    src = unit_bank(u)[:, :]
                else:
                    src = unit_bank(u)[:, :].rearrange("p (j b i) -> p j i b", j=NP, i=NP)
                    hi, lo = [v[:, 2 * c + part].rearrange("p (i j b) -> p j i b", i=NP, j=NP) for v in (xT_hi, xT_lo)]
                lo_part(lo, src, hi).then_inc(unit_lo, 1)
                if u == 3:
                    dve.wait_ge(posb_hi_ready, 1)
                    lo_part(posb_lo, posb, posb_hi).then_inc(posb_split, 1)
                    dve.wait_ge(ld_fw, 16)
                    after(step(nc.vector.tensor_reduce(wsc[:, 0], fw_in[:], AX.X, ALU.add, apply_absolute_value=True)))
                    after(step(nc.vector.tensor_scalar(wsc[:, 0], wsc[:, 0], 1.0 / D, 1e-5, ALU.mult, ALU.max)))
                    nc.vector.tensor_scalar(wsc[:, 1], wsc[:, 0], 0.5, None, ALU.mult)
                    nc.vector.tensor_scalar(wsc[:, 2], wsc[:, 0], -0.5, None, ALU.mult).then_inc(wsc_ready, 1)

            def moments(rows, t):
                after(step(nc.vector.bn_stats(stats[:, t], rows)))
                return step(nc.vector.bn_aggr(mv[:, t], stats[:, t]))

            def norm1_moments(p):
                for t in (2 * p, 2 * p + 1):
                    dve.wait_ge(h_ready, t + 1)
                    n = moments(h[:, t], t)
                after(n)
                nc.vector.tensor_scalar(var[:, 2 * p:2 * p + 2], mv[:, 2 * p:2 * p + 2, 1], EPS, None,
                                        ALU.add).then_inc(var1, 1)

            def norm1_rows(p):
                dve.wait_ge(rstd1, p + 1)
                for t in (2 * p, 2 * p + 1):
                    nc.vector.tensor_scalar(xhat[:, t], h[:, t], mv[:, t, 0:1], rstd[:, t:t + 1],
                                            ALU.subtract, ALU.mult).then_inc(xhat_ready, 1)

            def norm1_features(p):
                dve.wait_ge(xhat_T, p + 1)
                dve.wait_ge(ld_ln, 64)
                for dst in (xn_hi, xn):
                    nc.vector.tensor_scalar(dst[:, 1, pair_cols(p)], norm1_bank(p, 1)[:, 0:2 * P],
                                            ln1w[:, 1:2], ln1b[:, 1:2], ALU.mult, ALU.add).then_inc(xn_c1, 1)
                dve.wait_ge(xn_c0, 2 * p + 2)
                dve.wait_ge(xn_c1, 2 * p + 2)
                lo_part(xn_lo[:, :, pair_cols(p)], xn[:, :, pair_cols(p)], xn_hi[:, :, pair_cols(p)]).then_inc(xn_split, 1)

            norm1_moments(0)
            norm1_rows(0)
            norm1_moments(1)
            norm1_features(0)
            norm1_rows(1)
            norm1_features(1)

            dve.wait_ge(ld_gates, 48)
            for t in range(NT):
                if t:
                    after(n)
                n = step(nc.vector.scalar_tensor_tensor(junk, h[:, t], 1.0, wg_row[:, :], ALU.mult, ALU.mult,
                                                        accum_out=sc_rows[:, t:t + 1]))
            after(n)
            n_score = step(nc.vector.tensor_scalar(sc_rows[:, :], sc_rows[:, :], bg_col[:, 0:1], None, ALU.add))

            dve.wait_ge(krep_ready, 1)
            dve.wait_ge(ld_cst, 16)
            for e in range(HPC):
                nc.vector.tensor_scalar(kblk[:, :, e], krep.rearrange("p (b s) -> p b s", b=B), mask_k[:, e:e + 1], None,
                                        ALU.mult).then_inc(kblk_ready, 1)
            dve.wait_ge(vm_T, 1)
            nc.vector.tensor_tensor(v_masked, bank[5][:, 0:NT * HD].rearrange("p (t d) -> p t d", t=NT)
                                    .unsqueeze(1).to_broadcast([P, HPC, NT, HD]),
                                    mask_v.unsqueeze(2).unsqueeze(3).to_broadcast([P, HPC, NT, HD]),
                                    ALU.mult).then_inc(vm_ready, 1)
            after(n_score)
            for k in range(TPT):
                n = step(nc.vector.tensor_copy(sc[:, :].rearrange("b (t k) -> b t k", k=TPT)[:, :, k],
                                               sc_rows[B * k:B * k + B, :]))
            after(n)
            other = sc[:, :].unsqueeze(1).to_broadcast([B, T, T])
            own = sc[:, :].unsqueeze(2).to_broadcast([B, T, T])
            step(nc.vector.tensor_tensor(gt[:], other, own, ALU.is_gt))
            after(step(nc.vector.tensor_tensor(eq[:], other, own, ALU.is_equal)))
            after(step(nc.vector.tensor_tensor(eq[:], eq[:], earlier[0:B].rearrange("b (t s) -> b t s", s=T), ALU.mult)))
            after(step(nc.vector.tensor_tensor(gt[:], gt[:], eq[:], ALU.add)))
            after(step(nc.vector.tensor_reduce(rank[:, :], gt[:], AX.X, ALU.add)))
            after(step(nc.vector.tensor_scalar(m_bt[:, :], rank[:, :], TOPK - 0.5, None, ALU.is_lt)))
            for k in range(TPT):
                step(nc.vector.tensor_copy(m_rows[B * k:B * k + B, :],
                                           m_bt[:, :].rearrange("b (t k) -> b t k", k=TPT)[:, :, k]))
            step(nc.vector.tensor_scalar(gate[:, 0:1], sg_col[:, :], -1.0, None, ALU.mult))
            after(step(nc.vector.tensor_scalar(gate[:, 1:2], sg_col[:, :], 1.0, None, ALU.add)))
            nc.vector.tensor_scalar(c_rows[:, :], m_rows[:, :], gate[:, 0:1], gate[:, 1:2],
                                    ALU.mult, ALU.add).then_inc(mask_ready, 1)

            def split_states(t):
                dve.wait_ge(hid_hi_ready, t + 1)
                lo_part(hid_lo[:, :, tile_cols(t)], hid[:, :, tile_cols(t)], hid_hi[:, :, tile_cols(t)]).then_inc(hid_split, 1)

            def shift(n):
                dve.wait_ge(s_done, n + 1)
                dve.wait_ge(tern_ready, 1)
                s = bank[6 + n][:, :].rearrange("p (h s) -> p h s", s=T)
                after(step(nc.vector.tensor_reduce(smax[:, n], s, AX.X, ALU.max)))
                nc.vector.tensor_tensor(prob[:, n], s, smax[:, n].unsqueeze(2).to_broadcast([P, 32, T]),
                                        ALU.subtract).then_inc(s_shifted, 1)

            def sums(n):
                dve.wait_ge(exp_done, n + 1)
                after(step(nc.vector.tensor_reduce(ssum[:, n], prob[:, n], AX.X, ALU.add)))
                return step(nc.vector.reciprocal(srec[:, n], ssum[:, n]))

            def scale_heads(n, n_sum):
                dve.wait_ge(o_rows_done, n + 1)
                after(n_sum)
                nc.vector.tensor_tensor(head_rows[:, n].rearrange("p (h d) -> p h d", d=HD),
                                        bank[6 + n][:, :].rearrange("p (h d) -> p h d", d=HD),
                                        srec[:, n].unsqueeze(2).to_broadcast([P, 32, HD]), ALU.mult).then_inc(o_rows_ready, 1)

            def block_values_last():
                dve.wait_ge(vsd_ready, 1)
                dve.wait_ge(s_done, 1)
                for e in range(HPC):
                    nc.vector.tensor_scalar(vblk[1][:, :, e], v_sd[:, B // 2:B], mask_v[:, e:e + 1],
                                            None, ALU.mult).then_inc(vblk_dve, 1)

            shift(0)
            split_states(0)
            shift(1)
            block_values_last()
            n_sum0 = sums(0)
            n_sum1 = sums(1)
            scale_heads(0, n_sum0)
            split_states(1)
            scale_heads(1, n_sum1)
            dve.wait_ge(ternT_hi_s, 1)
            lo_part(ternT_lo[:].rearrange("p k n -> p (k n)"), bank[5][:, :],
                    ternT_hi[:].rearrange("p k n -> p (k n)")).then_inc(ternT_split, 1)

            def heads_lo(n):
                dve.wait_ge(o_hi, n + 1)
                for c in range(C):
                    ins = lo_part(oT_lo[:, c].rearrange("p (t b) -> p b t", b=B)[:, 16 * n:16 * n + 16],
                                  bank[6 + n][:, :].rearrange("p (b c t) -> p b c t", c=C, t=T)[:, :, c],
                                  oT_hi[:, c].rearrange("p (t b) -> p b t", b=B)[:, 16 * n:16 * n + 16])
                ins.then_inc(o_lo, 1)

            def residual(t):
                dve.wait_ge(skip_ready, t + 1)
                dve.wait_ge(hc_ready, t + 1)
                return step(nc.vector.scalar_tensor_tensor(skip[:, t], skip[:, t], m_rows[:, t:t + 1], hc[:, t],
                                                           ALU.mult, ALU.add))

            residual(0)
            residual(1)
            heads_lo(0)
            heads_lo(1)
            split_states(2)
            residual(2)
            n_residual = residual(3)
            after(n_residual)

            def add_mixed(p):
                dve.wait_ge(y_done, 2 * p + 2)
                for t in (2 * p, 2 * p + 1):
                    nc.vector.scalar_tensor_tensor(x2[:, t], bank[4 + p][:, (t % 2) * D:(t % 2 + 1) * D],
                                                   m_rows[:, t:t + 1], skip[:, t], ALU.mult, ALU.add).then_inc(x2_ready, 1)
                for t in (2 * p, 2 * p + 1):
                    dve.wait_ge(x2_ready, t + 1)
                    n = moments(x2[:, t], t)
                after(n)
                nc.vector.tensor_scalar(var[:, 2 * p:2 * p + 2], mv[:, 2 * p:2 * p + 2, 1], EPS, None,
                                        ALU.add).then_inc(var2, 1)

            def norm2(p):
                dve.wait_ge(rstd2, p + 1)
                for t in (2 * p, 2 * p + 1):
                    nc.vector.tensor_scalar(x2hat[:, t], x2[:, t], mv[:, t, 0:1], rstd[:, t:t + 1],
                                            ALU.subtract, ALU.mult).then_inc(x2hat_ready, 1)

            def split_norm2(p):
                dve.wait_ge(x2hat_T, p + 1)
                for dst in (xn2_hi, xn2):
                    nc.vector.tensor_scalar(dst[:, p, 1], norm2_bank(p, 1)[:, 0:2 * P], ln2w[:, 1:2], ln2b[:, 1:2],
                                            ALU.mult, ALU.add).then_inc(xn2_c1, 1)
                dve.wait_ge(xn2_c0, 2 * p + 2)
                dve.wait_ge(xn2_c1, 2 * p + 2)
                lo_part(xn2_lo[:, p], xn2[:, p], xn2_hi[:, p]).then_inc(xn2_split, 1)

            def split_gelu(p, j):
                dve.wait_ge(gelu_done, p * FJ + j + 1)
                lo_part(hidden(p, 1, j), g[:, j], hidden(p, 0, j)).then_inc(g_even, 1)

            def tail_norm_a(t):
                dve.wait_ge(down_done, t + 1)
                after(moments(down_bank[t][:, 0:D], t))
                nc.vector.tensor_scalar(var[:, t:t + 1], mv[:, t, 1:2], EPS, None, ALU.add).then_inc(var3, 1)

            def tail_norm_b(t):
                dve.wait_ge(rstd3, t + 1)
                nc.vector.tensor_scalar(h2[:, t], down_bank[t][:, 0:D], mv[:, t, 0:1], rstd[:, t:t + 1],
                                        ALU.subtract, ALU.mult).then_inc(h2_ready, 1)

            def tail_lo(t):
                dve.wait_ge(h2T_hi_s, t + 1)
                lo_part(h2T_lo[:, t].rearrange("p k n -> p (k n)"), down_bank[t][:, 0:D],
                        h2T_hi[:, t].rearrange("p k n -> p (k n)")).then_inc(h2T_lo_s, 1)

            def quantise_scale(t):
                dve.wait_ge(had_done, t + 1)
                after(step(nc.vector.tensor_reduce(amax[:, t:t + 1], down_bank[t][:, 0:D], AX.X, ALU.max,
                                                   apply_absolute_value=True)))
                after(step(nc.vector.tensor_scalar(qscale[:, t:t + 1], amax[:, t:t + 1], 1e-5, 1.0 / QMAX,
                                                   ALU.max, ALU.mult)))
                return step(nc.vector.reciprocal(qinv[:, t:t + 1], qscale[:, t:t + 1]))

            def quantise(t, n_scale):
                after(n_scale)
                after(step(nc.vector.tensor_scalar(quant[:, t], down_bank[t][:, 0:D], qinv[:, t:t + 1], QMAX,
                                                   ALU.mult, ALU.min)))
                nc.vector.tensor_scalar(quant[:, t], quant[:, t], QMIN, ROUND, ALU.max, ALU.add).then_inc(quant_ready, 1)

            def last_norm_a(t):
                dve.wait_ge(fin_done, t + 1)
                after(step(nc.vector.scalar_tensor_tensor(f_rows[:, t], down_bank[t][:, 0:D], qscale[:, t:t + 1],
                                                          h2[:, t], ALU.mult, ALU.add)))
                after(moments(f_rows[:, t], t))
                nc.vector.tensor_scalar(var[:, t:t + 1], mv[:, t, 1:2], EPS, None, ALU.add).then_inc(var4, 1)

            def last_norm_b(t):
                dve.wait_ge(rstd4, t + 1)
                nc.vector.tensor_scalar(o_rows[:, t], f_rows[:, t], mv[:, t, 0:1], rstd[:, t:t + 1],
                                        ALU.subtract, ALU.mult).then_inc(out_ready, 1)

            add_mixed(0)
            norm2(0)
            split_norm2(0)
            split_states(3)
            for j in (0,):
                split_gelu(0, j)
            add_mixed(1)
            norm2(1)
            for j in (2, 4, 6):
                split_gelu(0, j)
            split_norm2(1)
            tail_norm_a(0)
            split_gelu(1, 0)
            tail_norm_b(0)
            split_gelu(1, 2)
            tail_lo(0)
            split_gelu(1, 4)
            split_gelu(1, 6)
            quantise(0, quantise_scale(0))
            tail_norm_a(1)
            tail_norm_b(1)
            tail_norm_a(2)
            tail_lo(1)
            last_norm_a(0)
            tail_norm_b(2)
            last_norm_b(0)
            n = quantise_scale(1)
            tail_lo(2)
            quantise(1, n)
            tail_norm_a(3)
            n = quantise_scale(2)
            tail_norm_b(3)
            quantise(2, n)
            tail_lo(3)
            last_norm_a(1)
            n = quantise_scale(3)
            last_norm_b(1)
            quantise(3, n)
            last_norm_a(2)
            last_norm_b(2)
            last_norm_a(3)
            last_norm_b(3)

        @block.gpsimd
        def _(pool):
            count = [0]

            def step(ins):
                ins.then_inc(pool_done, 1)
                count[0] += 1
                return count[0]

            def after(n):
                pool.wait_ge(pool_done, n)

            def lo_part(hi_ready, n, full, hi, lo, done):
                pool.wait_ge(hi_ready, n)
                nc.gpsimd.tensor_tensor(lo, full, hi.bitcast(F32), ALU.subtract).then_inc(done, 1)

            def inverse_root(t, n, ready, value, done):
                pool.wait_ge(ready, value)
                nc.gpsimd.tensor_tensor(rstd[:, t:t + n], var[:, t:t + n], neg_half[:, 0:n], ALU.pow).then_inc(done, 1)

            nc.gpsimd.dma_start(posb[0:T, :], tok_pos).then_inc(ld_sel, 16)
            nc.gpsimd.dma_start(posb[T:T + 1, :], tok_b.rearrange("(a d) -> a d", a=1)).then_inc(ld_sel, 16)
            nc.gpsimd.dma_start(sel[:], row_sel).then_inc(ld_sel, 16)
            n_half = step(nc.gpsimd.memset(neg_half[:, :], -0.5))
            for c in range(CH):
                pool.wait_ge(ld_x[c], 16)
                group_patches(nc.gpsimd, c, 1).then_inc(x_grouped_pool, 1)
            pool.wait_ge(wsc_ready, 1)
            for a in range(C):
                step(nc.gpsimd.tensor_scalar(wpos[:, a], fw_in[:, a], wsc[:, 1, a:a + 1], wsc[:, 0, a:a + 1],
                                             ALU.is_gt, ALU.mult))
                n = step(nc.gpsimd.tensor_scalar(wneg[:, a], fw_in[:, a], wsc[:, 2, a:a + 1], wsc[:, 0, a:a + 1],
                                                 ALU.is_lt, ALU.mult))
            after(n)
            nc.gpsimd.tensor_tensor(tern[:], wpos[:], wneg[:], ALU.subtract).then_inc(tern_ready, 1)
            inverse_root(0, 2, var1, 1, rstd1)
            lo_part(wb_hi_ready, 1, wb_in[:], wb_hi[:], wb_lo[:], wb_split)
            inverse_root(2, 2, var1, 2, rstd1)
            pool.wait_ge(wkv_hi_ready, 1)
            for w, hi, lo in ((wk_in, wk_hi, wk_lo), (wv_in, wv_hi, wv_lo)):
                rep = w[:].unsqueeze(2).to_broadcast([P, C, HPC, HD])
                ins = nc.gpsimd.tensor_tensor(lo[:].rearrange("p k (h d) -> p k h d", h=HPC), rep,
                                              hi[:].bitcast(F32).rearrange("p k (h d) -> p k h d", h=HPC), ALU.subtract)
            ins.then_inc(wkv_split, 1)
            lo_part(wq_hi_ready, 1, wq_in[:], wq_hi[:], wq_lo[:], wq_split)
            pool.wait_ge(ld_rows, 64)
            pool.wait_ge(xhat_T, 2)
            step(nc.gpsimd.tensor_tensor(dw, dp_row[:, :], l1w_row[:, :], ALU.mult))
            after(step(nc.gpsimd.tensor_tensor(db, dp_row[:, :], l1b_row[:, :], ALU.mult)))
            pool.wait_ge(xhat_ready, NT)
            for t in range(NT):
                after(step(nc.gpsimd.tensor_tensor(skip[:, t], xhat[:, t], dw, ALU.mult)))
                nc.gpsimd.tensor_tensor(skip[:, t], skip[:, t], db, ALU.add).then_inc(skip_ready, 1)
            lo_part(wco_hi_ready, 1, wc_in[:], wc_hi[:], wc_lo[:], wco_split)
            lo_part(wco_hi_ready, 2, wo_in[:], wo_hi[:], wo_lo[:], wco_split)
            lo_part(w1_hi_ready, 2, w1_in[:], w1_hi[:], w1_lo[:], w1_lo_ready)
            pool.wait_ge(mask_ready, 1)
            for t in range(NT):
                nc.gpsimd.tensor_scalar(hc[:, t], h[:, t], c_rows[:, t:t + 1], None, ALU.mult).then_inc(hc_ready, 1)
            pool.wait_ge(vsd_done, 1)
            for t in range(NT):
                n_hb2 = step(nc.gpsimd.tensor_tensor(hb2[:, t], h[:, t], b2_row[:, :], ALU.add))
            def weights_down_lo(j):
                pool.wait_ge(w2_hi_ready, j // 2 + 1)
                nc.gpsimd.tensor_tensor(w2_lo[:, j:j + 2], w2_in[:, j:j + 2], w2_hi[:, j:j + 2].bitcast(F32),
                                        ALU.subtract).then_inc(w2_lo_ready, 1)

            def base(t):
                pool.wait_ge(x2_ready, t + 1)
                nc.gpsimd.tensor_tensor(base2[:, t], x2[:, t], hb2[:, t], ALU.add).then_inc(base2_ready, 1)

            def split_gelu(p, j):
                pool.wait_ge(gelu_done, p * FJ + j + 1)
                nc.gpsimd.tensor_tensor(hidden(p, 1, j), g[:, j], hidden(p, 0, j).bitcast(F32),
                                        ALU.subtract).then_inc(g_odd, 1)

            for j in range(0, FJ, 2):
                weights_down_lo(j)
            pool.wait_ge(ld_cst, 16)
            nc.gpsimd.tensor_copy(had[:].rearrange("p k n -> p (k n)"), hadamard).then_inc(had_ready, 1)
            inverse_root(0, 2, var2, 1, rstd2)
            after(n_hb2)
            base(0)
            split_gelu(0, 1)
            inverse_root(2, 2, var2, 2, rstd2)
            base(1)
            split_gelu(0, 3)
            split_gelu(0, 5)
            split_gelu(0, 7)
            base(2)
            base(3)
            inverse_root(0, 1, var3, 1, rstd3)
            split_gelu(1, 1)
            split_gelu(1, 3)
            split_gelu(1, 5)
            split_gelu(1, 7)
            inverse_root(1, 1, var3, 2, rstd3)
            inverse_root(2, 1, var3, 3, rstd3)
            inverse_root(0, 1, var4, 1, rstd4)
            inverse_root(3, 1, var3, 4, rstd3)
            inverse_root(1, 1, var4, 2, rstd4)
            inverse_root(2, 1, var4, 3, rstd4)
            inverse_root(3, 1, var4, 4, rstd4)


_INS = ['x', 'L0_tok_W', 'L0_tok_b', 'L0_tok_pos_emb', 'L0_attn_Wg', 'L0_attn_bg', 'L0_attn_Wq', 'L0_attn_Wk',
        'L0_attn_Wv', 'L0_attn_Wo', 'L0_attn_A', 'L0_attn_Wb', 'L0_attn_Wc', 'L0_attn_Dp', 'L0_attn_W1',
        'L0_attn_b1', 'L0_attn_W2', 'L0_attn_b2', 'L0_attn_ln1_w', 'L0_attn_ln1_b', 'L0_attn_ln2_w',
        'L0_attn_ln2_b', 'L0_attn_skip_gate', 'L0_ffn_weight']


def kernel(**inputs):
    import numpy as _np
    import concourse.bacc as _bacc
    from concourse import mybir as _mybir
    from concourse.bass_utils import run_bass_kernel_spmd as _run

    nc = _bacc.Bacc("TRN2", target_bir_lowering=False, num_devices=1)
    arrays, args = {}, []
    consts, row_sel = shape_constants()
    given = [(name, inputs[name]) for name in _INS] + [("consts", consts), ("row_sel", row_sel)]
    for name, value in given:
        a = _np.ascontiguousarray(value)
        arrays[f"in_{name}_dram"] = a
        args.append(nc.dram_tensor(f"in_{name}_dram", a.shape, _mybir.dt.from_np(a.dtype), kind="ExternalInput").ap())
    args.append(nc.dram_tensor("out_0_dram", (B, T, D), F32, kind="ExternalOutput").ap())
    vit_block(nc, *args)
    r = _run(nc, [arrays], core_ids=[0])
    return r.results[0]["out_0_dram"]
```

```python
from contextlib import ExitStack

import numpy as np

import concourse.bass as bass
from concourse import mybir

F32 = mybir.dt.float32
F32R = mybir.dt.float32r
ALU = mybir.AluOpType
ACT = mybir.ActivationFunctionType
AX = mybir.AxisListType

P = 128
B = 32
NP = 4
T = NP * NP
PS = 16
CH = 3
D = 256
C = D // P
H = 16
HD = D // H
HPC = P // HD
R = B * T
NT = R // P
TPT = T // NT
KT = CH * PS * PS // P
F = 4 * D
FJ = F // P
TOPK = T // 4
EPS = 1e-5
ROUND = 1.5 * 2.0 ** 23
QMAX, QMIN = 7.0, -8.0
V_HEAD = HPC - 32 // HD
V0 = V_HEAD * HD


def shape_constants():
    h = np.array([[1.0]])
    while h.shape[0] < D:
        h = np.block([[h, h], [h, -h]])
    h = ((h - h.mean(0, keepdims=True)) / np.sqrt(D)).astype(np.float32).reshape(C, P, D).transpose(1, 0, 2).reshape(P, C * D)
    head = (np.arange(P)[:, None] // HD == np.arange(HPC)[None, :]).astype(np.float32)
    earlier = (np.arange(T)[None, :] < np.arange(T)[:, None]).astype(np.float32).reshape(1, T * T)
    spread = (np.arange(P)[:, None] % T == np.arange(P)[None, :] % T).astype(np.float32)
    consts = np.concatenate([np.eye(P, dtype=np.float32), head / np.sqrt(HD), head, spread,
                             np.repeat(earlier, P, 0), h], axis=1).astype(np.float32)
    token = np.arange(R) // B
    rows = np.concatenate([(token[None, :] == np.arange(T)[:, None]), np.ones((1, R))], 0).astype(np.float32)
    return np.ascontiguousarray(consts), np.ascontiguousarray(rows)


def vit_block(nc, x, tok_W, tok_b, tok_pos, Wg, bg, Wq, Wk, Wv, Wo, A, Wb, Wc, Dp, W1, b1, W2, b2,
              ln1_w, ln1_b, ln2_w, ln2_b, skip_gate, ffn_w, consts, row_sel, out):
    with ExitStack() as ctx:
        def sb(name, shape, dt=F32):
            return ctx.enter_context(nc.sbuf_tensor(name, shape, dt))

        def sem(name):
            return ctx.enter_context(nc.semaphore(name))

        cst = sb("cst", [P, 2 * P + 2 * HPC + T * T + C * D])
        o = P
        ident = cst[:, 0:P]
        mask_k = cst[:, o:o + HPC]
        mask_v = cst[:, o + HPC:o + 2 * HPC]
        o += 2 * HPC
        spread = cst[:, o:o + P]
        o += P
        earlier = cst[:, o:o + T * T]
        hadamard = cst[:, o + T * T:]
        a_in = sb("a_in", [P, C, D])
        AT = sb("AT", [P, C, D])

        def carve(tensor, *shapes):
            at, views = 0, []
            for shape in shapes:
                size = int(np.prod(shape))
                names = " ".join("abcd"[:len(shape)])
                views.append(tensor[:, at:at + size].rearrange(f"p ({names}) -> p {names}",
                                                               **dict(zip("abcd", shape))))
                at += size
            return views

        early = sb("early", [P, CH * (PS * NP * PS + C * PS * PS)])
        x_in, w_in = carve(early, (CH, PS * NP * PS), (CH, C, PS * PS))
        kblk, dw, db = carve(early, (B, HPC, T), (D,), (D,))
        early_r = sb("early_r", [P, 2 * KT * (R + D)], F32R)
        xT_hi, xT_lo, tokWT_hi, tokWT_lo = carve(early_r, (KT, R), (KT, R), (KT, D), (KT, D))
        g_hi, g_lo, hid_hi, hid_lo, ternT_hi, ternT_lo, quantT, g2_lo_b = carve(
            early_r, (FJ, D), (FJ, D), (C, R), (C, R), (C, D), (C, D), (NT, C, P), (FJ // 2, D))
        proj_in = sb("proj_in", [P, 4 * C * D])
        wb_in, wq_in, wc_in, wo_in = carve(proj_in, *[(C, D)] * 4)
        vblk = [carve(t, (B // 2, HPC, HD))[0] for t in (proj_in, early)]

        def halves(name, chunks, cols):
            return sb(name + "_hi", [P, chunks, cols], F32R), sb(name + "_lo", [P, chunks, cols], F32R)

        proj_r = sb("proj_r", [P, (FJ + FJ // 2) * D], F32R)
        wb_hi, wb_lo, wq_hi, wq_lo, wkv_hi, wkv_lo = carve(proj_r, *[(C, D)] * 4, *[(C, P)] * 2)
        g2_hi, g2_lo_a = carve(proj_r, (FJ, D), (FJ // 2, D))
        wc_hi, wc_lo = halves("wc", C, D)
        wo_hi, wo_lo = halves("wo", C, D)
        w1_hi, w1_lo = halves("w1", C, F)
        w2_hi, w2_lo = halves("w2", FJ, D)
        ff_space = sb("ff_space", [P, C * F + FJ * D])
        x_by_patch, = carve(ff_space, (CH, 2, NP, P))
        w1_in, w2_in = carve(ff_space, (C, F), (FJ, D))
        g, h2, tail_rows = carve(ff_space, (FJ, D), (NT, D), (NT, D))

        def hidden(p, part, j):
            if p == 0:
                return (g_hi, g_lo)[part][:, j]
            if part == 0:
                return g2_hi[:, j]
            return g2_lo_a[:, j] if j < FJ // 2 else g2_lo_b[:, j - FJ // 2]
        wk_in = sb("wk_in", [P, C, HD])
        wv_in = sb("wv_in", [P, C, HD])
        had = sb("had", [P, C, D], F32R)
        ln1w = sb("ln1w", [P, C])
        ln1b = sb("ln1b", [P, C])
        ln2w = sb("ln2w", [P, C])
        ln2b = sb("ln2b", [P, C])
        b1c = sb("b1c", [P, FJ])
        wg_row = sb("wg_row", [P, D])
        b2_row = sb("b2_row", [P, D])
        dp_row = sb("dp_row", [P, D])
        l1w_row = sb("l1w_row", [P, D])
        l1b_row = sb("l1b_row", [P, D])
        bg_col = sb("bg_col", [P, 1])
        sg_col = sb("sg_col", [P, 1])
        fw_in = sb("fw_in", [P, C, D])
        tern = fw_in
        neg_half = sb("neg_half", [P, NT])

        h = sb("h", [P, NT, D])
        hb2_space = sb("hb2_space", [P, NT * D])
        (hb2,), (gt, eq, junk) = carve(hb2_space, (NT, D)), carve(hb2_space, (T, T), (T, T), (D,))
        gt, eq = gt[0:B], eq[0:B]
        sel, posb = [v[0:T + 1] for v in carve(hb2_space, (R,), (D,))]
        _, v_masked = carve(hb2_space, (2 * D,), (HPC, NT, HD))
        base2 = hb2
        xhat = sb("xhat", [P, NT, D])
        skip = xhat
        x2 = sb("x2", [P, NT, D])
        hc = x2
        xn_space = sb("xn_space", [P, C * R])
        xn, = carve(xn_space, (C, R))
        krep = xn_space[:, 0:R]
        vT = xn_space[0:HD, R:2 * R]
        xn2, = carve(xn_space, (2, C, D))
        xn_hi_space = sb("xn_hi_space", [P, C * R], F32R)
        xn_lo_space = sb("xn_lo_space", [P, C * R], F32R)
        (xn_hi,), (xn_lo,) = carve(xn_hi_space, (C, R)), carve(xn_lo_space, (C, R))
        (xn2_hi,), (xn2_lo,) = carve(xn_hi_space, (2, C, D)), carve(xn_lo_space, (2, C, D))
        q_space = sb("q_space", [P, B * C * T])
        (qT,), (x2hat,), (o_rows,) = carve(q_space, (B, C, T)), carve(q_space, (NT, D)), carve(q_space, (NT, D))
        pT = sb("pT", [P, B * C * T])
        f_rows, = carve(pT, (NT, D))
        prob_space = sb("prob_space", [P, B * C * T])
        (prob,), (head_rows,), (quant,) = [carve(prob_space, shape) for shape in ((2, 32, T), (2, 512), (NT, D))]
        wpos, wneg = carve(prob_space, (C, D), (C, D))
        o_hi_space = sb("o_hi_space", [P, C * R], F32R)
        o_lo_space = sb("o_lo_space", [P, C * R], F32R)
        (oT_hi,), (oT_lo,) = carve(o_hi_space, (C, R)), carve(o_lo_space, (C, R))
        sel_hi, (posb_hi, posb_lo) = o_hi_space[0:T + 1, 0:R], [v[0:T + 1] for v in carve(o_lo_space, (D,), (D,))]
        (h2T_hi,), (h2T_lo,) = carve(o_hi_space, (NT, C, P)), carve(o_lo_space, (NT, C, P))
        stats = sb("stats", [P, NT, 6])
        mv = sb("mv", [P, NT, 2])
        var = sb("var", [P, NT])
        rstd = sb("rstd", [P, NT])
        floor3 = sb("floor3", [P, NT])
        shift_tail = sb("shift_tail", [P, NT])
        hid = sb("hid", [P, C, R])
        v_sd = sb("v_sd", [P, B, HD])
        smax = sb("smax", [P, 2, 32])
        ssum = sb("ssum", [P, 2, 32])
        srec = sb("srec", [P, 2, 32])
        sc_rows = sb("sc_rows", [P, NT])
        sc = sb("sc", [B, T])
        rank = sb("rank", [B, T])
        m_bt = sb("m_bt", [B, T])
        m_rows = sb("m_rows", [P, NT])
        c_rows = sb("c_rows", [P, NT])
        gate = sb("gate", [P, 2])
        amax = sb("amax", [P, NT])
        qscale = sb("qscale", [P, NT])
        qinv = sb("qinv", [P, NT])
        qstep = sb("qstep", [P, NT])
        wsc = sb("wsc", [P, 3, C])
        bank = [ctx.enter_context(nc.psum_tensor(f"bank{i}", [P, 512], F32)) for i in range(8)]

        def by_head(w):
            return w.rearrange("p k (h d) -> p k h d", h=HPC)

        def scan_bank(m, par):
            return bank[2 * m + par]

        ld_ident, ld_cst, ld_sel, ld_a = sem("ld_ident"), sem("ld_cst"), sem("ld_sel"), sem("ld_a")
        ld_x = [sem(f"ld_x{c}") for c in range(CH)]
        ld_w = [sem(f"ld_tok{c}") for c in range(CH)]
        ld_ln, ld_wb, ld_wkv, ld_wq = sem("ld_ln"), sem("ld_wb"), sem("ld_wkv"), sem("ld_wq")
        ld_wc, ld_wo, ld_rows, ld_gates, ld_fw = sem("ld_wc"), sem("ld_wo"), sem("ld_rows"), sem("ld_gates"), sem("ld_fw")
        ld_w1, ld_w2, stored = sem("ld_w1"), sem("ld_w2"), sem("stored")
        x_grouped_dve, x_grouped_act, x_grouped_pool = sem("x_grouped_dve"), sem("x_grouped_act"), sem("x_grouped_pool")
        vm_T, vm_ready = sem("vm_T"), sem("vm_ready")
        unit_T, unit_hi, unit_lo = sem("unit_T"), sem("unit_hi"), sem("unit_lo")
        a_T, a_ready = sem("a_T"), sem("a_ready")
        tok_done, h_ready, var1, rstd1 = sem("tok_done"), sem("h_ready"), sem("var1"), sem("rstd1")
        xhat_ready, xhat_T, xn_c0, xn_c1, xn_split = (
            sem("xhat_ready"), sem("xhat_T"), sem("xn_c0"), sem("xn_c1"), sem("xn_split"))
        wb_split, wkv_split, wq_split, wco_split = sem("wb_split"), sem("wkv_split"), sem("wq_split"), sem("wco_split")
        had_ready, w1_hi_ready, w1_lo_ready, w2_hi_ready, w2_lo_ready = (
            sem("had_ready"), sem("w1_hi_ready"), sem("w1_lo_ready"), sem("w2_hi_ready"), sem("w2_lo_ready"))
        wb_hi_ready, wkv_hi_ready, wq_hi_ready, wco_hi_ready, hid_hi_ready = (
            sem("wb_hi_ready"), sem("wkv_hi_ready"), sem("wq_hi_ready"), sem("wco_hi_ready"), sem("hid_hi_ready"))
        pre_done, step_m0, step_m1 = sem("pre_done"), sem("step_m0"), sem("step_m1")
        state_m0, state_m1, hid_split = sem("state_m0"), sem("state_m1"), sem("hid_split")
        kv_done, krep_ready, kblk_ready = sem("kv_done"), sem("krep_ready"), sem("kblk_ready")
        vT_ready, vsd_done, vsd_ready = sem("vT_ready"), sem("vsd_done"), sem("vsd_ready")
        vblk_act, vblk_dve, o_rows_done, o_rows_ready = sem("vblk_act"), sem("vblk_dve"), sem("o_rows_done"), sem("o_rows_ready")
        q0_done, q1_done, q0_ready, q1_ready = sem("q0_done"), sem("q1_done"), sem("q0_ready"), sem("q1_ready")
        s_done, s_shifted = sem("s_done"), sem("s_shifted")
        exp_done, pT_done, pT_ready = sem("exp_done"), sem("pT_done"), sem("pT_ready")
        o_done, o_hi, o_lo = sem("o_done"), sem("o_hi"), sem("o_lo")
        mask_ready, skip_ready, hc_ready = sem("mask_ready"), sem("skip_ready"), sem("hc_ready")
        y_done, x2_ready, base2_ready, var2, rstd2 = sem("y_done"), sem("x2_ready"), sem("base2_ready"), sem("var2"), sem("rstd2")
        x2hat_ready, x2hat_T, xn2_c0, xn2_c1, xn2_split = (
            sem("x2hat_ready"), sem("x2hat_T"), sem("xn2_c0"), sem("xn2_c1"), sem("xn2_split"))
        up_done, gelu_done, g_even, g_odd, down_done = (
            sem("up_done"), sem("gelu_done"), sem("g_even"), sem("g_odd"), sem("down_done"))
        tail_rows_ready, var3, rstd3, shift3, h2_ready, h2_T, h2T_hi_s, h2T_lo_s = (
            sem("tail_rows_ready"), sem("var3"), sem("rstd3"), sem("shift3"), sem("h2_ready"), sem("h2_T"), sem("h2T_hi_s"), sem("h2T_lo_s"))
        had_done, quant_ready, quant_T, quantT_ready = sem("had_done"), sem("quant_ready"), sem("quant_T"), sem("quantT_ready")
        wsc_ready, posb_hi_ready, posb_split = sem("wsc_ready"), sem("posb_hi_ready"), sem("posb_split")
        tern_ready, tern_T, ternT_hi_s, ternT_split = sem("tern_ready"), sem("tern_T"), sem("ternT_hi_s"), sem("ternT_split")
        fin_done, var4, rstd4, out_ready, last_out_ready = (
            sem("fin_done"), sem("var4"), sem("rstd4"), sem("out_ready"), sem("last_out_ready"))
        dve_done = sem("dve_done")
        pool_done = sem("pool_done")

        block = ctx.enter_context(nc.Block())

        units = [(c, part) for c in range(CH) for part in ("w", 0, 1)]

        def unit_bank(u):
            return bank[4 + u % 4]

        def pair_cols(p):
            return slice(p * 2 * P, (p + 1) * 2 * P)

        def tile_cols(t):
            return slice(t * P, (t + 1) * P)

        down_bank = [bank[7], bank[4], bank[5], bank[6]]

        def norm1_bank(p, c):
            return bank[(6, 4)[p] + c]

        def norm2_bank(p, c):
            return bank[6] if c == 0 else (bank[7], bank[5])[p]

        def group_patches(engine, c, part):
            half = PS // 2
            src = x_in[:, c].rearrange("p (r j q) -> p j r q", r=PS, j=NP)[:, :, part * half:(part + 1) * half]
            dst = x_by_patch[:, c, part].rearrange("p j (r q) -> p j r q", r=half)
            return (engine.copy if engine is nc.scalar else engine.tensor_copy)(dst, src)

        @block.sync
        def _(sp):
            for c in range(CH):
                if c == 0:
                    sp.dma_start(cst[:, 0:P], consts[:, 0:P]).then_inc(ld_ident, 16)
                sp.dma_start(w_in[:, c], tok_W.rearrange("(a p) (c f) -> p c a f", p=P, c=CH)[:, c]).then_inc(ld_w[c], 16)
                sp.dma_start(x_in[:, c], x.rearrange("b c (i r) w -> c b i (r w)", i=NP)[c]).then_inc(ld_x[c], 16)
            sp.dma_start(fw_in[:], ffn_w.rearrange("(a p) n -> p a n", p=P)).then_inc(ld_fw, 16)
            sp.dma_start(a_in[:], A.rearrange("(a p) n -> p a n", p=P)).then_inc(ld_a, 16)
            sp.dma_start(wb_in[:], Wb.rearrange("(a p) n -> p a n", p=P)).then_inc(ld_wb, 16)
            for dst, src in ((ln1w, ln1_w), (ln1b, ln1_b), (ln2w, ln2_w), (ln2b, ln2_b)):
                sp.dma_start(dst[:], src.rearrange("(a p) -> p a", p=P), allow_slow_non_contiguous=True).then_inc(ld_ln, 16)
            sp.dma_start(wk_in[:], Wk.rearrange("(a p) n -> p a n", p=P)).then_inc(ld_wkv, 16)
            sp.dma_start(wv_in[:], Wv.rearrange("(a p) n -> p a n", p=P)).then_inc(ld_wkv, 16)
            sp.dma_start(wq_in[:], Wq.rearrange("(a p) n -> p a n", p=P)).then_inc(ld_wq, 16)
            sp.dma_start(cst[:, P:], consts[:, P:]).then_inc(ld_cst, 16)
            sp.dma_start(bg_col[:], bg.partition_broadcast(P)).then_inc(ld_gates, 16)
            sp.dma_start(sg_col[:], skip_gate.partition_broadcast(P)).then_inc(ld_gates, 16)
            sp.dma_start(wg_row[:], Wg.rearrange("d a -> (d a)").partition_broadcast(P)).then_inc(ld_gates, 16)
            for dst, src in ((dp_row, Dp), (l1w_row, ln1_w), (l1b_row, ln1_b), (b2_row, b2)):
                sp.dma_start(dst[:], src.partition_broadcast(P)).then_inc(ld_rows, 16)
            sp.dma_start(wc_in[:], Wc.rearrange("(a p) n -> p a n", p=P)).then_inc(ld_wc, 16)
            sp.dma_start(wo_in[:], Wo.rearrange("(a p) n -> p a n", p=P)).then_inc(ld_wo, 16)
            sp.wait_ge(unit_T, len(units))
            sp.dma_start(w1_in[:], W1.rearrange("(a p) n -> p a n", p=P)).then_inc(ld_w1, 16)
            sp.dma_start(b1c[:], b1.rearrange("(a p) -> p a", p=P), allow_slow_non_contiguous=True).then_inc(ld_w1, 16)
            sp.dma_start(w2_in[:], W2.rearrange("(a p) n -> p a n", p=P)).then_inc(ld_w2, 16)
            for t in range(NT):
                if t < NT - 1:
                    sp.wait_ge(out_ready, t + 1)
                else:
                    sp.wait_ge(last_out_ready, 1)
                sp.dma_start(out[:, TPT * t:TPT * (t + 1), :].rearrange("b k d -> k b d"), o_rows[:, t]).then_inc(stored, 16)
            sp.wait_ge(stored, 16 * NT)

        @block.tensor
        def _(pe):
            def tr(dst, src, identity=None):
                return nc.tensor.transpose(dst, src, ident if identity is None else identity)

            def product(dst, lhs, rhs, first=True, last=True, check=False, parts=((0, 0), (1, 0), (0, 1))):
                passes = [(i, a, b) for a, b in parts for i in range(len(lhs))
                          if lhs[i][a] is not None and rhs[i][b] is not None]
                for n, (i, a, b) in enumerate(passes):
                    ins = nc.tensor.matmul(dst, lhs[i][a], rhs[i][b], start=first and n == 0,
                                           stop=last and n == len(passes) - 1, skip_group_check=check)
                return ins

            rhs_hi_part, rhs_lo_part = ((0, 0), (1, 0)), ((0, 1),)

            def unit_transposes(u):
                c, part = units[u]
                if u >= 4:
                    pe.wait_ge(unit_lo, u - 3)
                dst = unit_bank(u)
                if part == "w":
                    pe.wait_ge(ld_w[c], 16)
                    for hf in range(2):
                        for a in range(C):
                            k = hf * C + a
                            ins = tr(dst[:, k * P:(k + 1) * P], w_in[:, c, a, hf * P:(hf + 1) * P])
                else:
                    if part == 0:
                        pe.wait_ge(x_grouped_dve, c + 1)
                    elif c == 0:
                        pe.wait_ge(x_grouped_act, 1)
                    else:
                        pe.wait_ge(x_grouped_pool, c)
                    for j in range(NP):
                        ins = tr(dst[:, j * P:(j + 1) * P], x_by_patch[:, c, part, j])
                ins.then_inc(unit_T, 1)

            def patch_product(k, p):
                c, part = k // 2, k % 2
                pe.wait_ge(unit_lo, 3 * c + part + 2)
                for t in (2 * p, 2 * p + 1):
                    ins = product(bank[t][:, 0:D], [(xT_hi[:, k, tile_cols(t)], xT_lo[:, k, tile_cols(t)])],
                                  [(tokWT_hi[:, k], tokWT_lo[:, k])], first=(k == 0), last=(k == KT - 1))
                    if k == KT - 1:
                        ins.then_inc(tok_done, 1)


            def place_product(p):
                pe.wait_ge(posb_split, 1)
                for t in (2 * p, 2 * p + 1):
                    product(bank[t][:, 0:D], [(sel_hi[:, tile_cols(t)], None)], [(posb_hi, posb_lo)],
                            first=False, last=False)

            def norm1_transposes(p):
                if p == 0:
                    pe.wait_ge(unit_lo, 8)
                else:
                    pe.wait_ge(unit_lo, 9)
                    pe.wait_ge(a_ready, 1)
                for t in (2 * p, 2 * p + 1):
                    pe.wait_ge(xhat_ready, t + 1)
                    for c in range(C):
                        ins = tr(norm1_bank(p, c)[:, t % 2 * P:(t % 2 + 1) * P], xhat[:, t, c * P:(c + 1) * P])
                ins.then_inc(xhat_T, 1)

            pe.wait_ge(ld_ident, 16)
            for u in (0, 1, 2, 3):
                unit_transposes(u)
            patch_product(0, 0)
            unit_transposes(4)
            unit_transposes(5)
            patch_product(1, 0)
            unit_transposes(6)
            unit_transposes(7)
            unit_transposes(8)
            place_product(0)
            for k in range(2, KT):
                patch_product(k, 0)
            patch_product(0, 1)
            place_product(1)
            for k in range(1, KT - 2):
                patch_product(k, 1)
            pe.wait_ge(ld_a, 16)
            for k in range(C):
                for a in range(C):
                    ins = tr(bank[5][:, (2 * k + a) * P:(2 * k + a + 1) * P], a_in[:, a, k * P:(k + 1) * P])
            ins.then_inc(a_T, 1)
            norm1_transposes(0)
            for k in range(KT - 2, KT):
                patch_product(k, 1)

            def scan_inputs(p, par, parts, first, last):
                for m in range(C):
                    rhs = [tuple(v[:, k, pair_cols(p)].rearrange("q (u e b) -> q u e b", e=2, b=B)[:, :, par, :]
                                 for v in (xn_hi, xn_lo)) for k in range(C)]
                    lhs = [(wb_hi[:, k, m * P:(m + 1) * P], wb_lo[:, k, m * P:(m + 1) * P]) for k in range(C)]
                    ins = product(scan_bank(m, par)[:, p * P:(p + 1) * P], lhs, rhs, first=first, last=last, check=True,
                                  parts=parts)
                return ins

            xn_pairs = [(xn_hi[:, k], xn_lo[:, k]) for k in range(C)]

            def queries(m, p, done, parts=rhs_hi_part + rhs_lo_part):
                ins = product(bank[6 + m][:, pair_cols(p)], [(wq_hi[:, k, m * P:(m + 1) * P], wq_lo[:, k, m * P:(m + 1) * P])
                                                             for k in range(C)],
                              [(hi[:, pair_cols(p)], lo[:, pair_cols(p)]) for hi, lo in xn_pairs],
                              first=(parts[0] == (0, 0)), last=(parts[-1] == (0, 1)), parts=parts)
                if p == 1:
                    ins.then_inc(done, 1)

            pe.wait_ge(wq_split, 1)
            pe.wait_ge(xn_c0, 2)
            pe.wait_ge(xn_c1, 2)
            queries(0, 0, q0_done, rhs_hi_part)
            queries(1, 0, q1_done, rhs_hi_part)
            pe.wait_ge(wb_split, 1)
            pe.wait_ge(h_ready, NT)
            for par in range(2):
                scan_inputs(0, par, rhs_hi_part, True, False)
            pe.wait_ge(xn_split, 1)
            for par in range(2):
                scan_inputs(0, par, rhs_lo_part, False, False).then_inc(pre_done, 1)
            norm1_transposes(1)

            def scan_step(t):
                dst = [scan_bank(m, t % 2)[:, t // 2 * B:(t // 2 + 1) * B] for m in range(C)]
                for k, state in ((0, state_m0), (1, state_m1)):
                    pe.wait_ge(state, t)
                    for m in range(C):
                        ins = nc.tensor.matmul(dst[m], AT[:, k, m * P:(m + 1) * P], hid[:, k, (t - 1) * B:t * B],
                                               start=False, stop=(k == 1), skip_group_check=True)
                        if k == 1:
                            ins.then_inc((step_m0, step_m1)[m], 1)

            def scores(n):
                pe.wait_ge(q0_ready, 1)
                pe.wait_ge(q1_ready, 1)
                pe.wait_ge(kblk_ready, HPC)
                for b in range(16 * n, 16 * n + 16):
                    i, q = b % 16 // 4, b % 4
                    ins = nc.tensor.matmul(bank[6 + n][32 * q:32 * q + 32, i * P:(i + 1) * P],
                                           qT[:, b].rearrange("p c t -> p (c t)"),
                                           kblk[:, b].rearrange("p h s -> p (h s)"), start=True, stop=True)
                ins.then_inc(s_done, 1)

            scan_step(1)
            queries(0, 0, q0_done, rhs_lo_part)
            queries(1, 0, q1_done, rhs_lo_part)
            pe.wait_ge(wkv_split, 1)
            pe.wait_ge(xn_c0, 4)
            pe.wait_ge(xn_c1, 3)
            wkv_pairs = [(wkv_hi[:, k], wkv_lo[:, k]) for k in range(C)]
            product(bank[4][:, :], wkv_pairs, xn_pairs, last=False, parts=rhs_hi_part)
            pe.wait_ge(xn_split, 2)
            product(bank[4][:, :], wkv_pairs, xn_pairs, first=False, parts=rhs_lo_part).then_inc(kv_done, 1)
            scan_step(2)
            queries(0, 1, q0_done)
            scan_step(3)
            pe.wait_ge(vT_ready, 1)
            for t in range(NT):
                ins = tr(bank[5][:, t * HD:(t + 1) * HD], vT[:, t * P:(t + 1) * P], ident[0:HD, 0:HD])
            ins.then_inc(vm_T, 1)
            queries(1, 1, q1_done)
            scan_step(4)
            pe.wait_ge(krep_ready, 2)
            pe.wait_ge(vm_ready, 1)
            nc.tensor.matmul(bank[4][:, :], spread, v_masked.rearrange("p e t d -> p (e t d)"),
                             start=True, stop=True).then_inc(vsd_done, 1)
            scan_step(5)
            scores(0)
            scan_step(6)
            scores(1)
            scan_step(7)
            scan_inputs(1, 0, rhs_hi_part + rhs_lo_part, False, True)

            def probs_to_keys(n):
                pe.wait_ge(exp_done, n + 1)
                for i in range(4):
                    ins = tr(bank[6 + n][:, i * P:(i + 1) * P],
                             prob[:, n, i * 8:i * 8 + 8, :].rearrange("p h s -> p (h s)"))
                ins.then_inc(pT_done, 1)

            def attend(n):
                pe.wait_ge(pT_ready, n + 1)
                pe.wait_ge((vblk_act, vblk_dve)[n], HPC)
                for b in range(16 * n, 16 * n + 16):
                    i, q = b % 16 // 4, b % 4
                    ins = nc.tensor.matmul(bank[6 + n][32 * q:32 * q + 32, i * P:(i + 1) * P], pT[:, b * 32:(b + 1) * 32],
                                           vblk[n][:, b % 16].rearrange("p h d -> p (h d)"), start=True, stop=True)
                ins.then_inc(o_rows_done, 1)

            def heads_to_features(n):
                pe.wait_ge(o_rows_ready, n + 1)
                for i in range(4):
                    ins = tr(bank[6 + n][:, i * P:(i + 1) * P], head_rows[:, n, i * P:(i + 1) * P])
                ins.then_inc(o_done, 1)

            def mix_dst(t):
                return bank[4 + t // 2][:, (t % 2) * D:(t % 2 + 1) * D]

            def mix_states(t, last=False):
                if t < 2:
                    pe.wait_ge(vsd_ready, 1)
                else:
                    pe.wait_ge(vm_ready, 1)
                pe.wait_ge(hid_split, t + 1)
                pe.wait_ge(wco_split, 1)
                ins = product(mix_dst(t), [(hid_hi[:, k, tile_cols(t)], hid_lo[:, k, tile_cols(t)]) for k in range(C)],
                              [(wc_hi[:, k], wc_lo[:, k]) for k in range(C)], first=(t % 2 == 0), last=last, check=True)
                if last:
                    ins.then_inc(y_done, 1)

            def mix_heads(t, last=True):
                pe.wait_ge(wco_split, 2)
                pe.wait_ge(o_lo, 2)
                ins = product(mix_dst(t), [(oT_hi[:, k, tile_cols(t)], oT_lo[:, k, tile_cols(t)]) for k in range(C)],
                              [(wo_hi[:, k], wo_lo[:, k]) for k in range(C)], first=False, last=last, check=True)
                if last:
                    ins.then_inc(y_done, 1)

            probs_to_keys(0)
            scan_step(8)
            scan_inputs(1, 1, rhs_hi_part + rhs_lo_part, False, True)
            probs_to_keys(1)
            attend(0)
            scan_step(9)
            attend(1)
            mix_states(0)
            heads_to_features(0)
            scan_step(10)
            heads_to_features(1)
            mix_states(1)
            scan_step(11)
            mix_heads(0)
            mix_heads(1)
            scan_step(12)
            mix_states(2)
            mix_heads(2)
            scan_step(13)
            pe.wait_ge(tern_ready, 1)
            pe.wait_ge(x2_ready, 2)
            for k in range(C):
                for a in range(C):
                    ins = tr(bank[4][:, (2 * k + a) * P:(2 * k + a + 1) * P], tern[:, a, k * P:(k + 1) * P])
            ins.then_inc(tern_T, 1)
            scan_step(14)

            def norm2_transposes(p):
                pe.wait_ge(x2hat_ready, 2 * p + 2)
                if p == 0:
                    pe.wait_ge(o_lo, 2)
                else:
                    pe.wait_ge(x2_ready, NT)
                    pe.wait_ge(xn2_c0, 2)
                for t in range(2):
                    for c in range(C):
                        ins = tr(norm2_bank(p, c)[:, t * P:(t + 1) * P], x2hat[:, 2 * p + t, c * P:(c + 1) * P])
                ins.then_inc(x2hat_T, 1)

            def up(p, j, parts=rhs_hi_part + rhs_lo_part):
                n = p * FJ + j
                if parts[0] == (0, 0):
                    if n < 4:
                        pe.wait_ge((state_m0, state_m1)[j // 2], T - 1 + j % 2)
                        pe.wait_ge(w1_hi_ready, 2)
                        pe.wait_ge(w1_lo_ready, 1)
                    if n >= 4:
                        pe.wait_ge(gelu_done, n - 3)
                    if j == 0:
                        pe.wait_ge(xn2_c0, 2 * p + 1)
                        pe.wait_ge(xn2_c1, 2 * p + 1)
                if parts[-1] == (0, 1):
                    pe.wait_ge(xn2_split, p + 1)
                ins = product(bank[j % 4][:, (j // 4) * D:(j // 4 + 1) * D],
                              [(w1_hi[:, k, j * P:(j + 1) * P], w1_lo[:, k, j * P:(j + 1) * P]) for k in range(C)],
                              [(xn2_hi[:, p, k], xn2_lo[:, p, k]) for k in range(C)],
                              first=(parts[0] == (0, 0)), last=(parts[-1] == (0, 1)), parts=parts)
                if parts[-1] == (0, 1):
                    ins.then_inc(up_done, 1)

            def down(t, chunks=range(FJ)):
                p, i = t // 2, t % 2
                pe.wait_ge(w2_hi_ready, 4)
                pe.wait_ge(w2_lo_ready, 4)
                if t == 0:
                    pe.wait_ge(xn2_c1, 2)
                elif t == 1:
                    pe.wait_ge(ternT_split, 1)
                elif t == 2:
                    pe.wait_ge(xn2_c1, 4)
                else:
                    pe.wait_ge(xn2_c0, 4)
                for j in chunks:
                    pe.wait_ge((g_even, g_odd)[j % 2], p * FJ // 2 + j // 2 + 1)
                    ins = product(down_bank[t][:, 0:D], [tuple(hidden(p, part, j)[:, i * P:(i + 1) * P] for part in (0, 1))],
                                  [(w2_hi[:, j], w2_lo[:, j])], first=(j == 0), last=(j == FJ - 1))
                if chunks[-1] == FJ - 1:
                    ins.then_inc(down_done, 1)

            def tail_transposes(t):
                pe.wait_ge(tail_rows_ready, t + 1)
                for c in range(C):
                    ins = tr(down_bank[t][:, c * P:(c + 1) * P], tail_rows[:, t, c * P:(c + 1) * P])
                ins.then_inc(h2_T, 1)

            def rotate(t):
                pe.wait_ge(had_ready, 1)
                pe.wait_ge(h2T_lo_s, t + 1)
                product(down_bank[t][:, 0:D], [(h2T_hi[:, t, k], h2T_lo[:, t, k]) for k in range(C)],
                        [(had[:, k], None) for k in range(C)]).then_inc(had_done, 1)

            def quant_transposes(t):
                pe.wait_ge(quant_ready, t + 1)
                for c in range(C):
                    ins = tr(down_bank[t][:, c * P:(c + 1) * P], quant[:, t, c * P:(c + 1) * P])
                ins.then_inc(quant_T, 1)

            def ternary(t):
                pe.wait_ge(quantT_ready, t + 1)
                product(down_bank[t][:, 0:D], [(quantT[:, t, k], None) for k in range(C)],
                        [(ternT_hi[:, k], ternT_lo[:, k]) for k in range(C)]).then_inc(fin_done, 1)

            norm2_transposes(0)
            scan_step(15)
            mix_heads(3, last=False)
            for j in (0, 2, 1):
                up(0, j, rhs_hi_part)
            for j in (0, 1):
                up(0, j, rhs_lo_part)
            mix_states(3, last=True)
            up(0, 2, rhs_lo_part)
            up(0, 3)
            for j in range(4, FJ):
                up(0, j)
            down(0, range(0, 2))
            norm2_transposes(1)
            down(0, range(2, FJ))
            for part in (rhs_hi_part, rhs_lo_part):
                for j in (0, 1):
                    up(1, j, part)
            tail_transposes(0)
            down(1, range(0, 4))
            up(1, 2)
            down(1, range(4, FJ))
            up(1, 3)
            rotate(0)
            up(1, 4)
            tail_transposes(1)
            up(1, 5)
            up(1, 6)
            up(1, 7)
            quant_transposes(0)
            down(2, range(0, 2))
            rotate(1)
            down(2, range(2, 4))
            ternary(0)
            down(2, range(4, 6))
            down(2, range(6, FJ))
            quant_transposes(1)
            down(3, range(0, 2))
            tail_transposes(2)
            ternary(1)
            down(3, range(2, 4))
            rotate(2)
            down(3, range(4, FJ))
            tail_transposes(3)
            quant_transposes(2)
            rotate(3)
            ternary(2)
            quant_transposes(3)
            ternary(3)

        @block.scalar
        def _(act):
            def unit_views(u):
                c, part = units[u]
                if part == "w":
                    dst = [v[:, 2 * c:2 * c + 2].rearrange("p k n -> p (k n)") for v in (tokWT_hi, tokWT_lo)]
                    return unit_bank(u)[:, :], *dst
                src = unit_bank(u)[:, :].rearrange("p (j b i) -> p j i b", j=NP, i=NP)
                return src, *[v[:, 2 * c + part].rearrange("p (i j b) -> p j i b", i=NP, j=NP) for v in (xT_hi, xT_lo)]

            act.wait_ge(ld_x[0], 16)
            group_patches(nc.scalar, 0, 1).then_inc(x_grouped_act, 1)
            for u in range(len(units)):
                act.wait_ge(unit_T, u + 1)
                src, hi, _lo = unit_views(u)
                nc.scalar.copy(hi, src).then_inc(unit_hi, 1)
                if u == 3:
                    act.wait_ge(ld_sel, 48)
                    nc.scalar.copy(posb_hi, posb)
                    nc.scalar.copy(sel_hi, sel).then_inc(posb_hi_ready, 1)

            def token_rows(t):
                act.wait_ge(tok_done, t + 1)
                nc.scalar.copy(h[:, t], bank[t][:, 0:D]).then_inc(h_ready, 1)

            def weights_hi(load, n, pairs, done):
                act.wait_ge(load, n)
                for dst, src in pairs:
                    ins = nc.scalar.copy(dst, src)
                ins.then_inc(done, 1)

            weights_hi(ld_wb, 16, [(wb_hi[:], wb_in[:])], wb_hi_ready)
            weights_hi(ld_wkv, 32, [(heads, w[:].unsqueeze(2).to_broadcast(heads.shape))
                                    for w, heads in ((wk_in, by_head(wkv_hi)[:, :, 0:V_HEAD]),
                                                     (wv_in, by_head(wkv_hi)[:, :, V_HEAD:]))], wkv_hi_ready)
            token_rows(0)
            token_rows(1)
            weights_hi(ld_wq, 16, [(wq_hi[:], wq_in[:])], wq_hi_ready)
            act.wait_ge(ld_ln, 64)

            def norm1(p):
                act.wait_ge(xhat_T, p + 1)
                for dst in (xn_hi, xn):
                    nc.scalar.activation(dst[:, 0, pair_cols(p)], norm1_bank(p, 0)[:, 0:2 * P], ACT.Identity,
                                         scale=ln1w[:, 0:1], bias=ln1b[:, 0:1]).then_inc(xn_c0, 1)

            def down_weights_hi(j):
                weights_hi(ld_w2, 16, [(w2_hi[:, j:j + 2], w2_in[:, j:j + 2])], w2_hi_ready)

            def tanh_step(t):
                for m, (step, state) in enumerate(((step_m0, state_m0), (step_m1, state_m1))):
                    if t == 0:
                        act.wait_ge(pre_done, 1)
                    else:
                        act.wait_ge(step, t)
                    nc.scalar.activation(hid[:, m, t * B:(t + 1) * B], scan_bank(m, t % 2)[:, t // 2 * B:(t // 2 + 1) * B],
                                         ACT.Tanh).then_inc(state, 1)

            def copy_after(ready, n, dst, src, done):
                act.wait_ge(ready, n)
                nc.scalar.copy(dst, src).then_inc(done, 1)

            def states_hi(t):
                act.wait_ge(state_m0, TPT * (t + 1))
                act.wait_ge(state_m1, TPT * (t + 1))
                nc.scalar.copy(hid_hi[:, :, tile_cols(t)], hid[:, :, tile_cols(t)]).then_inc(hid_hi_ready, 1)

            def exp_half(n):
                act.wait_ge(s_shifted, n + 1)
                v = prob[:, n].rearrange("p h s -> p (h s)")
                nc.scalar.activation(v, v, ACT.Exp).then_inc(exp_done, 1)

            norm1(0)
            token_rows(2)
            token_rows(3)
            act.wait_ge(a_T, 1)
            nc.scalar.copy(AT[:].rearrange("p k n -> p (k n)"), bank[5][:, :]).then_inc(a_ready, 1)
            tanh_step(0)
            norm1(1)
            tanh_step(1)
            weights_hi(ld_w1, 32, [(w1_hi[:, 0], w1_in[:, 0])], w1_hi_ready)
            weights_hi(ld_w1, 32, [(w1_hi[:, 1], w1_in[:, 1])], w1_hi_ready)
            kv = bank[4][:, :].rearrange("p (s b) -> p s b", b=B)
            krep_sb = krep.rearrange("p (b s) -> p s b", b=B)
            copy_after(kv_done, 1, krep_sb[0:V0], kv[0:V0], krep_ready)
            copy_after(kv_done, 1, krep_sb[V0:P], kv[0:P - V0], krep_ready)
            tanh_step(2)
            copy_after(kv_done, 1, vT.rearrange("p (b s) -> p s b", b=B), kv[V0:V0 + HD], vT_ready)
            weights_hi(ld_wc, 16, [(wc_hi[:], wc_in[:])], wco_hi_ready)
            tanh_step(3)
            weights_hi(ld_wo, 16, [(wo_hi[:], wo_in[:])], wco_hi_ready)
            copy_after(q0_done, 1, qT[:, :, 0, :].rearrange("p b t -> p t b"),
                       bank[6][:, :].rearrange("p (t b) -> p t b", b=B), q0_ready)
            tanh_step(4)
            down_weights_hi(0)
            copy_after(q1_done, 1, qT[:, :, 1, :].rearrange("p b t -> p t b"),
                       bank[7][:, :].rearrange("p (t b) -> p t b", b=B), q1_ready)
            down_weights_hi(2)
            tanh_step(5)
            copy_after(vsd_done, 1, v_sd[:].rearrange("p (t e) d -> p e t d", e=HPC),
                       bank[4][:, :].rearrange("p (e t d) -> p e t d", e=HPC, t=NT), vsd_ready)

            def block_values_first(heads):
                act.wait_ge(vsd_ready, 1)
                act.wait_ge(wb_split, 1)
                act.wait_ge(wq_split, 1)
                act.wait_ge(wco_split, 2)
                for e in heads:
                    nc.scalar.activation(vblk[0][:, :, e], v_sd[:, 0:B // 2], ACT.Copy,
                                         scale=mask_v[:, e:e + 1]).then_inc(vblk_act, 1)

            states_hi(0)
            tanh_step(6)
            block_values_first(range(0, 2))
            exp_half(0)
            tanh_step(7)
            block_values_first(range(2, 5))
            exp_half(1)
            copy_after(pT_done, 1, pT[:, 0:512], bank[6][:, :], pT_ready)
            block_values_first(range(5, 6))
            tanh_step(8)
            block_values_first(range(6, HPC))
            copy_after(pT_done, 2, pT[:, 512:1024], bank[7][:, :], pT_ready)
            states_hi(1)
            down_weights_hi(4)
            tanh_step(9)
            down_weights_hi(6)
            act.wait_ge(ld_cst, 16)
            nc.scalar.copy(had[:].rearrange("p k n -> p (k n)"), hadamard).then_inc(had_ready, 1)

            def heads_hi(n):
                act.wait_ge(o_done, n + 1)
                for c in range(C):
                    ins = nc.scalar.copy(
                        oT_hi[:, c].rearrange("p (t b) -> p b t", b=B)[:, 16 * n:16 * n + 16],
                        bank[6 + n][:, :].rearrange("p (b c t) -> p b c t", c=C, t=T)[:, :, c])
                ins.then_inc(o_hi, 1)

            heads_hi(0)
            tanh_step(10)
            heads_hi(1)
            tanh_step(11)
            states_hi(2)
            tanh_step(12)
            tanh_step(13)
            copy_after(tern_T, 1, ternT_hi[:].rearrange("p k n -> p (k n)"), bank[4][:, :], ternT_hi_s)
            tanh_step(14)

            def norm2(p, parts=(xn2_hi, xn2)):
                act.wait_ge(x2hat_T, p + 1)
                for dst in parts:
                    nc.scalar.activation(dst[:, p, 0], norm2_bank(p, 0)[:, 0:2 * P], ACT.Identity,
                                         scale=ln2w[:, 0:1], bias=ln2b[:, 0:1]).then_inc(xn2_c0, 1)

            def gelu(p, j):
                n = p * FJ + j
                act.wait_ge(up_done, n + 1)
                if n >= FJ:
                    act.wait_ge((g_even, g_odd)[j % 2], j // 2 + 1)
                for dst in (g[:, j], hidden(p, 0, j)):
                    ins = nc.scalar.activation(dst, bank[j % 4][:, (j // 4) * D:(j // 4 + 1) * D], ACT.Gelu,
                                               bias=b1c[:, j:j + 1])
                ins.then_inc(gelu_done, 1)

            def tail_hi(t):
                act.wait_ge(h2_T, t + 1)
                nc.scalar.copy(h2T_hi[:, t].rearrange("p k n -> p (k n)"), down_bank[t][:, 0:D]).then_inc(h2T_hi_s, 1)

            def tail_norm(t):
                act.wait_ge(shift3, t + 1)
                nc.scalar.activation(h2[:, t], tail_rows[:, t], ACT.Identity, scale=rstd[:, t:t + 1],
                                     bias=shift_tail[:, t:t + 1]).then_inc(h2_ready, 1)

            def last_norm(t):
                act.wait_ge(rstd4, t + 1)
                nc.scalar.activation(o_rows[:, t], f_rows[:, t], ACT.Identity, scale=rstd[:, t:t + 1],
                                     bias=shift_tail[:, t:t + 1]).then_inc(out_ready, 1)

            def quant_copy(t):
                act.wait_ge(quant_T, t + 1)
                nc.scalar.activation(quantT[:, t].rearrange("p k n -> p (k n)"), down_bank[t][:, 0:D], ACT.Copy,
                                     bias=-ROUND).then_inc(quantT_ready, 1)

            norm2(0, (xn2_hi,))
            tanh_step(15)
            states_hi(3)
            norm2(0, (xn2,))
            for j in range(FJ):
                gelu(0, j)
            norm2(1)
            gelu(1, 0)
            gelu(1, 1)
            tail_hi(0)
            gelu(1, 2)
            gelu(1, 3)
            gelu(1, 4)
            tail_hi(1)
            gelu(1, 5)
            gelu(1, 6)
            gelu(1, 7)
            quant_copy(0)
            tail_norm(0)
            tail_norm(1)
            quant_copy(1)
            tail_hi(2)
            tail_norm(2)
            last_norm(0)
            tail_hi(3)
            quant_copy(2)
            last_norm(1)
            tail_norm(3)
            quant_copy(3)
            last_norm(2)

        @block.vector
        def _(dve):
            count = [0]

            def step(ins):
                ins.then_inc(dve_done, 1)
                count[0] += 1
                return count[0]

            def after(n):
                dve.wait_ge(dve_done, n)

            def lo_part(dst, full, hi):
                return nc.vector.tensor_tensor(dst, full, hi.bitcast(F32), ALU.subtract)

            dve.wait_ge(ld_x[0], 16)
            group_patches(nc.vector, 0, 0).then_inc(x_grouped_dve, 1)
            for u in range(len(units)):
                c, part = units[u]
                dve.wait_ge(unit_hi, u + 1)
                if part == "w":
                    hi, lo = [v[:, 2 * c:2 * c + 2].rearrange("p k n -> p (k n)") for v in (tokWT_hi, tokWT_lo)]
                    src = unit_bank(u)[:, :]
                else:
                    src = unit_bank(u)[:, :].rearrange("p (j b i) -> p j i b", j=NP, i=NP)
                    hi, lo = [v[:, 2 * c + part].rearrange("p (i j b) -> p j i b", i=NP, j=NP) for v in (xT_hi, xT_lo)]
                lo_part(lo, src, hi).then_inc(unit_lo, 1)
                if u in (1, 3):
                    dve.wait_ge(ld_x[u // 2 + 1], 16)
                    group_patches(nc.vector, u // 2 + 1, 0).then_inc(x_grouped_dve, 1)
                if u == 3:
                    dve.wait_ge(posb_hi_ready, 1)
                    lo_part(posb_lo, posb, posb_hi).then_inc(posb_split, 1)
                    dve.wait_ge(ld_fw, 16)
                    after(step(nc.vector.tensor_reduce(wsc[:, 0], fw_in[:], AX.X, ALU.add, apply_absolute_value=True)))
                    after(step(nc.vector.tensor_scalar(wsc[:, 0], wsc[:, 0], 1.0 / D, 1e-5, ALU.mult, ALU.max)))
                    nc.vector.tensor_scalar(wsc[:, 1], wsc[:, 0], 0.5, None, ALU.mult)
                    nc.vector.tensor_scalar(wsc[:, 2], wsc[:, 0], -0.5, None, ALU.mult).then_inc(wsc_ready, 1)

            def moments(rows, t):
                after(step(nc.vector.bn_stats(stats[:, t], rows)))
                return step(nc.vector.bn_aggr(mv[:, t], stats[:, t]))

            def norm1_moments(t):
                dve.wait_ge(h_ready, t + 1)
                return moments(h[:, t], t)

            def norm1_variance(p, n_moments):
                after(n_moments)
                nc.vector.tensor_scalar(var[:, 2 * p:2 * p + 2], mv[:, 2 * p:2 * p + 2, 1], EPS, None,
                                        ALU.add).then_inc(var1, 1)

            def norm1_rows(p):
                dve.wait_ge(rstd1, p + 1)
                for t in (2 * p, 2 * p + 1):
                    nc.vector.tensor_scalar(xhat[:, t], h[:, t], mv[:, t, 0:1], rstd[:, t:t + 1],
                                            ALU.subtract, ALU.mult).then_inc(xhat_ready, 1)

            def norm1_features(p):
                dve.wait_ge(xhat_T, p + 1)
                dve.wait_ge(ld_ln, 64)
                for dst in (xn_hi, xn):
                    nc.vector.tensor_scalar(dst[:, 1, pair_cols(p)], norm1_bank(p, 1)[:, 0:2 * P],
                                            ln1w[:, 1:2], ln1b[:, 1:2], ALU.mult, ALU.add).then_inc(xn_c1, 1)

            def norm1_rest(p):
                dve.wait_ge(xn_c0, 2 * p + 2)
                dve.wait_ge(xn_c1, 2 * p + 2)
                lo_part(xn_lo[:, :, pair_cols(p)], xn[:, :, pair_cols(p)], xn_hi[:, :, pair_cols(p)]).then_inc(xn_split, 1)

            norm1_moments(0)
            norm1_variance(0, norm1_moments(1))
            norm1_rows(0)
            norm1_features(0)
            norm1_rest(0)
            norm1_moments(2)
            norm1_variance(1, norm1_moments(3))
            norm1_rows(1)
            norm1_features(1)
            norm1_rest(1)

            dve.wait_ge(ld_gates, 48)
            for t in range(NT):
                if t:
                    after(n)
                n = step(nc.vector.scalar_tensor_tensor(junk, h[:, t], 1.0, wg_row[:, :], ALU.mult, ALU.mult,
                                                        accum_out=sc_rows[:, t:t + 1]))
            after(n)
            n_score = step(nc.vector.tensor_scalar(sc_rows[:, :], sc_rows[:, :], bg_col[:, 0:1], None, ALU.add))

            dve.wait_ge(krep_ready, 2)
            dve.wait_ge(ld_cst, 16)
            for e in range(HPC):
                nc.vector.tensor_scalar(kblk[:, :, e], krep.rearrange("p (b s) -> p b s", b=B), mask_k[:, e:e + 1], None,
                                        ALU.mult).then_inc(kblk_ready, 1)
                if e == HPC // 2:
                    dve.wait_ge(vm_T, 1)
                    nc.vector.tensor_tensor(v_masked, bank[5][:, 0:NT * HD].rearrange("p (t d) -> p t d", t=NT)
                                            .unsqueeze(1).to_broadcast([P, HPC, NT, HD]),
                                            mask_v.unsqueeze(2).unsqueeze(3).to_broadcast([P, HPC, NT, HD]),
                                            ALU.mult).then_inc(vm_ready, 1)
            after(n_score)
            for k in range(TPT):
                n = step(nc.vector.tensor_copy(sc[:, :].rearrange("b (t k) -> b t k", k=TPT)[:, :, k],
                                               sc_rows[B * k:B * k + B, :]))
            after(n)
            other = sc[:, :].unsqueeze(1).to_broadcast([B, T, T])
            own = sc[:, :].unsqueeze(2).to_broadcast([B, T, T])
            step(nc.vector.tensor_tensor(gt[:], other, own, ALU.is_gt))
            after(step(nc.vector.tensor_tensor(eq[:], other, own, ALU.is_equal)))
            after(step(nc.vector.tensor_tensor(eq[:], eq[:], earlier[0:B].rearrange("b (t s) -> b t s", s=T), ALU.mult)))
            after(step(nc.vector.tensor_tensor(gt[:], gt[:], eq[:], ALU.add)))
            n_rank = step(nc.vector.tensor_reduce(rank[:, :], gt[:], AX.X, ALU.add))

            def split_states(t):
                dve.wait_ge(hid_hi_ready, t + 1)
                lo_part(hid_lo[:, :, tile_cols(t)], hid[:, :, tile_cols(t)], hid_hi[:, :, tile_cols(t)]).then_inc(hid_split, 1)

            def shift(n):
                dve.wait_ge(s_done, n + 1)
                dve.wait_ge(tern_ready, 1)
                s = bank[6 + n][:, :].rearrange("p (h s) -> p h s", s=T)
                after(step(nc.vector.tensor_reduce(smax[:, n], s, AX.X, ALU.max)))
                nc.vector.tensor_tensor(prob[:, n], s, smax[:, n].unsqueeze(2).to_broadcast([P, 32, T]),
                                        ALU.subtract).then_inc(s_shifted, 1)

            def sums(n):
                dve.wait_ge(exp_done, n + 1)
                after(step(nc.vector.tensor_reduce(ssum[:, n], prob[:, n], AX.X, ALU.add)))
                return step(nc.vector.reciprocal(srec[:, n], ssum[:, n]))

            def scale_heads(n, n_sum):
                dve.wait_ge(o_rows_done, n + 1)
                after(n_sum)
                nc.vector.tensor_tensor(head_rows[:, n].rearrange("p (h d) -> p h d", d=HD),
                                        bank[6 + n][:, :].rearrange("p (h d) -> p h d", d=HD),
                                        srec[:, n].unsqueeze(2).to_broadcast([P, 32, HD]), ALU.mult).then_inc(o_rows_ready, 1)

            def block_values_last():
                dve.wait_ge(vsd_ready, 1)
                dve.wait_ge(s_done, 1)
                for e in range(HPC):
                    nc.vector.tensor_scalar(vblk[1][:, :, e], v_sd[:, B // 2:B], mask_v[:, e:e + 1],
                                            None, ALU.mult).then_inc(vblk_dve, 1)

            shift(0)
            after(n_rank)
            after(step(nc.vector.tensor_scalar(m_bt[:, :], rank[:, :], TOPK - 0.5, None, ALU.is_lt)))
            for k in range(TPT):
                step(nc.vector.tensor_copy(m_rows[B * k:B * k + B, :],
                                           m_bt[:, :].rearrange("b (t k) -> b t k", k=TPT)[:, :, k]))
            step(nc.vector.tensor_scalar(gate[:, 0:1], sg_col[:, :], -1.0, None, ALU.mult))
            after(step(nc.vector.tensor_scalar(gate[:, 1:2], sg_col[:, :], 1.0, None, ALU.add)))
            nc.vector.tensor_scalar(c_rows[:, :], m_rows[:, :], gate[:, 0:1], gate[:, 1:2],
                                    ALU.mult, ALU.add).then_inc(mask_ready, 1)
            shift(1)
            split_states(0)
            block_values_last()
            n_sum0 = sums(0)
            n_sum1 = sums(1)
            scale_heads(0, n_sum0)
            split_states(1)
            scale_heads(1, n_sum1)

            def heads_lo(n):
                dve.wait_ge(o_hi, n + 1)
                for c in range(C):
                    ins = lo_part(oT_lo[:, c].rearrange("p (t b) -> p b t", b=B)[:, 16 * n:16 * n + 16],
                                  bank[6 + n][:, :].rearrange("p (b c t) -> p b c t", c=C, t=T)[:, :, c],
                                  oT_hi[:, c].rearrange("p (t b) -> p b t", b=B)[:, 16 * n:16 * n + 16])
                ins.then_inc(o_lo, 1)

            def residual(t):
                dve.wait_ge(skip_ready, t + 1)
                dve.wait_ge(hc_ready, t + 1)
                return step(nc.vector.scalar_tensor_tensor(skip[:, t], skip[:, t], m_rows[:, t:t + 1], hc[:, t],
                                                           ALU.mult, ALU.add))

            residual(0)
            residual(1)
            heads_lo(0)
            heads_lo(1)
            split_states(2)
            residual(2)
            n_residual = residual(3)
            after(n_residual)

            def add_mixed(p):
                dve.wait_ge(y_done, 2 * p + 2)
                for t in (2 * p, 2 * p + 1):
                    nc.vector.scalar_tensor_tensor(x2[:, t], bank[4 + p][:, (t % 2) * D:(t % 2 + 1) * D],
                                                   m_rows[:, t:t + 1], skip[:, t], ALU.mult, ALU.add).then_inc(x2_ready, 1)
                for t in (2 * p, 2 * p + 1):
                    dve.wait_ge(x2_ready, t + 1)
                    n = moments(x2[:, t], t)
                after(n)
                nc.vector.tensor_scalar(var[:, 2 * p:2 * p + 2], mv[:, 2 * p:2 * p + 2, 1], EPS, None,
                                        ALU.add).then_inc(var2, 1)

            def norm2(p):
                dve.wait_ge(rstd2, p + 1)
                for t in (2 * p, 2 * p + 1):
                    nc.vector.tensor_scalar(x2hat[:, t], x2[:, t], mv[:, t, 0:1], rstd[:, t:t + 1],
                                            ALU.subtract, ALU.mult).then_inc(x2hat_ready, 1)

            def split_norm2(p):
                dve.wait_ge(x2hat_T, p + 1)
                for dst in (xn2_hi, xn2):
                    nc.vector.tensor_scalar(dst[:, p, 1], norm2_bank(p, 1)[:, 0:2 * P], ln2w[:, 1:2], ln2b[:, 1:2],
                                            ALU.mult, ALU.add).then_inc(xn2_c1, 1)
                if p == 0:
                    split_states(3)
                dve.wait_ge(xn2_c0, 2 * p + 2)
                dve.wait_ge(xn2_c1, 2 * p + 2)
                lo_part(xn2_lo[:, p], xn2[:, p], xn2_hi[:, p]).then_inc(xn2_split, 1)

            def split_gelu(p, j):
                dve.wait_ge(gelu_done, p * FJ + j + 1)
                lo_part(hidden(p, 1, j), g[:, j], hidden(p, 0, j)).then_inc(g_even, 1)

            def tail_sum(t):
                dve.wait_ge(down_done, t + 1)
                dve.wait_ge(base2_ready, t + 1)
                nc.vector.tensor_tensor(tail_rows[:, t], down_bank[t][:, 0:D], base2[:, t],
                                        ALU.add).then_inc(tail_rows_ready, 1)

            def tail_stats(t):
                dve.wait_ge(tail_rows_ready, t + 1)
                return step(nc.vector.bn_stats(stats[:, t], tail_rows[:, t]))

            def aggregate(t, n_stats):
                after(n_stats)
                return step(nc.vector.bn_aggr(mv[:, t], stats[:, t]))

            def add_eps(t, n_aggr, done):
                after(n_aggr)
                nc.vector.tensor_scalar(var[:, t:t + 1], mv[:, t, 1:2], EPS, None, ALU.add).then_inc(done, 1)

            def tail_moments(t):
                add_eps(t, aggregate(t, tail_stats(t)), var3)

            def tail_lo(t):
                dve.wait_ge(h2T_hi_s, t + 1)
                lo_part(h2T_lo[:, t].rearrange("p k n -> p (k n)"), down_bank[t][:, 0:D],
                        h2T_hi[:, t].rearrange("p k n -> p (k n)")).then_inc(h2T_lo_s, 1)

            def row_size(t):
                dve.wait_ge(had_done, t + 1)
                return step(nc.vector.tensor_reduce(amax[:, t:t + 1], down_bank[t][:, 0:D], AX.X, ALU.max,
                                                 apply_absolute_value=True))

            def quantum(t, n_size):
                dve.wait_ge(rstd3, t + 1)
                after(n_size)
                return step(nc.vector.tensor_scalar(qstep[:, t:t + 1], amax[:, t:t + 1], 1.0 / QMAX, floor3[:, t:t + 1],
                                                    ALU.mult, ALU.max))

            def invert(t, n_quantum):
                after(n_quantum)
                return step(nc.vector.reciprocal(qinv[:, t:t + 1], qstep[:, t:t + 1]))

            n_qscale = []

            def scale_rows(t, n_inverse):
                after(n_inverse)
                return step(nc.vector.tensor_scalar(quant[:, t], down_bank[t][:, 0:D], qinv[:, t:t + 1], QMAX,
                                                    ALU.mult, ALU.min))

            def round_rows(t, n_scaled):
                after(n_scaled)
                nc.vector.tensor_scalar(quant[:, t], quant[:, t], QMIN, ROUND, ALU.max, ALU.add).then_inc(quant_ready, 1)
                n_qscale.append(step(nc.vector.tensor_tensor(qscale[:, t:t + 1], qstep[:, t:t + 1], rstd[:, t:t + 1],
                                                             ALU.mult)))

            def quantise(t, n_size):
                round_rows(t, scale_rows(t, invert(t, quantum(t, n_size))))

            def last_sum(t):
                dve.wait_ge(fin_done, t + 1)
                dve.wait_ge(h2_ready, t + 1)
                after(n_qscale[t])
                return step(nc.vector.scalar_tensor_tensor(f_rows[:, t], down_bank[t][:, 0:D], qscale[:, t:t + 1],
                                                           h2[:, t], ALU.mult, ALU.add))

            def last_stats(t, n_sum):
                after(n_sum)
                return step(nc.vector.bn_stats(stats[:, t], f_rows[:, t]))

            def last_moments(t, n_sum):
                add_eps(t, aggregate(t, last_stats(t, n_sum)), var4)

            def last_norm(t):
                dve.wait_ge(rstd4, t + 1)
                nc.vector.tensor_scalar(o_rows[:, t], f_rows[:, t], mv[:, t, 0:1], rstd[:, t:t + 1],
                                        ALU.subtract, ALU.mult).then_inc(last_out_ready, 1)

            add_mixed(0)
            norm2(0)
            split_norm2(0)
            dve.wait_ge(ternT_hi_s, 1)
            lo_part(ternT_lo[:].rearrange("p k n -> p (k n)"), bank[4][:, :],
                    ternT_hi[:].rearrange("p k n -> p (k n)")).then_inc(ternT_split, 1)
            add_mixed(1)
            split_gelu(0, 0)
            split_gelu(0, 2)
            norm2(1)
            split_gelu(0, 4)
            split_gelu(0, 6)
            split_norm2(1)
            tail_sum(0)
            tail_moments(0)
            split_gelu(1, 0)
            tail_lo(0)
            split_gelu(1, 2)
            tail_sum(1)
            n = row_size(0)
            tail_moments(1)
            quantise(0, n)
            split_gelu(1, 4)
            tail_lo(1)
            split_gelu(1, 6)
            quantise(1, row_size(1))
            tail_sum(2)
            n2 = tail_stats(2)
            n0 = last_sum(0)
            n2 = aggregate(2, n2)
            n0 = last_stats(0, n0)
            add_eps(2, n2, var3)
            tail_lo(2)
            add_eps(0, aggregate(0, n0), var4)
            n1 = last_sum(1)
            n2 = row_size(2)
            n1 = last_stats(1, n1)
            n2 = quantum(2, n2)
            n1 = aggregate(1, n1)
            n2 = invert(2, n2)
            add_eps(1, n1, var4)
            n2 = scale_rows(2, n2)
            tail_sum(3)
            round_rows(2, n2)
            tail_moments(3)
            tail_lo(3)
            quantise(3, row_size(3))
            last_moments(2, last_sum(2))
            last_moments(3, last_sum(3))
            last_norm(3)

        @block.gpsimd
        def _(pool):
            count = [0]

            def step(ins):
                ins.then_inc(pool_done, 1)
                count[0] += 1
                return count[0]

            def after(n):
                pool.wait_ge(pool_done, n)

            def lo_part(hi_ready, n, full, hi, lo, done):
                pool.wait_ge(hi_ready, n)
                nc.gpsimd.tensor_tensor(lo, full, hi.bitcast(F32), ALU.subtract).then_inc(done, 1)

            def inverse_root(t, n, ready, value, done):
                pool.wait_ge(ready, value)
                nc.gpsimd.tensor_tensor(rstd[:, t:t + n], var[:, t:t + n], neg_half[:, 0:n], ALU.pow).then_inc(done, 1)

            def tail_scale(t, ready):
                pool.wait_ge(ready, t + 1)
                after(step(nc.gpsimd.tensor_tensor(rstd[:, t:t + 1], var[:, t:t + 1], neg_half[:, 0:1], ALU.pow)))

            def tail_shift(t, done):
                nc.gpsimd.tensor_scalar(shift_tail[:, t:t + 1], mv[:, t, 0:1], rstd[:, t:t + 1], -1.0,
                                        ALU.mult, ALU.mult).then_inc(done, 1)

            def block_norm(t):
                tail_scale(t, var3)
                nc.gpsimd.tensor_scalar(floor3[:, t:t + 1], var[:, t:t + 1], rstd[:, t:t + 1], 1e-5 / QMAX,
                                        ALU.mult, ALU.mult).then_inc(rstd3, 1)
                tail_shift(t, shift3)

            def result_norm(t):
                if t < NT - 1:
                    tail_scale(t, var4)
                    tail_shift(t, rstd4)
                else:
                    inverse_root(t, 1, var4, t + 1, rstd4)

            def ternary_part(dst, a, threshold, compare):
                return step(nc.gpsimd.tensor_scalar(dst[:, a], fw_in[:, a], wsc[:, threshold, a:a + 1], wsc[:, 0, a:a + 1],
                                                    compare, ALU.mult))

            def weights_down_lo(j):
                pool.wait_ge(w2_hi_ready, j // 2 + 1)
                nc.gpsimd.tensor_tensor(w2_lo[:, j:j + 2], w2_in[:, j:j + 2], w2_hi[:, j:j + 2].bitcast(F32),
                                        ALU.subtract).then_inc(w2_lo_ready, 1)

            def base(t):
                pool.wait_ge(x2_ready, t + 1)
                nc.gpsimd.tensor_tensor(base2[:, t], x2[:, t], hb2[:, t], ALU.add).then_inc(base2_ready, 1)

            def split_gelu(p, j):
                pool.wait_ge(gelu_done, p * FJ + j + 1)
                nc.gpsimd.tensor_tensor(hidden(p, 1, j), g[:, j], hidden(p, 0, j).bitcast(F32),
                                        ALU.subtract).then_inc(g_odd, 1)

            nc.gpsimd.dma_start(posb[0:T, :], tok_pos).then_inc(ld_sel, 16)
            nc.gpsimd.dma_start(posb[T:T + 1, :], tok_b.rearrange("(a d) -> a d", a=1)).then_inc(ld_sel, 16)
            nc.gpsimd.dma_start(sel[:], row_sel).then_inc(ld_sel, 16)
            n_half = step(nc.gpsimd.memset(neg_half[:, :], -0.5))
            for c in range(1, CH):
                pool.wait_ge(ld_x[c], 16)
                group_patches(nc.gpsimd, c, 1).then_inc(x_grouped_pool, 1)
            pool.wait_ge(wsc_ready, 1)
            ternary_part(wpos, 0, 1, ALU.is_gt)
            ternary_part(wneg, 0, 2, ALU.is_lt)
            lo_part(wb_hi_ready, 1, wb_in[:], wb_hi[:], wb_lo[:], wb_split)
            pool.wait_ge(wkv_hi_ready, 1)
            for w, heads in ((wk_in, slice(0, V_HEAD)), (wv_in, slice(V_HEAD, HPC))):
                hi, lo = by_head(wkv_hi)[:, :, heads].bitcast(F32), by_head(wkv_lo)[:, :, heads]
                ins = nc.gpsimd.tensor_tensor(lo, w[:].unsqueeze(2).to_broadcast(lo.shape), hi, ALU.subtract)
            ins.then_inc(wkv_split, 1)
            after(n_half)
            inverse_root(0, 2, var1, 1, rstd1)
            lo_part(wq_hi_ready, 1, wq_in[:], wq_hi[:], wq_lo[:], wq_split)
            ternary_part(wpos, 1, 1, ALU.is_gt)
            inverse_root(2, 2, var1, 2, rstd1)
            after(ternary_part(wneg, 1, 2, ALU.is_lt))
            nc.gpsimd.tensor_tensor(tern[:], wpos[:], wneg[:], ALU.subtract).then_inc(tern_ready, 1)
            pool.wait_ge(ld_rows, 64)
            pool.wait_ge(xhat_T, 2)
            step(nc.gpsimd.tensor_tensor(dw, dp_row[:, :], l1w_row[:, :], ALU.mult))
            after(step(nc.gpsimd.tensor_tensor(db, dp_row[:, :], l1b_row[:, :], ALU.mult)))
            pool.wait_ge(xhat_ready, NT)
            for t in range(NT):
                after(step(nc.gpsimd.tensor_tensor(skip[:, t], xhat[:, t], dw, ALU.mult)))
                nc.gpsimd.tensor_tensor(skip[:, t], skip[:, t], db, ALU.add).then_inc(skip_ready, 1)
            lo_part(wco_hi_ready, 1, wc_in[:], wc_hi[:], wc_lo[:], wco_split)
            lo_part(wco_hi_ready, 2, wo_in[:], wo_hi[:], wo_lo[:], wco_split)
            lo_part(w1_hi_ready, 2, w1_in[:], w1_hi[:], w1_lo[:], w1_lo_ready)
            pool.wait_ge(mask_ready, 1)
            for t in range(NT):
                nc.gpsimd.tensor_scalar(hc[:, t], h[:, t], c_rows[:, t:t + 1], None, ALU.mult).then_inc(hc_ready, 1)
            pool.wait_ge(vsd_done, 1)
            for t in range(NT):
                n_hb2 = step(nc.gpsimd.tensor_tensor(hb2[:, t], h[:, t], b2_row[:, :], ALU.add))
            for j in range(0, FJ, 2):
                weights_down_lo(j)
            inverse_root(0, 2, var2, 1, rstd2)
            after(n_hb2)
            base(0)
            split_gelu(0, 1)
            inverse_root(2, 2, var2, 2, rstd2)
            base(1)
            split_gelu(0, 3)
            split_gelu(0, 5)
            split_gelu(0, 7)
            base(2)
            base(3)
            block_norm(0)
            split_gelu(1, 1)
            block_norm(1)
            split_gelu(1, 3)
            split_gelu(1, 5)
            split_gelu(1, 7)
            block_norm(2)
            result_norm(0)
            result_norm(1)
            block_norm(3)
            result_norm(2)
            result_norm(3)


_INS = ['x', 'L0_tok_W', 'L0_tok_b', 'L0_tok_pos_emb', 'L0_attn_Wg', 'L0_attn_bg', 'L0_attn_Wq', 'L0_attn_Wk',
        'L0_attn_Wv', 'L0_attn_Wo', 'L0_attn_A', 'L0_attn_Wb', 'L0_attn_Wc', 'L0_attn_Dp', 'L0_attn_W1',
        'L0_attn_b1', 'L0_attn_W2', 'L0_attn_b2', 'L0_attn_ln1_w', 'L0_attn_ln1_b', 'L0_attn_ln2_w',
        'L0_attn_ln2_b', 'L0_attn_skip_gate', 'L0_ffn_weight']


def kernel(**inputs):
    import numpy as _np
    import concourse.bacc as _bacc
    from concourse import mybir as _mybir
    from concourse.bass_utils import run_bass_kernel_spmd as _run

    nc = _bacc.Bacc("TRN2", target_bir_lowering=False, num_devices=1)
    arrays, args = {}, []
    consts, row_sel = shape_constants()
    given = [(name, inputs[name]) for name in _INS] + [("consts", consts), ("row_sel", row_sel)]
    for name, value in given:
        a = _np.ascontiguousarray(value)
        arrays[f"in_{name}_dram"] = a
        args.append(nc.dram_tensor(f"in_{name}_dram", a.shape, _mybir.dt.from_np(a.dtype), kind="ExternalInput").ap())
    args.append(nc.dram_tensor("out_0_dram", (B, T, D), F32, kind="ExternalOutput").ap())
    vit_block(nc, *args)
    r = _run(nc, [arrays], core_ids=[0])
    return r.results[0]["out_0_dram"]
```
